# Optimizing a Trainium2 kernel written in Bass

```python
import numpy as np
import jax
import jax.numpy as jnp

def _softmax(x, axis=-1):
    return jax.nn.softmax(x, axis=axis)

def _gelu(x):
    return jax.nn.gelu(x, approximate=True)

def _silu(x):
    return jax.nn.silu(x)

def _sigmoid(x):
    return jax.nn.sigmoid(x)

def _layernorm(x, axis=-1, eps=1e-05):
    m = jnp.mean(x, axis=axis, keepdims=True)
    v = jnp.var(x, axis=axis, keepdims=True)
    return (x - m) / jnp.sqrt(v + eps)

def _scatter_add(tgt, idx, src, axis=0):
    return tgt.at[idx].add(src)

def _segment_sum(src, seg, n):
    return jax.ops.segment_sum(src, seg, n)
kernel_name = 'mk_gnn_preln_d2_gnn_r32_957418'

def setup_inputs(seed: int=0):
    np.random.seed(seed)
    _w = jnp.asarray

    def _rec_inputs():
        import jax
        import jax.numpy as jnp
        _gk = jax.random.key(seed)
        x = -0.000202 + 1 * jax.random.normal(jax.random.fold_in(_gk, 1), (50000, 128), jnp.float32)
        src = jax.random.randint(jax.random.fold_in(_gk, 2), (50000,), 0, 50000, jnp.int32)
        dst = jax.random.randint(jax.random.fold_in(_gk, 3), (50000,), 0, 50000, jnp.int32)
        _o = jnp.argsort(dst, stable=True)
        src = src[_o]
        dst = dst[_o]
        edge_attr_64 = -0.000128692 + 0.999872 * jax.random.normal(jax.random.fold_in(_gk, 12), (50000, 64), jnp.float32)
        return (x, src, dst, edge_attr_64)
    x, src, dst, edge_attr_64 = _rec_inputs()

    def _L0_gnn_setup():
        import jax, jax.numpy as jnp
        import numpy as np
        N_NODES = 50000
        HEADS = 16
        HEAD_DIM = 8
        IN_DIM = 128
        HID = HEADS * HEAD_DIM
        NEG_SLOPE = 0.2

        def _gat_conv(x, src, dst, W, a_src, a_dst, bias):
            N = x.shape[0]
            xh = (x @ W).reshape(N, HEADS, HEAD_DIM)
            al_s = jnp.einsum('nhc,hc->nh', xh, a_src)
            al_d = jnp.einsum('nhc,hc->nh', xh, a_dst)
            e = jax.nn.leaky_relu(al_s[src] + al_d[dst], NEG_SLOPE)
            m = jax.ops.segment_max(e, dst, num_segments=N)
            m = jnp.where(jnp.isfinite(m), m, 0.0)
            ex = jnp.exp(e - m[dst])
            denom = jax.ops.segment_sum(ex, dst, num_segments=N)
            alpha = ex / (denom[dst] + 1e-16)
            msg = xh[src] * alpha[:, :, None]
            out = jax.ops.segment_sum(msg, dst, num_segments=N)
            return out.reshape(N, HID) + bias
        key = jax.random.key(seed)
        ks = jax.random.split(key, 12)
        s = 1.0 / np.sqrt(IN_DIM)
        s2 = 1.0 / np.sqrt(HID)
        return {'x': jax.random.normal(ks[0], (N_NODES, IN_DIM), jnp.float32), 'edge_index': jax.random.randint(ks[1], (2, 25000), 0, N_NODES, jnp.int64), 'W1': jax.random.normal(ks[2], (IN_DIM, HID), jnp.float32) * s, 'a_src1': jax.random.normal(ks[3], (HEADS, HEAD_DIM), jnp.float32) * s, 'a_dst1': jax.random.normal(ks[4], (HEADS, HEAD_DIM), jnp.float32) * s, 'b1': jnp.zeros((HID,), jnp.float32), 'W2': jax.random.normal(ks[5], (HID, HID), jnp.float32) * s2, 'a_src2': jax.random.normal(ks[6], (HEADS, HEAD_DIM), jnp.float32) * s2, 'a_dst2': jax.random.normal(ks[7], (HEADS, HEAD_DIM), jnp.float32) * s2, 'b2': jnp.zeros((HID,), jnp.float32)}
    _L0_gnn_all = _L0_gnn_setup()
    _L0_gnn_in = {k: v for k, v in _L0_gnn_all.items() if k in ('W1', 'a_src1', 'a_dst1', 'b1', 'W2', 'a_src2', 'a_dst2', 'b2')}
    del _L0_gnn_all

    def _L1_gnn_setup():
        import jax, jax.numpy as jnp
        import numpy as np
        N_NODES = 625
        N_EDGES = 20000
        D_NODE = 128
        D_EDGE = 64
        D_OUT = 128
        key = jax.random.key(seed)
        ks = jax.random.split(key, 7)
        feats_node = jax.random.normal(ks[0], (N_NODES, D_NODE), dtype=jnp.float32)
        feats_edge = jax.random.normal(ks[1], (N_EDGES, D_EDGE), dtype=jnp.float32)
        Wn = 0.5 * jax.random.normal(ks[2], (D_OUT, D_NODE), dtype=jnp.float32)
        We = 0.5 * jax.random.normal(ks[3], (D_OUT, D_EDGE), dtype=jnp.float32)
        Wa = 0.5 * jax.random.normal(ks[4], (1, 3 * D_OUT), dtype=jnp.float32)
        src = jax.random.randint(ks[5], (N_EDGES,), 0, N_NODES, dtype=jnp.int32)
        dst = jax.random.randint(ks[6], (N_EDGES,), 0, N_NODES, dtype=jnp.int32)
        return {'feats_node': feats_node, 'feats_edge': feats_edge, 'Wn': Wn, 'We': We, 'Wa': Wa, 'src': src, 'dst': dst}
    _L1_gnn_all = _L1_gnn_setup()
    _L1_gnn_in = {k: v for k, v in _L1_gnn_all.items() if k in ('Wn', 'We', 'Wa')}
    del _L1_gnn_all
    return {'x': x, 'src': src, 'dst': dst, 'edge_attr_64': edge_attr_64, 'L0_gnn_W1': _L0_gnn_in['W1'], 'L0_gnn_a_src1': _L0_gnn_in['a_src1'], 'L0_gnn_a_dst1': _L0_gnn_in['a_dst1'], 'L0_gnn_b1': _L0_gnn_in['b1'], 'L0_gnn_W2': _L0_gnn_in['W2'], 'L0_gnn_a_src2': _L0_gnn_in['a_src2'], 'L0_gnn_a_dst2': _L0_gnn_in['a_dst2'], 'L0_gnn_b2': _L0_gnn_in['b2'], 'L1_gnn_Wn': _L1_gnn_in['Wn'], 'L1_gnn_We': _L1_gnn_in['We'], 'L1_gnn_Wa': _L1_gnn_in['Wa']}

def reference(x, src, dst, edge_attr_64, L0_gnn_W1, L0_gnn_a_src1, L0_gnn_a_dst1, L0_gnn_b1, L0_gnn_W2, L0_gnn_a_src2, L0_gnn_a_dst2, L0_gnn_b2, L1_gnn_Wn, L1_gnn_We, L1_gnn_Wa):
    import jax
    import jax.numpy as jnp

    def _L0_gnn_ref(x, edge_index, W1, a_src1, a_dst1, b1, W2, a_src2, a_dst2, b2):
        import jax, jax.numpy as jnp
        import numpy as np
        N_NODES = 50000
        HEADS = 16
        HEAD_DIM = 8
        IN_DIM = 128
        HID = HEADS * HEAD_DIM
        NEG_SLOPE = 0.2

        def _gat_conv(x, src, dst, W, a_src, a_dst, bias):
            N = x.shape[0]
            xh = (x @ W).reshape(N, HEADS, HEAD_DIM)
            al_s = jnp.einsum('nhc,hc->nh', xh, a_src)
            al_d = jnp.einsum('nhc,hc->nh', xh, a_dst)
            e = jax.nn.leaky_relu(al_s[src] + al_d[dst], NEG_SLOPE)
            m = jax.ops.segment_max(e, dst, num_segments=N)
            m = jnp.where(jnp.isfinite(m), m, 0.0)
            ex = jnp.exp(e - m[dst])
            denom = jax.ops.segment_sum(ex, dst, num_segments=N)
            alpha = ex / (denom[dst] + 1e-16)
            msg = xh[src] * alpha[:, :, None]
            out = jax.ops.segment_sum(msg, dst, num_segments=N)
            return out.reshape(N, HID) + bias
        N = x.shape[0]
        loops = jnp.arange(N, dtype=edge_index.dtype)
        src = jnp.concatenate([edge_index[0], loops])
        dst = jnp.concatenate([edge_index[1], loops])
        h = jax.nn.elu(_gat_conv(x, src, dst, W1, a_src1, a_dst1, b1))
        h = _gat_conv(h, src, dst, W2, a_src2, a_dst2, b2)
        return h

    def _L1_gnn_ref(feats_node, feats_edge, Wn, We, Wa, src, dst):
        import jax, jax.numpy as jnp
        import numpy as np
        N_NODES = 625
        N_EDGES = 20000
        D_NODE = 128
        D_EDGE = 64
        D_OUT = 128
        n_nodes = feats_node.shape[0]
        d = Wn.shape[0]
        z_node = feats_node @ Wn.T
        z_edge = feats_edge @ We.T
        a_src, a_dst, a_e = (Wa[0, :d], Wa[0, d:2 * d], Wa[0, 2 * d:])
        z_src = z_node[src]
        z_dst = z_node[dst]
        logits = z_src @ a_src + z_dst @ a_dst + z_edge @ a_e
        e = jax.nn.leaky_relu(logits, negative_slope=0.2)
        m = jax.ops.segment_max(e, dst, num_segments=n_nodes)
        ex = jnp.exp(e - m[dst])
        s = jax.ops.segment_sum(ex, dst, num_segments=n_nodes)
        alpha = ex / jnp.where(s[dst] == 0, 1.0, s[dst])
        h = jax.ops.segment_sum(alpha[:, None] * z_src, dst, num_segments=n_nodes)
        return h
    edge_index = jnp.stack([src, dst])
    h = jnp.maximum(_layernorm(x, axis=-1), 0.0)
    x = x + _L0_gnn_ref(h, edge_index, L0_gnn_W1, L0_gnn_a_src1, L0_gnn_a_dst1, L0_gnn_b1, L0_gnn_W2, L0_gnn_a_src2, L0_gnn_a_dst2, L0_gnn_b2)
    h = jnp.maximum(_layernorm(x, axis=-1), 0.0)
    x = x + _L1_gnn_ref(h, edge_attr_64, L1_gnn_Wn, L1_gnn_We, L1_gnn_Wa, src, dst)
    return x

_drawn_inputs = setup_inputs


def setup_inputs(seed=0):
    import zlib

    import numpy as np

    out = dict(_drawn_inputs(seed))
    spreads = {'L0_gnn_b1': (0.0, 0.1), 'L0_gnn_b2': (0.0, 0.1)}
    factors = {'L0_gnn_a_src1': 3.202,
     'L0_gnn_a_dst1': 21.398,
     'L0_gnn_a_src2': 6.023,
     'L0_gnn_a_dst2': 22.315}
    for name, (base, spread) in spreads.items():
        noise = np.random.default_rng([zlib.crc32(name.encode()), seed]).standard_normal(out[name].shape)
        drawn = base * np.exp(spread * noise) if base else spread * noise
        out[name] = jnp.asarray(drawn.astype(out[name].dtype))
    for name, factor in factors.items():
        out[name] = (out[name] * factor).astype(out[name].dtype)
    return out
```

```python
from contextlib import ExitStack

import concourse.bass as bass
from concourse import mybir

F32 = mybir.dt.float32
I32 = mybir.dt.int32
ALU = mybir.AluOpType
ACT = mybir.ActivationFunctionType
AX = mybir.AxisListType

P = 128
N = 50000
TILES_PER_GROUP = 4
GROUP = TILES_PER_GROUP * P
GROUPS = -(-N // GROUP)
ROUNDS = GROUPS // 2
TILES = GROUPS * TILES_PER_GROUP
PADDED = GROUPS * GROUP
TAIL = N - (GROUPS - 1) * GROUP
HEADS, HEAD_DIM, D = 16, 8, 128
D_EDGE = 64
ROW = D + 2 * HEADS
LOGIT_SRC = slice(D, D + HEADS)
LOGIT_DST = slice(D + HEADS, ROW)
WEIGHT = slice(D, D + HEADS)
MAXIMUM = slice(D + HEADS, ROW)
LOW = -1.0e30
NEG_SLOPE, EPS = 0.2, 1e-5
SKIP = 65536
NEUTRAL = PADDED
SEAM_CHUNK = 112
SEAM_CHUNKS = 2 * TILES // SEAM_CHUNK
SEAMS = 2 * TILES
HALVES = ((0, 4), (4, SEAM_CHUNKS))


def build(nc, x, src, dst, edge_attr, W1, a_src1, a_dst1, b1, W2, a_src2, a_dst2, b2, Wn, We, Wa, out):
    ctx = ExitStack()
    with ctx:
        def sb(name, shape, dt=F32):
            return ctx.enter_context(nc.sbuf_tensor(name, shape, dt))

        def sem(name):
            return ctx.enter_context(nc.semaphore(name))

        def dram(name, shape, dt=F32):
            return nc.dram_tensor(name, shape, dt, kind="Internal").ap()

        table = {k: dram(f"table{k}", [PADDED, ROW]) for k in (1, 2, 3)}
        partial = dram("partial", [PADDED + P, ROW])
        last_edge = dram("last_edge", [PADDED, 1], I32)
        residual = dram("residual", [PADDED, D])
        dst_row = dram("dst_row", [PADDED])
        run_marks = dram("run_marks", [GROUPS, 4, HEADS, 2, P])
        seam_dst = dram("seam_dst", [SEAMS + 2])

        ident = sb("ident", [P, P])
        ones = sb("ones", [P, P])
        head_mask = sb("head_mask", [P, HEADS])
        minus_half = sb("minus_half", [P, 4])
        neutral_rows = sb("neutral_rows", [P, ROW])
        w_ext = {k: sb(f"w_ext{k}", [P, ROW]) for k in (1, 2, 3)}
        wn_sb = sb("wn_sb", [P, P])
        we_sb = sb("we_sb", [P, D_EDGE])
        wT = sb("wT", [P, 2, P])
        att_cols = sb("att_cols", [P, 8])
        att_mat = sb("att_mat", [P, 3, 2 * HEADS])
        wa_rep = sb("wa_rep", [P, P])
        we_row = sb("we_row", [P, D_EDGE])
        b2_row = sb("b2_row", [P, P])

        src_g = sb("src_g", [GROUPS, GROUP], I32)
        dst_g = sb("dst_g", [GROUPS, GROUP], I32)
        next_g = sb("next_g", [GROUPS, GROUP], I32)
        srcf_g = sb("srcf_g", [GROUPS, GROUP])
        dstf_g = sb("dstf_g", [GROUPS, GROUP])
        nextf_g = sb("nextf_g", [GROUPS, GROUP])
        start_g = sb("start_g", [GROUPS, GROUP])
        end_g = sb("end_g", [GROUPS, GROUP])
        lastf_g = sb("lastf_g", [GROUPS, GROUP])
        default_g = sb("default_g", [GROUPS, GROUP], I32)
        src_i = sb("src_i", [P, TILES], I32)
        dst_i = sb("dst_i", [P, TILES], I32)
        dst_f = sb("dst_f", [P, TILES])
        last_i = sb("last_i", [P, TILES], I32)
        pos_i = sb("pos_i", [P, TILES], I32)

        seam_ends = sb("seam_ends", [GROUPS, 8])
        sentinels = sb("sentinels", [1, 2])
        seam_cur = sb("seam_cur", [P, SEAMS])
        seam_prev = sb("seam_prev", [P, SEAMS])
        seam_reset = sb("seam_reset", [P, SEAMS])
        seam_once = sb("seam_once", [P, SEAMS])
        seam_row_cur = sb("seam_row_cur", [SEAM_CHUNK, SEAM_CHUNKS])
        seam_row_next = sb("seam_row_next", [SEAM_CHUNK, SEAM_CHUNKS])
        seam_node_i = sb("seam_node_i", [SEAM_CHUNK, SEAM_CHUNKS], I32)
        seam_last_i = sb("seam_last_i", [SEAM_CHUNK, SEAM_CHUNKS], I32)
        seam_to_f = sb("seam_to_f", [SEAM_CHUNK, SEAM_CHUNKS])
        seam_to_i = sb("seam_to_i", [SEAM_CHUNK, SEAM_CHUNKS], I32)
        seam_rows = sb("seam_rows", [SEAM_CHUNK, SEAM_CHUNKS, ROW])
        seam_wide = sb("seam_wide", [SEAM_CHUNK, SEAM_CHUNKS, 2, D])
        seam_new = sb("seam_new", [SEAM_CHUNK, SEAM_CHUNKS, ROW])
        seam_max = sb("seam_max", [P, SEAMS + 1])
        seam_exp = sb("seam_exp", [P, 2, SEAMS])
        seam_sumw = sb("seam_sumw", [P, SEAMS])
        seam_sumx = sb("seam_sumx", [P, SEAMS])
        seam_w = sb("seam_w", [P, SEAMS])
        seam_x = sb("seam_x", [P, SEAMS])

        src_stage = [sb(f"src_stage{s}", [P, 4], I32) for s in range(2)]
        dst_stage = [sb(f"dst_stage{s}", [P, 4], I32) for s in range(2)]
        src_rows = [sb(f"src_rows{s}", [P, 4, ROW]) for s in range(2)]
        dst_logit = [sb(f"dst_logit{s}", [P, 4, HEADS]) for s in range(2)]
        marks = [sb(f"marks{s}", [64, 2, P]) for s in range(2)]
        dst_bc = [sb(f"dst_bc{s}", [P, 4, P]) for s in range(2)]
        attr = [sb(f"attr{s}", [P, 4, D_EDGE]) for s in range(2)]
        same = [sb(f"same{s}", [P, 4, P]) for s in range(2)]
        msg = [sb(f"msg{s}", [P, 4, D + HEADS]) for s in range(2)]
        part_rows = [sb(f"part_rows{s}", [P, 4, ROW]) for s in range(2)]
        attr_prod = sb("attr_prod", [P, 4, D_EDGE])
        attr_dot = sb("attr_dot", [P, 4])
        logit_sum = sb("logit_sum", [P, 4, HEADS])
        logit_all = sb("logit_all", [P, 4, HEADS])
        logit = sb("logit", [P, 4, HEADS])
        run_fwd = sb("run_fwd", [64, P])
        run_max = sb("run_max", [64, P])
        shifted = sb("shifted", [P, 4, HEADS])

        node_idx = [sb(f"node_idx{s}", [P, 4], I32) for s in range(2)]
        last_stage = [sb(f"last_stage{s}", [P, 4], I32) for s in range(2)]
        pos_stage = [sb(f"pos_stage{s}", [P, 4], I32) for s in range(2)]
        xin = [sb(f"xin{s}", [P, 4, D]) for s in range(2)]
        self_rows = [sb(f"self_rows{s}", [P, 4, ROW]) for s in range(2)]
        edge_part = [sb(f"edge_part{s}", [P, 4, ROW]) for s in range(2)]
        self_sum = sb("self_sum", [P, 4, HEADS])
        self_logit = sb("self_logit", [P, 4, HEADS])
        both_max = sb("both_max", [P, 4, HEADS])
        both_shift = sb("both_shift", [P, 4, 2, HEADS])
        both_w = sb("both_w", [P, 4, 2, HEADS])
        edge_w = sb("edge_w", [P, 4, HEADS])
        total_w = sb("total_w", [P, 4, HEADS])
        inv_w = sb("inv_w", [P, 4, HEADS])
        norm_w = sb("norm_w", [P, 4, 2, HEADS])
        from_edges = sb("from_edges", [P, 4, D])
        from_self = sb("from_self", [P, 4, D])
        merged = [sb(f"merged{s}", [P, 4, D]) for s in range(2)]
        with_x = sb("with_x", [P, 4, D])
        x1 = [sb(f"x1_{s}", [P, 4, D]) for s in range(2)]
        stats = sb("stats", [P, 4, 6])
        moments = sb("moments", [P, 4, 2])
        var_eps = [sb(f"var_eps{s}", [P, 4]) for s in range(2)]
        rstd = [sb(f"rstd{s}", [P, 4]) for s in range(2)]
        neg_mean = [sb(f"neg_mean{s}", [P, 4]) for s in range(2)]
        h = [sb(f"h{s}", [P, 4, D]) for s in range(2)]
        hT = [sb(f"hT{s}", [P, GROUP]) for s in range(2)]
        below = [sb(f"below{s}", [P, GROUP]) for s in range(2)]
        exp_below = [sb(f"exp_below{s}", [P, GROUP]) for s in range(2)]
        above = [sb(f"above{s}", [P, GROUP]) for s in range(2)]
        table_rows = [sb(f"table_rows{s}", [P, 4, ROW]) for s in range(2)]
        out_rows = [sb(f"out_rows{s}", [P, 4, D]) for s in range(2)]

        bank = [ctx.enter_context(nc.psum_tensor(f"bank{i}", [P, 512], F32)) for i in range(8)]
        ps_logitT, ps_maxT = bank[0], bank[1]
        ps_hT = [bank[2], bank[3]]
        ps_rows = [[bank[4], bank[5]], [bank[6], bank[7]]]

        def pair(b, width):
            return b[:, :].rearrange("p (j c) -> p j c", j=2)[:, :, 0:width]

        names = """consts weights att_mat w_T w_T_sb w_ext_ps w_ext_sb idx_in idx_f idx_start idx_mark idx_last
            idx_T idx_out idx_spread seam_mask seam_const neutral_out seam_loaded seam_wide seam_T seam_maxed seam_a seam_b
            seam_exped seam_c seam_scans seam_back seam_new seam_out seam_idx seam_node seam_lastd
            staged gather_round logit_sum attr_prod attr_dot logit_all logit logitT fwd bwd maxT
            same row_max shifted prob msg agg agg_out
            last_staged scatter_round part_round self_sum self_logit both_max both_shift both_exp edge_w total_w
            inv_w zero_w norm_w from_edges from_self merged with_x x1 stats stats_round moments var_eps rstd
            neg_mean h hT_ps hT below exp_below above elu proj table_v table_a out_row""".split()
        S = {n: sem("s_" + n) for n in names}
        slot_names = """marks dst_bc attr src_rows dst_logit part_out node_idx xin self_rows edge_part table_out
            x1_out out last_out""".split()
        SL = {n: [sem(f"s_{n}{i}") for i in range(2)] for n in slot_names}

        def done(passes, k, r, s):
            return GROUPS * passes.index(k) + 2 * r + s + 1

        def landed(passes, k, r, n=1):
            return 16 * n * (ROUNDS * passes.index(k) + r + 1)

        def after(eng, s, count):
            if not isinstance(count, int) or count > 0:
                eng.wait_ge(s, count)

        def rounds(eng, *stages):
            def one(r):
                for s in range(2):
                    for stage, lag in stages:
                        r2, s2 = r + (s - lag) // 2, (s - lag) % 2
                        if not isinstance(r2, int) or 0 <= r2 < ROUNDS:
                            stage(r2, s2)
            lags = -(-max(lag for _, lag in stages) // 2)
            for r in range(1 + lags):
                one(r)
            with eng.Fori(1 + lags, ROUNDS - 1) as r:
                one(r)
            for r in range(ROUNDS - 1, ROUNDS + lags):
                one(r)

        E = (1, 2, 3)
        def node_rows(t, r, s, rows=GROUP):
            g = 2 * r + s
            return t[bass.ds(g * GROUP, rows), :].rearrange("(p j) c -> p j c", j=4)

        def edge_rows(t, r, s):
            g = 2 * r + s
            return t[bass.ds(g * GROUP, GROUP), :].rearrange("(j p) c -> p j c", p=P)

        def is_last(r, s):
            return isinstance(r, int) and r == ROUNDS - 1 and s == 1

        def spread(t, j=4):
            return t.unsqueeze(3).broadcast_to((P, j, HEADS, HEAD_DIM))

        def by_head(t):
            return t.rearrange("p j (h c) -> p j h c", h=HEADS)

        block = ctx.enter_context(nc.Block())

        N_WEIGHTS = 11
        @block.sync
        def _(sp):
            col = lambda a: a.rearrange("h c -> (h c)").unsqueeze(1)
            for dst_ap, src_ap in (
                (w_ext[1][:, 0:D], W1), (w_ext[2][:, 0:D], W2), (wn_sb[:, :], Wn), (we_sb[:, :], We),
                (att_cols[:, 0:1], col(a_src1)), (att_cols[:, 1:2], col(a_dst1)),
                (att_cols[:, 2:3], col(a_src2)), (att_cols[:, 3:4], col(a_dst2)),
                (att_cols[:, 7:8], b1.unsqueeze(1)),
                (b2_row[:, :], b2.unsqueeze(0).broadcast_to((P, D))),
            ):
                sp.dma_start(dst_ap, src_ap).then_inc(S["weights"], 16)
            sp.dma_start(att_cols[:, 4:7], Wa.rearrange("a (s o) -> o (a s)", o=D),
                         allow_slow_non_contiguous=True).then_inc(S["weights"], 16)

            sp.wait_ge(S["consts"], 1)
            full = (GROUPS - 1) * GROUP
            for t, a, shift in ((src_g, src, 0), (dst_g, dst, 0), (next_g, dst, 1)):
                sp.dma_start(t[0:GROUPS - 1, :], a[shift:full + shift].rearrange("(g e) -> g e", e=GROUP))\
                  .then_inc(S["idx_in"], 16)
                sp.dma_start(t[GROUPS - 1:GROUPS, 0:TAIL - shift], a[full + shift:N].unsqueeze(0))\
                  .then_inc(S["idx_in"], 16)
            sp.dma_start(last_edge.rearrange("(g e) a -> g (e a)", e=GROUP), default_g[:, :])\
              .then_inc(S["neutral_out"], 16)
            sp.dma_start(partial[PADDED:PADDED + P, :], neutral_rows[:, :]).then_inc(S["neutral_out"], 16)

            sp.wait_ge(S["idx_mark"], 4)
            sp.dma_start(dst_row.rearrange("(g e) -> g e", e=GROUP), dstf_g[:, :]).then_inc(S["idx_spread"], 16)
            for head in range(HEADS):
                for m, t in enumerate((start_g, end_g)):
                    sp.dma_start(run_marks[:, :, head, m, :], t[:, :].rearrange("g (j e) -> g j e", e=P))\
                      .then_inc(S["idx_spread"], 16)
            sp.dma_start(seam_dst[1:SEAMS + 1].rearrange("(g i) -> g i", i=8), seam_ends[:, :])\
              .then_inc(S["seam_idx"], 16)
            sp.dma_start(seam_dst[0:1].unsqueeze(0), sentinels[0:1, 0:1]).then_inc(S["seam_idx"], 16)
            sp.dma_start(seam_dst[SEAMS + 1:SEAMS + 2].unsqueeze(0), sentinels[0:1, 1:2]).then_inc(S["seam_idx"], 16)
            sp.wait_ge(S["seam_idx"], 48)
            sp.dma_start(seam_cur[:, :], seam_dst[1:SEAMS + 1].unsqueeze(0).broadcast_to((P, SEAMS)))\
              .then_inc(S["seam_const"], 16)
            sp.dma_start(seam_prev[:, :], seam_dst[0:SEAMS].unsqueeze(0).broadcast_to((P, SEAMS)))\
              .then_inc(S["seam_const"], 16)
            for t, first in ((seam_row_cur, 1), (seam_row_next, 2)):
                sp.dma_start(t[:, :], seam_dst[first:first + SEAMS].rearrange("(c p) -> p c", p=SEAM_CHUNK),
                             allow_slow_non_contiguous=True).then_inc(S["seam_const"], 16)

            def load_x(k):
                passes = (0, 2, 3)
                def load(r, s):
                    if k == 0:
                        after(sp, S["h"], done((0, 2), 0, r, s) - 2)
                    if k == 2:
                        after(sp, S["with_x"] if not isinstance(r, int) or r > 0 else S["h"],
                              done((2,), 2, r, s) - 2 if not isinstance(r, int) or r > 0 else GROUPS)
                    if k == 3:
                        after(sp, S["out_row"] if not isinstance(r, int) or r > 0 else S["with_x"],
                              done((3,), 3, r, s) - 2 if not isinstance(r, int) or r > 0 else GROUPS)
                    if k == 3:
                        sp.dma_start(xin[s][:, :, :], node_rows(residual, r, s)).then_inc(SL["xin"][s], 16)
                    elif is_last(r, s):
                        sp.dma_start(xin[s][0:TAIL // 4, :, :], node_rows(x, r, s, TAIL)).then_inc(SL["xin"][s], 16)
                    else:
                        sp.dma_start(xin[s][:, :, :], node_rows(x, r, s)).then_inc(SL["xin"][s], 16)
                return load

            def load_node(k):
                def load(r, s):
                    after(sp, SL["edge_part"][s], landed(E, k, r, 4) - 64)
                    sp.dma_start(node_idx[s][:, :], node_rows(last_edge, r, s).rearrange("p j c -> p (j c)"))\
                      .then_inc(SL["node_idx"][s], 16)
                    if k < 3:
                        after(sp, S["from_self"], done((1, 2), k, r, s) - 2)
                        sp.dma_start(self_rows[s][:, :, :], node_rows(table[k], r, s))\
                          .then_inc(SL["self_rows"][s], 16)
                return load

            def store_table(k):
                def store(r, s):
                    sp.wait_ge(S["table_v"], done((0, 1, 2), k, r, s))
                    sp.wait_ge(S["table_a"], done((0, 1, 2), k, r, s))
                    sp.dma_start(node_rows(table[k + 1], r, s), table_rows[s][:, :, :])\
                      .then_inc(SL["table_out"][s], 16)
                return store

            def store_x1(r, s):
                sp.wait_ge(S["x1"], done((2,), 2, r, s))
                sp.dma_start(node_rows(residual, r, s), x1[s][:, :, :]).then_inc(SL["x1_out"][s], 16)

            def store_out(r, s):
                sp.wait_ge(S["out_row"], done((3,), 3, r, s))
                if is_last(r, s):
                    sp.dma_start(node_rows(out, r, s, TAIL), out_rows[s][0:TAIL // 4, :, :]).then_inc(SL["out"][s], 16)
                else:
                    sp.dma_start(node_rows(out, r, s), out_rows[s][:, :, :]).then_inc(SL["out"][s], 16)

            def load_edge(k):
                def load(r, s):
                    g = 2 * r + s
                    after(sp, S["bwd"], done(E, k, r, s) - 2)
                    sp.dma_start(marks[s][:, :, :],
                                 run_marks[bass.ds(g, 1), :, :, :, :].rearrange("g j h m e -> (g j h) m e"))\
                      .then_inc(SL["marks"][s], 16)
                    after(sp, S["same"], done(E, k, r, s) - 2)
                    sp.dma_start(dst_bc[s][:, :, :].rearrange("p j e -> p (j e)"),
                                 dst_row[bass.ds(g * GROUP, GROUP)].unsqueeze(0).broadcast_to((P, GROUP)))\
                      .then_inc(SL["dst_bc"][s], 16)
                    if k == 3:
                        after(sp, S["attr_prod"], done((3,), 3, r, s) - 2)
                        if is_last(r, s):
                            whole = TAIL // P
                            base = (GROUPS - 1) * GROUP
                            sp.dma_start(attr[s][:, 0:whole, :],
                                         edge_attr[base:base + whole * P, :].rearrange("(j p) c -> p j c", p=P))\
                              .then_inc(SL["attr"][s], 16)
                            sp.dma_start(attr[s][0:TAIL - whole * P, whole, :], edge_attr[base + whole * P:N, :])\
                              .then_inc(SL["attr"][s], 16)
                        else:
                            sp.dma_start(attr[s][:, :, :], edge_rows(edge_attr, r, s)).then_inc(SL["attr"][s], 16)
                return load

            def store_part(k):
                def store(r, s):
                    sp.wait_ge(S["agg_out"], done(E, k, r, s))
                    sp.wait_ge(S["row_max"], done(E, k, r, s))
                    sp.dma_start(edge_rows(partial, r, s), part_rows[s][:, :, :]).then_inc(SL["part_out"][s], 16)
                return store

            rounds(sp, (load_x(0), 0), (store_table(0), 2))
            for k in E:
                sp.wait_ge(S["idx_spread"], 16 * (1 + 2 * HEADS))
                rounds(sp, (load_edge(k), 0), (store_part(k), 1))
                for s in range(2):
                    sp.wait_ge(SL["part_out"][s], landed(E, k, ROUNDS - 1))
                if k > 1:
                    sp.wait_ge(S["seam_new"], k - 1)
                for end in range(2):
                    sp.dma_start(seam_rows[end:SEAM_CHUNK:2, :, :],
                                 partial[0:PADDED, :].rearrange("(c t p) w -> t c p w", p=P, c=SEAM_CHUNKS)[
                                     :, :, end * (P - 1), :]).then_inc(S["seam_loaded"], 16)
                if k < 3:
                    for s in range(2):
                        sp.wait_ge(SL["table_out"][s], landed((0, 1, 2), k - 1, ROUNDS - 1))
                if k == 1:
                    sp.wait_ge(S["neutral_out"], 32)
                    for s in range(2):
                        sp.wait_ge(SL["last_out"][s], landed((0,), 0, ROUNDS - 1, 4))
                    rounds(sp, (load_node(1), 0), (store_table(1), 3))
                elif k == 2:
                    rounds(sp, (load_node(2), 0), (load_x(2), 0), (store_x1, 1), (store_table(2), 3))
                else:
                    for s in range(2):
                        sp.wait_ge(SL["x1_out"][s], landed((2,), 2, ROUNDS - 1))
                    rounds(sp, (load_node(3), 0), (load_x(3), 0), (store_out, 1))
            for s in range(2):
                sp.wait_ge(SL["out"][s], landed((3,), 3, ROUNDS - 1))

        @block.gpsimd
        def _(pool):
            pool.memset(src_g[:, :], 0)
            pool.memset(dst_g[:, :], N)
            pool.memset(next_g[:, :], N)
            pool.memset(default_g[:, :], NEUTRAL)
            pool.memset(neutral_rows[:, 0:D + HEADS], 0.0)
            pool.memset(neutral_rows[:, MAXIMUM], LOW)
            pool.memset(sentinels[:, 0:1], -1.0)
            pool.memset(sentinels[:, 1:2], float(N))
            pool.memset(ones[:, :], 1.0)
            pool.memset(minus_half[:, :], -0.5)
            pool.memset(seam_max[:, 0:1], LOW)
            pool.iota(pos_i[:, :], pattern=[[P, TILES]], base=0, channel_multiplier=1)
            pool.memset(head_mask[:, :], 1.0)
            pool.memset(ident[:, :], 0.0).then_inc(S["consts"], 1)
            pool.wait_ge(S["consts"], 1)
            pool.affine_select(out=ident[:, :], in_=ident[:, :], compare_op=ALU.not_equal, fill=1.0,
                               base=0, pattern=[[-1, P]], channel_multiplier=1)
            pool.affine_select(out=head_mask[:, :], in_=head_mask[:, :], compare_op=ALU.is_ge, fill=0.0,
                               base=0, pattern=[[-HEAD_DIM, HEADS]], channel_multiplier=1).then_inc(S["consts"], 1)
            pool.wait_ge(S["consts"], 2)
            pool.affine_select(out=head_mask[:, :], in_=head_mask[:, :], compare_op=ALU.is_ge, fill=0.0,
                               base=HEAD_DIM - 1, pattern=[[HEAD_DIM, HEADS]], channel_multiplier=-1)\
                .then_inc(S["consts"], 1)
            node_limit = pool.to_reg(N - 1)
            row_limit = pool.to_reg(PADDED - 1)
            neutral_limit = pool.to_reg(NEUTRAL)
            part_limit = pool.to_reg(PADDED * ROW // HEADS - 1)

            def gather(to, frm, idx, limit, s):
                pool.indirect_dma_start(out=to, out_offset=None, in_=frm,
                                        in_offset=bass.IndirectOffsetOnAxis(ap=idx, axis=0),
                                        bounds_check=limit, oob_is_err=False).then_inc(s, 16)

            def scatter(to, frm, idx, limit, s):
                pool.indirect_dma_start(out=to, out_offset=bass.IndirectOffsetOnAxis(ap=idx, axis=0),
                                        in_=frm, in_offset=None,
                                        bounds_check=limit, oob_is_err=False).then_inc(s, 16)

            def rsqrt(k):
                def step(r, s):
                    pool.wait_ge(S["var_eps"], done((0, 2), k, r, s))
                    after(pool, S["neg_mean"], done((0, 2), k, r, s) - 2)
                    after(pool, S["h"], done((0, 2), k, r, s) - 2)
                    pool.tensor_tensor(rstd[s][:, :], var_eps[s][:, :], minus_half[:, :], ALU.pow)\
                        .then_inc(S["rstd"], 1)
                return step

            def scatter_last(r, s):
                pool.wait_ge(S["last_staged"], done((0,), 0, r, s))
                pool.sem_inc(S["scatter_round"], 1)
                for j in range(4):
                    scatter(last_edge[:, :], pos_stage[s][:, j:j + 1], last_stage[s][:, j:j + 1], node_limit,
                            SL["last_out"][s])

            def gather_edge(k):
                def step(r, s):
                    pool.wait_ge(S["staged"], done(E, k, r, s))
                    pool.sem_inc(S["gather_round"], 1)
                    for j in range(4):
                        gather(src_rows[s][:, j, :], table[k], src_stage[s][:, j:j + 1], row_limit, SL["src_rows"][s])
                        gather(dst_logit[s][:, j, :], table[k].rearrange("n (a b) -> (n a) b", b=HEADS),
                               dst_stage[s][:, j:j + 1], part_limit, SL["dst_logit"][s])
                return step

            def gather_part(k):
                def step(r, s):
                    pool.wait_ge(SL["node_idx"][s], landed(E, k, r))
                    pool.sem_inc(S["part_round"], 1)
                    after(pool, S["from_edges"], done(E, k, r, s) - 2)
                    pool.sem_inc(S["part_round"], 1)
                    for j in range(4):
                        gather(edge_part[s][:, j, :], partial[0:NEUTRAL + 1, :], node_idx[s][:, j:j + 1],
                               neutral_limit, SL["edge_part"][s])
                return step

            pool.wait_ge(S["neutral_out"], 32)
            rounds(pool, (scatter_last, 0), (rsqrt(0), 0))
            for s in range(2):
                pool.wait_ge(SL["last_out"][s], landed((0,), 0, ROUNDS - 1, 4))
            pool.wait_ge(S["seam_node"], 1)
            for c in range(SEAM_CHUNKS):
                gather(seam_last_i[:, c:c + 1], last_edge[:, :], seam_node_i[:, c:c + 1], row_limit, S["seam_lastd"])
            for k in E:
                for s in range(2):
                    pool.wait_ge(SL["table_out"][s], landed((0, 1, 2), k - 1, ROUNDS - 1))
                rounds(pool, (gather_edge(k), 0))
                pool.wait_ge(S["seam_new"], k)
                for c in range(SEAM_CHUNKS):
                    scatter(partial[0:PADDED, :], seam_new[:, c, :], seam_to_i[:, c:c + 1], row_limit, S["seam_out"])
                pool.wait_ge(S["seam_out"], 16 * SEAM_CHUNKS * k)
                if k == 2:
                    rounds(pool, (gather_part(k), 0), (rsqrt(2), 1))
                else:
                    rounds(pool, (gather_part(k), 0))

        @block.tensor
        def _(pe):
            pe.wait_ge(S["weights"], 16 * N_WEIGHTS)
            pe.wait_ge(S["consts"], 3)
            pe.transpose(bank[0][:, 0:P], w_ext[1][:, 0:D], ident[:, :])
            pe.transpose(bank[0][:, P:2 * P], w_ext[2][:, 0:D], ident[:, :])
            pe.transpose(bank[0][:, 2 * P:3 * P], wn_sb[:, :], ident[:, :]).then_inc(S["w_T"], 1)
            pe.wait_ge(S["w_T_sb"], 1)
            pe.wait_ge(S["att_mat"], 1)
            for i, lhs in enumerate((wT[:, 0, :], wT[:, 1, :], wn_sb[:, :])):
                pe.matmul(bank[1][:, 32 * i:32 * i + 32], lhs, att_mat[:, i, :], start=True, stop=True)
            pe.matmul(bank[1][:, 128:128 + D_EDGE], wa_rep[:, :], we_sb[:, :], start=True, stop=True)\
                .then_inc(S["w_ext_ps"], 1)
            for i, t in enumerate((srcf_g, dstf_g, lastf_g)):
                if i == 0:
                    pe.wait_ge(S["idx_f"], 1)
                if i == 2:
                    pe.wait_ge(S["idx_last"], 1)
                for j in range(4):
                    mm = pe.transpose(bank[4 + i][:, j * GROUPS:(j + 1) * GROUPS], t[:, j * P:(j + 1) * P],
                                      ident[0:GROUPS, 0:GROUPS])
                mm.then_inc(S["idx_T"], 1)
            pe.wait_ge(S["idx_out"], 3)

            def transpose_h(k):
                def step(r, s):
                    pe.wait_ge(S["h"] if k != 1 else S["merged"], done((0, 2) if k != 1 else (1, 2), k, r, s))
                    n = done((0, 1, 2), k, r, s) - 2
                    free(k, r, s)
                    rows = merged[s] if k == 1 else h[s]
                    for j in range(4):
                        mm = pe.transpose(ps_hT[s][:, j * P:(j + 1) * P], rows[:, j, :], ident[:, :])
                    mm.then_inc(S["hT_ps"], 1)
                return step

            def free(k, r, s):
                first = isinstance(r, int) and r == 0
                if k == 0:
                    after(pe, S["hT"], done((0, 2), 0, r, s) - 2)
                elif k == 1 and first:
                    pe.wait_ge(S["hT"], GROUPS)
                elif k == 1:
                    pe.wait_ge(S["below"], done((1,), 1, r, s) - 2)
                    pe.wait_ge(S["above"], done((1,), 1, r, s) - 2)
                elif first:
                    pe.wait_ge(S["above"], GROUPS)
                    pe.wait_ge(S["below"], GROUPS)
                else:
                    pe.wait_ge(S["hT"], done((0, 2), 2, r, s) - 2)

            def project(k):
                def step(r, s):
                    pe.wait_ge(S["hT"] if k != 1 else S["elu"], done((0, 2) if k != 1 else (1,), k, r, s))
                    after(pe, S["table_v"], done((0, 1, 2), k, r, s) - 2)
                    after(pe, S["table_a"], done((0, 1, 2), k, r, s) - 2)
                    for j in range(4):
                        o = (j % 2) * 256
                        mm = pe.matmul(ps_rows[s][j // 2][:, o:o + ROW], hT[s][:, j * P:(j + 1) * P],
                                       w_ext[k + 1][:, :], start=True, stop=True)
                    mm.then_inc(S["proj"], 1)
                return step

            def edge(k):
                def step(r, s):
                    pe.wait_ge(S["logit"], done(E, k, r, s))
                    after(pe, S["fwd"], done(E, k, r, s) - 1)
                    pe.matmul(ps_logitT[0:64, 0:P], logit[:, :, :].rearrange("p j h -> p (j h)"), ident[:, :],
                              start=True, stop=True).then_inc(S["logitT"], 1)
                    pe.wait_ge(S["bwd"], done(E, k, r, s))
                    after(pe, S["shifted"], done(E, k, r, s) - 1)
                    after(pe, S["row_max"], done(E, k, r, s) - 1)
                    pe.matmul(ps_maxT[:, 0:64], run_max[:, :], ident[0:64, 0:64], start=True, stop=True)\
                        .then_inc(S["maxT"], 1)
                    pe.wait_ge(S["msg"], done(E, k, r, s))
                    pe.wait_ge(S["same"], done(E, k, r, s))
                    after(pe, S["agg_out"], done(E, k, r, s) - 2)
                    for j in range(4):
                        o = (j % 2) * 256
                        mm = pe.matmul(ps_rows[s][j // 2][:, o:o + D + HEADS], same[s][:, j, :], msg[s][:, j, :],
                                       start=True, stop=True)
                    mm.then_inc(S["agg"], 1)
                return step

            def seam(k):
                pe.wait_ge(S["agg_out"], done(E, k, ROUNDS - 1, 1))
                pe.wait_ge(S["shifted"], done(E, k, ROUNDS - 1, 1))
                pe.wait_ge(S["row_max"], done(E, k, ROUNDS - 1, 1))
                pe.wait_ge(S["seam_loaded"], 32 * k)
                pe.wait_ge(S["seam_wide"], 2 * k)
                for half, (c0, c1) in enumerate(HALVES):
                    for c in range(c0, c1):
                        o = (c - c0) * SEAM_CHUNK
                        rows = seam_rows[:, c, :]
                        pe.transpose(bank[half][:, o:o + SEAM_CHUNK], rows[:, 0:D], ident[0:SEAM_CHUNK, 0:SEAM_CHUNK])
                        for i, b in enumerate((2, 4)):
                            mm = pe.transpose(bank[b + half][:, o:o + SEAM_CHUNK], seam_wide[:, c, i, :],
                                              ident[0:SEAM_CHUNK, 0:SEAM_CHUNK])
                mm.then_inc(S["seam_T"], 1)
                pe.wait_ge(S["seam_scans"], 2 * k)
                for b, t in ((0, seam_sumx[:, :]), (2, seam_sumw[:, :]), (4, seam_max[:, 1:SEAMS + 1])):
                    for c in range(SEAM_CHUNKS):
                        mm = pe.transpose(bank[b + c // 4][0:SEAM_CHUNK, (c % 4) * P:(c % 4 + 1) * P],
                                          t[:, c * SEAM_CHUNK:(c + 1) * SEAM_CHUNK], ident[:, :])
                mm.then_inc(S["seam_back"], 1)

            rounds(pe, (transpose_h(0), 0), (project(0), 1))
            for k in E:
                if k > 1:
                    pe.wait_ge(S["table_a"], GROUPS * k)
                    pe.wait_ge(S["table_v"], GROUPS * k)
                if k == 1:
                    pe.wait_ge(S["table_a"], GROUPS)
                    pe.wait_ge(S["table_v"], GROUPS)
                rounds(pe, (edge(k), 0))
                seam(k)
                pe.wait_ge(S["seam_new"], k)
                if k < 3:
                    rounds(pe, (transpose_h(k), 0), (project(k), 1))

        @block.scalar
        def _(act):
            def relu_rows(k):
                def step(r, s):
                    act.wait_ge(S["neg_mean"], done((0, 2), k, r, s))
                    n = done((0, 1, 2), k, r, s) - 2
                    if k == 0:
                        act.wait_ge(SL["xin"][s], landed((0, 2, 3), 0, r))
                        after(act, S["hT_ps"], n)
                    else:
                        act.wait_ge(S["hT_ps"], n)
                    rows = xin[s] if k == 0 else x1[s]
                    for j in range(4):
                        ins = act.activation(h[s][:, j, :], rows[:, j, :], ACT.Relu, bias=neg_mean[s][:, j:j + 1],
                                             scale=rstd[s][:, j:j + 1])
                    ins.then_inc(S["h"], 1)
                return step

            def copy_hT(k):
                def step(r, s):
                    act.wait_ge(S["hT_ps"], done((0, 1, 2), k, r, s))
                    after(act, S["proj"], done((0, 1, 2), k, r, s) - 2)
                    act.activation(hT[s][:, :], ps_hT[s][:, :], ACT.Copy).then_inc(S["hT"], 1)
                return step

            def elu_parts(r, s):
                act.wait_ge(S["hT_ps"], done((0, 1, 2), 1, r, s))
                after(act, S["elu"], done((1,), 1, r, s) - 2)
                act.activation(above[s][:, :], ps_hT[s][:, :], ACT.Relu, bias=att_cols[:, 7:8]).then_inc(S["above"], 1)
                act.wait_ge(S["below"], done((1,), 1, r, s))
                act.activation(exp_below[s][:, :], below[s][:, :], ACT.Exp).then_inc(S["exp_below"], 1)

            def evac(k):
                def step(r, s):
                    act.wait_ge(S["proj"], done((0, 1, 2), k, r, s))
                    after(act, SL["table_out"][s], landed((0, 1, 2), k, r) - 16)
                    act.activation(table_rows[s][:, 2:4, :], pair(ps_rows[s][1], ROW), ACT.Copy)\
                        .then_inc(S["table_a"], 1)
                return step

            def merge_exp(k):
                def step(r, s):
                    act.wait_ge(S["both_shift"], done((1, 2), k, r, s))
                    after(act, S["norm_w"], done((1, 2), k, r, s) - 1)
                    act.activation(both_w[:, :, :, :], both_shift[:, :, :, :], ACT.Exp).then_inc(S["both_exp"], 1)
                return step

            def edge(k):
                def step(r, s):
                    act.wait_ge(S["shifted"], done(E, k, r, s))
                    after(act, S["agg"], done(E, k, r, s) - 2)
                    act.activation(msg[s][:, :, D:D + HEADS], shifted[:, :, :], ACT.Exp).then_inc(S["prob"], 1)
                    act.wait_ge(S["agg"], done(E, k, r, s))
                    after(act, SL["part_out"][s], landed(E, k, r) - 16)
                    act.activation(part_rows[s][:, 0:2, 0:D + HEADS], pair(ps_rows[s][0], D + HEADS), ACT.Copy)
                    act.activation(part_rows[s][:, 2:4, 0:D + HEADS], pair(ps_rows[s][1], D + HEADS), ACT.Copy)\
                        .then_inc(S["agg_out"], 1)
                return step

            rounds(act, (relu_rows(0), 0), (copy_hT(0), 0), (evac(0), 1))
            for k in E:
                rounds(act, (edge(k), 0))
                act.wait_ge(S["seam_b"], 2 * k)
                act.activation(seam_exp[:, :, :], seam_exp[:, :, :], ACT.Exp).then_inc(S["seam_exped"], 1)
                if k == 1:
                    rounds(act, (merge_exp(1), 0), (elu_parts, 1), (evac(1), 2))
                if k == 2:
                    rounds(act, (merge_exp(2), 0), (relu_rows(2), 1), (copy_hT(2), 1), (evac(2), 2))

        @block.vector
        def _(dve):
            dve.wait_ge(S["weights"], 16 * N_WEIGHTS)
            dve.wait_ge(S["consts"], 3)
            for i in range(2):
                for j in range(2):
                    c = 2 * i + j
                    dve.tensor_scalar(att_mat[:, i, HEADS * j:HEADS * j + HEADS], head_mask[:, :],
                                      att_cols[:, c:c + 1], None, ALU.mult)
            for j in range(2):
                dve.tensor_scalar(att_mat[:, 2, HEADS * j:HEADS * j + HEADS], ones[:, 0:HEADS],
                                  att_cols[:, 4 + j:5 + j], None, ALU.mult)
            dve.tensor_scalar(wa_rep[:, :], ones[:, :], att_cols[:, 6:7], None, ALU.mult).then_inc(S["att_mat"], 1)
            dve.wait_ge(S["w_T"], 1)
            dve.tensor_copy(w_ext[3][:, 0:D], bank[0][:, 2 * P:3 * P])
            dve.tensor_copy(wT[:, :, :], bank[0][:, 0:2 * P].rearrange("p (a b) -> p a b", a=2))\
                .then_inc(S["w_T_sb"], 1)
            dve.wait_ge(S["w_ext_ps"], 1)
            for i in range(3):
                dve.tensor_copy(w_ext[i + 1][:, D:ROW], bank[1][:, 32 * i:32 * i + 32])
            dve.tensor_copy(we_row[:, :], bank[1][:, 128:128 + D_EDGE]).then_inc(S["w_ext_sb"], 1)

            dve.wait_ge(S["idx_in"], 96)
            dve.tensor_copy(srcf_g[:, :], src_g[:, :])
            dve.tensor_copy(dstf_g[:, :], dst_g[:, :])
            dve.tensor_copy(nextf_g[:, :], next_g[:, :]).then_inc(S["idx_f"], 1)
            dve.wait_ge(S["idx_f"], 1)
            dve.tensor_tensor(end_g[:, :], dstf_g[:, :], nextf_g[:, :], ALU.not_equal)
            dve.memset(start_g[:, 0:1], 1.0)
            dve.tensor_tensor(start_g[:, 1:GROUP], dstf_g[:, 1:GROUP], dstf_g[:, 0:GROUP - 1], ALU.not_equal)\
                .then_inc(S["idx_start"], 1)
            dve.wait_ge(S["idx_start"], 1)
            dve.tensor_scalar(lastf_g[:, :], end_g[:, :], -float(SKIP), float(SKIP), ALU.mult, ALU.add)\
                .then_inc(S["idx_start"], 1)
            dve.wait_ge(S["idx_start"], 2)
            dve.tensor_tensor(lastf_g[:, :], lastf_g[:, :], dstf_g[:, :], ALU.add).then_inc(S["idx_last"], 1)
            dve.tensor_scalar(end_g[:, :], end_g[:, :], LOW, None, ALU.mult).then_inc(S["idx_mark"], 1)
            dve.tensor_scalar(start_g[:, :], start_g[:, :], LOW, None, ALU.mult).then_inc(S["idx_mark"], 1)
            ends = dstf_g[:, :].rearrange("g (j e) -> g j e", e=P)[:, :, 0:P:P - 1]
            dve.tensor_copy(seam_ends[:, :].rearrange("g (j i) -> g j i", i=2), ends).then_inc(S["idx_mark"], 2)
            tile_major = lambda t: t[:, :].rearrange("p (g j) -> p j g", j=4)
            by_tile = lambda b: b[:, 0:TILES].rearrange("p (j g) -> p j g", j=4)
            dve.wait_ge(S["idx_T"], 1)
            dve.tensor_copy(tile_major(src_i), by_tile(bank[4])).then_inc(S["idx_out"], 1)
            dve.wait_ge(S["idx_T"], 2)
            dve.tensor_copy(tile_major(dst_f), by_tile(bank[5]))
            width = ROW // HEADS
            dve.tensor_scalar(tile_major(dst_i), by_tile(bank[5]), float(width), float(width - 1), ALU.mult, ALU.add)\
                .then_inc(S["idx_out"], 1)
            dve.wait_ge(S["idx_T"], 3)
            dve.tensor_copy(tile_major(last_i), by_tile(bank[6])).then_inc(S["idx_out"], 1)
            dve.wait_ge(S["seam_const"], 64)
            dve.tensor_tensor(seam_cur[:, :], seam_cur[:, :], seam_prev[:, :], ALU.is_equal).then_inc(S["seam_mask"], 1)
            dve.tensor_copy(seam_node_i[:, :], seam_row_cur[:, :]).then_inc(S["seam_node"], 1)
            dve.tensor_tensor(seam_to_f[:, :], seam_row_cur[:, :], seam_row_next[:, :], ALU.is_equal)
            dve.memset(seam_once[:, :], 1.0).then_inc(S["seam_mask"], 1)
            dve.wait_ge(S["seam_mask"], 2)
            dve.tensor_scalar(seam_reset[:, :], seam_cur[:, :], -LOW, LOW, ALU.mult, ALU.add)
            dve.tensor_scalar(seam_once[:, 1:SEAMS:2], seam_cur[:, 1:SEAMS:2], -1.0, 1.0, ALU.mult, ALU.add)\
                .then_inc(S["seam_mask"], 1)
            dve.wait_ge(S["seam_mask"], 3)
            dve.wait_ge(S["idx_out"], 3)
            dve.wait_ge(S["w_ext_sb"], 1)

            def stage_last(r, s):
                g = 2 * r + s
                after(dve, SL["last_out"][s], landed((0,), 0, r, 4) - 64)
                dve.tensor_scalar(last_stage[s][:, :], last_i[:, bass.ds(g * 4, 4)], 0.0, None, ALU.add)
                dve.tensor_scalar(pos_stage[s][:, :], pos_i[:, bass.ds(g * 4, 4)], 0.0, None, ALU.add)\
                    .then_inc(S["last_staged"], 1)

            def norm_stats(k):
                L = (0, 2)
                def step(r, s):
                    if k == 0:
                        dve.wait_ge(SL["xin"][s], landed((0, 2, 3), 0, r))
                    else:
                        dve.wait_ge(S["x1"], done((2,), 2, r, s))
                    rows = xin[s] if k == 0 else x1[s]
                    for j in range(4):
                        ins = dve.bn_stats(stats[:, j, :], rows[:, j, :])
                    ins.then_inc(S["stats"], 1)
                    dve.wait_ge(S["stats"], done(L, k, r, s))
                    dve.sem_inc(S["stats_round"], 1)
                    for j in range(4):
                        ins = dve.bn_aggr(moments[:, j, :], stats[:, j, :])
                    ins.then_inc(S["moments"], 1)
                    dve.wait_ge(S["moments"], done(L, k, r, s))
                    dve.tensor_scalar(var_eps[s][:, :], moments[:, :, 1], EPS, None, ALU.add).then_inc(S["var_eps"], 1)
                    dve.wait_ge(S["rstd"], done(L, k, r, s))
                    after(dve, S["h"], done(L, k, r, s) - 2)
                    dve.scalar_tensor_tensor(out=neg_mean[s][:, :], in0=moments[:, :, 0], scalar=-1.0,
                                             in1=rstd[s][:, :], op0=ALU.mult, op1=ALU.mult).then_inc(S["neg_mean"], 1)
                return step

            def evac(k):
                def step(r, s):
                    dve.wait_ge(S["proj"], done((0, 1, 2), k, r, s))
                    after(dve, SL["table_out"][s], landed((0, 1, 2), k, r) - 16)
                    dve.tensor_copy(table_rows[s][:, 0:2, :], pair(ps_rows[s][0], ROW)).then_inc(S["table_v"], 1)
                return step

            def stage_edge(k, r, s):
                g = 2 * r + s
                dve.tensor_scalar(src_stage[s][:, :], src_i[:, bass.ds(g * 4, 4)], 0.0, None, ALU.add)
                dve.tensor_scalar(dst_stage[s][:, :], dst_i[:, bass.ds(g * 4, 4)], 0.0, None, ALU.add)\
                    .then_inc(S["staged"], 1)

            def edge(k):
                def step(r, s):
                    n = done(E, k, r, s)
                    if k == 3:
                        dve.wait_ge(SL["attr"][s], 16 * (r + 1) + (16 if is_last(r, s) else 0))
                        dve.tensor_tensor(attr_prod[:, :, :], attr[s][:, :, :],
                                          we_row[:, :].unsqueeze(1).broadcast_to((P, 4, D_EDGE)), ALU.mult)\
                            .then_inc(S["attr_prod"], 1)
                        dve.wait_ge(S["attr_prod"], done((3,), 3, r, s))
                        dve.tensor_reduce(attr_dot[:, :], attr_prod[:, :, :], AX.X, ALU.add).then_inc(S["attr_dot"], 1)
                    dve.wait_ge(SL["dst_bc"][s], landed(E, k, r))
                    after(dve, S["agg"], n - 2)
                    g = 2 * r + s
                    dve.tensor_tensor(same[s][:, :, :], dst_bc[s][:, :, :],
                                      dst_f[:, bass.ds(g * 4, 4)].unsqueeze(2).broadcast_to((P, 4, P)), ALU.is_equal)\
                        .then_inc(S["same"], 1)
                    dve.wait_ge(SL["src_rows"][s], landed(E, k, r, 4))
                    dve.wait_ge(SL["dst_logit"][s], landed(E, k, r, 4))
                    dve.tensor_tensor(logit_sum[:, :, :], src_rows[s][:, :, LOGIT_SRC], dst_logit[s][:, :, :], ALU.add)\
                        .then_inc(S["logit_sum"], 1)
                    dve.wait_ge(S["logit_sum"], n)
                    summed = logit_sum
                    if k == 3:
                        dve.wait_ge(S["attr_dot"], done((3,), 3, r, s))
                        dve.tensor_tensor(logit_all[:, :, :], logit_sum[:, :, :],
                                          attr_dot[:, :].unsqueeze(2).broadcast_to((P, 4, HEADS)), ALU.add)\
                            .then_inc(S["logit_all"], 1)
                        dve.wait_ge(S["logit_all"], done((3,), 3, r, s))
                        summed = logit_all
                    dve.scalar_tensor_tensor(out=logit[:, :, :], in0=summed[:, :, :], scalar=NEG_SLOPE,
                                             in1=summed[:, :, :], op0=ALU.mult, op1=ALU.max).then_inc(S["logit"], 1)
                    dve.wait_ge(S["logitT"], n)
                    dve.wait_ge(SL["marks"][s], landed(E, k, r))
                    dve.tensor_tensor_scan(run_fwd[:, :], marks[s][:, 0, :], ps_logitT[0:64, 0:P], LOW,
                                           ALU.add, ALU.max).then_inc(S["fwd"], 1)
                    dve.wait_ge(S["fwd"], n)
                    dve.tensor_tensor_scan(run_max[:, ::-1], marks[s][:, 1, ::-1], run_fwd[:, ::-1], LOW,
                                           ALU.add, ALU.max).then_inc(S["bwd"], 1)
                    dve.wait_ge(S["maxT"], n)
                    maxima = ps_maxT[:, 0:64].rearrange("p (j h) -> p j h", h=HEADS)
                    dve.tensor_tensor(shifted[:, :, :], logit[:, :, :], maxima, ALU.subtract).then_inc(S["shifted"], 1)
                    after(dve, SL["part_out"][s], landed(E, k, r) - 16)
                    dve.tensor_copy(part_rows[s][:, :, MAXIMUM], maxima).then_inc(S["row_max"], 1)
                    dve.wait_ge(S["prob"], n)
                    dve.tensor_tensor(by_head(msg[s][:, :, 0:D]), by_head(src_rows[s][:, :, 0:D]),
                                      spread(msg[s][:, :, D:D + HEADS]), ALU.mult).then_inc(S["msg"], 1)
                    dve.wait_ge(S["msg"], n)
                    if not isinstance(r, int) or r < ROUNDS - 1:
                        stage_edge(k, r + 1, s)
                return step

            def seam(k):
                if k == 1:
                    dve.wait_ge(S["seam_lastd"], 16 * SEAM_CHUNKS)
                    dve.scalar_tensor_tensor(out=seam_to_i[:, :], in0=seam_to_f[:, :], scalar=float(SKIP),
                                             in1=seam_last_i[:, :], op0=ALU.mult, op1=ALU.add)
                dve.wait_ge(S["seam_loaded"], 32 * k)
                for i, part in enumerate((WEIGHT, MAXIMUM)):
                    dve.tensor_copy(seam_wide[:, :, i, :].rearrange("p c (h d) -> p c h d", h=HEADS),
                                    seam_rows[:, :, part].unsqueeze(3).broadcast_to(
                                        (SEAM_CHUNK, SEAM_CHUNKS, HEADS, HEAD_DIM))).then_inc(S["seam_wide"], 1)
                dve.wait_ge(S["seam_T"], k)
                cols = [(c0 * SEAM_CHUNK, c1 * SEAM_CHUNK) for c0, c1 in HALVES]
                for half, (a, b) in enumerate(cols):
                    if half:
                        dve.wait_ge(S["seam_maxed"], 2 * k - 1)
                    dve.tensor_tensor_scan(seam_max[:, 1 + a:1 + b], seam_reset[:, a:b], bank[4 + half][:, 0:b - a],
                                           seam_max[:, a:a + 1], ALU.add, ALU.max).then_inc(S["seam_maxed"], 1)
                dve.wait_ge(S["seam_maxed"], 2 * k)
                dve.tensor_tensor(seam_w[:, :], seam_max[:, 0:SEAMS], seam_reset[:, :], ALU.add).then_inc(S["seam_a"], 1)
                dve.wait_ge(S["seam_a"], k)
                dve.tensor_tensor(seam_exp[:, 0, :], seam_w[:, :], seam_max[:, 1:SEAMS + 1], ALU.subtract)\
                    .then_inc(S["seam_b"], 1)
                for half, (a, b) in enumerate(cols):
                    ins = dve.tensor_tensor(seam_exp[:, 1, a:b], bank[4 + half][:, 0:b - a], seam_max[:, 1 + a:1 + b],
                                            ALU.subtract)
                ins.then_inc(S["seam_b"], 1)
                dve.wait_ge(S["seam_exped"], k)
                dve.tensor_tensor(seam_x[:, :], seam_exp[:, 1, :], seam_once[:, :], ALU.mult).then_inc(S["seam_c"], 1)
                dve.wait_ge(S["seam_c"], 3 * k - 2)
                for half, (a, b) in enumerate(cols):
                    ins = dve.tensor_tensor(seam_w[:, a:b], seam_x[:, a:b], bank[2 + half][:, 0:b - a], ALU.mult)
                ins.then_inc(S["seam_c"], 1)
                dve.wait_ge(S["seam_c"], 3 * k - 1)
                for half, (a, b) in enumerate(cols):
                    ins = dve.tensor_tensor(seam_x[:, a:b], seam_x[:, a:b], bank[half][:, 0:b - a], ALU.mult)
                ins.then_inc(S["seam_c"], 1)
                dve.tensor_tensor_scan(seam_sumw[:, :], seam_exp[:, 0, :], seam_w[:, :], 0.0, ALU.mult, ALU.add)\
                    .then_inc(S["seam_scans"], 1)
                dve.wait_ge(S["seam_c"], 3 * k)
                dve.tensor_tensor_scan(seam_sumx[:, :], seam_exp[:, 0, :], seam_x[:, :], 0.0, ALU.mult, ALU.add)\
                    .then_inc(S["seam_scans"], 1)
                dve.wait_ge(S["seam_back"], k)
                if k > 1:
                    dve.wait_ge(S["seam_out"], 16 * SEAM_CHUNKS * (k - 1))
                for half in range(2):
                    c0, c1 = 4 * half, min(4 * half + 4, SEAM_CHUNKS)
                    for b, part, step in ((0, slice(0, D), 1), (2, WEIGHT, HEAD_DIM), (4, MAXIMUM, HEAD_DIM)):
                        got = bank[b + half][0:SEAM_CHUNK, 0:(c1 - c0) * P].rearrange("p (c f) -> p c f", f=P)
                        ins = dve.tensor_copy(seam_new[:, c0:c1, part], got[:, :, 0:P:step])
                ins.then_inc(S["seam_new"], 1)

            M = (1, 2)
            def merge(k):
                def step(r, s):
                    n = done(M, k, r, s)
                    dve.wait_ge(SL["self_rows"][s], landed(M, k, r))
                    dve.tensor_tensor(self_sum[:, :, :], self_rows[s][:, :, LOGIT_SRC], self_rows[s][:, :, LOGIT_DST],
                                      ALU.add).then_inc(S["self_sum"], 1)
                    dve.wait_ge(S["self_sum"], n)
                    dve.scalar_tensor_tensor(out=self_logit[:, :, :], in0=self_sum[:, :, :], scalar=NEG_SLOPE,
                                             in1=self_sum[:, :, :], op0=ALU.mult, op1=ALU.max)\
                        .then_inc(S["self_logit"], 1)
                    dve.wait_ge(S["self_logit"], n)
                    dve.wait_ge(SL["edge_part"][s], landed(E, k, r, 4))
                    dve.tensor_tensor(both_max[:, :, :], self_logit[:, :, :], edge_part[s][:, :, MAXIMUM], ALU.max)\
                        .then_inc(S["both_max"], 1)
                    dve.wait_ge(S["both_max"], n)
                    dve.tensor_tensor(both_shift[:, :, 0, :], edge_part[s][:, :, MAXIMUM], both_max[:, :, :], ALU.subtract)
                    dve.tensor_tensor(both_shift[:, :, 1, :], self_logit[:, :, :], both_max[:, :, :], ALU.subtract)\
                        .then_inc(S["both_shift"], 1)
                    dve.wait_ge(S["both_exp"], n)
                    dve.tensor_tensor(edge_w[:, :, :], edge_part[s][:, :, WEIGHT], both_w[:, :, 0, :], ALU.mult)\
                        .then_inc(S["edge_w"], 1)
                    dve.wait_ge(S["edge_w"], n)
                    dve.scalar_tensor_tensor(out=total_w[:, :, :], in0=edge_w[:, :, :], scalar=1e-16,
                                             in1=both_w[:, :, 1, :], op0=ALU.add, op1=ALU.add).then_inc(S["total_w"], 1)
                    dve.wait_ge(S["total_w"], done(E, k, r, s))
                    dve.reciprocal(inv_w[:, :, :], total_w[:, :, :]).then_inc(S["inv_w"], 1)
                    dve.wait_ge(S["inv_w"], done(E, k, r, s))
                    dve.tensor_tensor(norm_w[:, :, :, :], both_w[:, :, :, :],
                                      inv_w[:, :, :].unsqueeze(2).broadcast_to((P, 4, 2, HEADS)), ALU.mult)\
                        .then_inc(S["norm_w"], 1)
                    dve.wait_ge(S["norm_w"], n)
                    dve.tensor_tensor(by_head(from_edges[:, :, :]), by_head(edge_part[s][:, :, 0:D]),
                                      spread(norm_w[:, :, 0, :]), ALU.mult).then_inc(S["from_edges"], 1)
                    dve.tensor_tensor(by_head(from_self[:, :, :]), by_head(self_rows[s][:, :, 0:D]),
                                      spread(norm_w[:, :, 1, :]), ALU.mult).then_inc(S["from_self"], 1)
                    dve.wait_ge(S["from_edges"], done(E, k, r, s))
                    dve.wait_ge(S["from_self"], n)
                    if k == 1:
                        after(dve, S["hT_ps"], done((0, 1, 2), 1, r, s) - 2)
                    dve.tensor_tensor(merged[s][:, :, :], from_edges[:, :, :], from_self[:, :, :], ALU.add)\
                        .then_inc(S["merged"], 1)
                    if k == 2:
                        dve.wait_ge(S["merged"], n)
                        dve.tensor_tensor(with_x[:, :, :], merged[s][:, :, :],
                                          b2_row[:, :].unsqueeze(1).broadcast_to((P, 4, D)), ALU.add)\
                            .then_inc(S["with_x"], 1)
                        dve.wait_ge(S["with_x"], done((2,), 2, r, s))
                        dve.wait_ge(SL["xin"][s], landed((0, 2, 3), 2, r))
                        after(dve, SL["x1_out"][s], landed((2,), 2, r) - 16)
                        after(dve, S["h"], done((0, 2), 2, r, s) - 2)
                        dve.tensor_tensor(x1[s][:, :, :], with_x[:, :, :], xin[s][:, :, :], ALU.add)\
                            .then_inc(S["x1"], 1)
                return step

            def below_zero(r, s):
                dve.wait_ge(S["hT_ps"], done((0, 1, 2), 1, r, s))
                after(dve, S["exp_below"], done((1,), 1, r, s) - 2)
                dve.wait_ge(S["above"], done((1,), 1, r, s))
                dve.tensor_scalar(below[s][:, :], ps_hT[s][:, :], att_cols[:, 7:8], 0.0, ALU.add, ALU.min)\
                    .then_inc(S["below"], 1)

            def elu(r, s):
                dve.wait_ge(S["exp_below"], done((1,), 1, r, s))
                dve.wait_ge(S["above"], done((1,), 1, r, s))
                after(dve, S["proj"], done((0, 1, 2), 1, r, s) - 2)
                dve.scalar_tensor_tensor(out=hT[s][:, :], in0=exp_below[s][:, :], scalar=-1.0, in1=above[s][:, :],
                                         op0=ALU.add, op1=ALU.add).then_inc(S["elu"], 1)

            def finish(r, s):
                n = done(E, 3, r, s)
                dve.wait_ge(SL["edge_part"][s], landed(E, 3, r, 4))
                dve.tensor_scalar(edge_w[:, :, :], edge_part[s][:, :, WEIGHT], 0.0, None, ALU.is_equal)\
                    .then_inc(S["zero_w"], 1)
                dve.wait_ge(S["zero_w"], done((3,), 3, r, s))
                dve.tensor_tensor(total_w[:, :, :], edge_w[:, :, :], edge_part[s][:, :, WEIGHT], ALU.add)\
                    .then_inc(S["total_w"], 1)
                dve.wait_ge(S["total_w"], n)
                dve.reciprocal(inv_w[:, :, :], total_w[:, :, :]).then_inc(S["inv_w"], 1)
                dve.wait_ge(S["inv_w"], n)
                dve.tensor_tensor(by_head(from_edges[:, :, :]), by_head(edge_part[s][:, :, 0:D]),
                                  spread(inv_w[:, :, :]), ALU.mult).then_inc(S["from_edges"], 1)
                dve.wait_ge(S["from_edges"], n)
                dve.wait_ge(SL["xin"][s], landed((0, 2, 3), 3, r))
                after(dve, SL["out"][s], landed((3,), 3, r) - 16)
                dve.tensor_tensor(out_rows[s][:, :, :], from_edges[:, :, :], xin[s][:, :, :], ALU.add)\
                    .then_inc(S["out_row"], 1)

            rounds(dve, (stage_last, 0), (norm_stats(0), 0), (evac(0), 1))
            for k in E:
                for s in range(2):
                    stage_edge(k, 0, s)
                rounds(dve, (edge(k), 0))
                seam(k)
                if k == 1:
                    rounds(dve, (merge(1), 0), (below_zero, 1), (evac(1), 2), (elu, 1))
                elif k == 2:
                    rounds(dve, (merge(2), 0), (norm_stats(2), 0), (evac(2), 2))
                else:
                    rounds(dve, (finish, 0))


_INS = ['x', 'src', 'dst', 'edge_attr_64', 'L0_gnn_W1', 'L0_gnn_a_src1', 'L0_gnn_a_dst1', 'L0_gnn_b1', 'L0_gnn_W2',
        'L0_gnn_a_src2', 'L0_gnn_a_dst2', 'L0_gnn_b2', 'L1_gnn_Wn', 'L1_gnn_We', 'L1_gnn_Wa']


def kernel(**inputs):
    import numpy as _np
    import concourse.bacc as _bacc
    from concourse import mybir as _mybir
    from concourse.bass_utils import run_bass_kernel_spmd as _run

    nc = _bacc.Bacc("TRN2", target_bir_lowering=False, num_devices=1)
    arrays, args = {}, []
    for name in _INS:
        a = _np.ascontiguousarray(inputs[name])
        arrays[f"in_{name}"] = a
        args.append(nc.dram_tensor(f"in_{name}", a.shape, _mybir.dt.from_np(a.dtype), kind="ExternalInput").ap())
    args.append(nc.dram_tensor("out_0", (N, D), _mybir.dt.float32, kind="ExternalOutput").ap())
    build(nc, *args)
    r = _run(nc, [arrays], core_ids=[0])
    return r.results[0]["out_0"]
```

```python
from contextlib import ExitStack

import concourse.bass as bass
from concourse import mybir

F32 = mybir.dt.float32
I32 = mybir.dt.int32
ALU = mybir.AluOpType
ACT = mybir.ActivationFunctionType
AX = mybir.AxisListType

P = 128
N = 50000
TILES_PER_GROUP = 4
GROUP = TILES_PER_GROUP * P
GROUPS = -(-N // GROUP)
STEPS = 4
ROUNDS = -(-GROUPS // STEPS)
TILES = GROUPS * TILES_PER_GROUP
PADDED = GROUPS * GROUP
TAIL = N - (GROUPS - 1) * GROUP
HEADS, HEAD_DIM, D = 16, 8, 128
D_EDGE = 64
ROW = D + 2 * HEADS
LOGIT_SRC = slice(D, D + HEADS)
LOGIT_DST = slice(D + HEADS, ROW)
WEIGHT = slice(D, D + HEADS)
MAXIMUM = slice(D + HEADS, ROW)
LOW = -1.0e30
NEG_SLOPE, EPS = 0.2, 1e-5
SKIP = 65536
NEUTRAL = PADDED
SEAM_CHUNK = 112
SEAM_CHUNKS = 2 * TILES // SEAM_CHUNK
SEAMS = 2 * TILES
HALVES = ((0, 4), (4, SEAM_CHUNKS))


def build(nc, x, src, dst, edge_attr, W1, a_src1, a_dst1, b1, W2, a_src2, a_dst2, b2, Wn, We, Wa, out):
    ctx = ExitStack()
    with ctx:
        def sb(name, shape, dt=F32):
            return ctx.enter_context(nc.sbuf_tensor(name, shape, dt))

        def slots(name, shape, dt=F32, n=2):
            made = [sb(f"{name}{i}", shape, dt) for i in range(n)]
            return [made[i % n] for i in range(STEPS)]

        def sem(name):
            return ctx.enter_context(nc.semaphore(name))

        def dram(name, shape, dt=F32):
            return nc.dram_tensor(name, shape, dt, kind="Internal").ap()

        table = {k: dram(f"table{k}", [PADDED, ROW]) for k in (1, 2, 3)}
        partial = dram("partial", [PADDED + P, ROW])
        last_edge = dram("last_edge", [PADDED, 1], I32)
        residual = dram("residual", [PADDED, D])
        dst_row = dram("dst_row", [PADDED])
        run_marks = dram("run_marks", [GROUPS, 4, HEADS, 2, P])
        seam_dst = dram("seam_dst", [SEAMS + 2])

        ident = sb("ident", [P, P])
        ones = sb("ones", [P, P])
        head_mask = sb("head_mask", [P, HEADS])
        minus_half = sb("minus_half", [P, 4])
        neutral_rows = sb("neutral_rows", [P, ROW])
        w_ext = {k: sb(f"w_ext{k}", [P, ROW]) for k in (1, 2, 3)}
        wn_sb = sb("wn_sb", [P, P])
        we_sb = sb("we_sb", [P, D_EDGE])
        wT = sb("wT", [P, 2, P])
        att_cols = sb("att_cols", [P, 8])
        att_mat = sb("att_mat", [P, 3, 2 * HEADS])
        wa_rep = sb("wa_rep", [P, P])
        we_row = sb("we_row", [P, D_EDGE])
        b2_row = sb("b2_row", [P, P])

        src_g = sb("src_g", [GROUPS, GROUP], I32)
        dst_g = sb("dst_g", [GROUPS, GROUP], I32)
        next_g = sb("next_g", [GROUPS, GROUP], I32)
        srcf_g = sb("srcf_g", [GROUPS, GROUP])
        dstf_g = sb("dstf_g", [GROUPS, GROUP])
        nextf_g = sb("nextf_g", [GROUPS, GROUP])
        start_g = sb("start_g", [GROUPS, GROUP])
        end_g = sb("end_g", [GROUPS, GROUP])
        lastf_g = sb("lastf_g", [GROUPS, GROUP])
        default_g = sb("default_g", [GROUPS, GROUP], I32)
        src_i = sb("src_i", [P, TILES], I32)
        dst_i = sb("dst_i", [P, TILES], I32)
        dst_f = sb("dst_f", [P, TILES])
        last_i = sb("last_i", [P, TILES], I32)
        pos_i = sb("pos_i", [P, TILES], I32)

        seam_ends = sb("seam_ends", [GROUPS, 8])
        sentinels = sb("sentinels", [1, 2])
        seam_cur = sb("seam_cur", [P, SEAMS])
        seam_prev = sb("seam_prev", [P, SEAMS])
        seam_reset = sb("seam_reset", [P, SEAMS])
        seam_once = sb("seam_once", [P, SEAMS])
        seam_row_cur = sb("seam_row_cur", [SEAM_CHUNK, SEAM_CHUNKS])
        seam_row_next = sb("seam_row_next", [SEAM_CHUNK, SEAM_CHUNKS])
        seam_node_i = sb("seam_node_i", [SEAM_CHUNK, SEAM_CHUNKS], I32)
        seam_last_i = sb("seam_last_i", [SEAM_CHUNK, SEAM_CHUNKS], I32)
        seam_to_f = sb("seam_to_f", [SEAM_CHUNK, SEAM_CHUNKS])
        seam_to_i = sb("seam_to_i", [SEAM_CHUNK, SEAM_CHUNKS], I32)
        seam_rows = sb("seam_rows", [SEAM_CHUNK, SEAM_CHUNKS, ROW])
        seam_wide = sb("seam_wide", [SEAM_CHUNK, SEAM_CHUNKS, 2, D])
        seam_new = sb("seam_new", [SEAM_CHUNK, SEAM_CHUNKS, ROW])
        seam_max = sb("seam_max", [P, SEAMS + 1])
        seam_exp = sb("seam_exp", [P, 2, SEAMS])
        seam_sumw = sb("seam_sumw", [P, SEAMS])
        seam_sumx = sb("seam_sumx", [P, SEAMS])
        seam_w = sb("seam_w", [P, SEAMS])
        seam_x = sb("seam_x", [P, SEAMS])

        src_stage = slots("src_stage", [P, 4], I32)
        dst_stage = slots("dst_stage", [P, 4], I32)
        src_rows = slots("src_rows", [P, 4, ROW])
        dst_logit = slots("dst_logit", [P, 4, HEADS])
        marks = slots("marks", [64, 2, P])
        dst_bc = slots("dst_bc", [P, 4, P])
        attr = slots("attr", [P, 4, D_EDGE])
        same = slots("same", [P, 4, P])
        msg = slots("msg", [P, 4, D + HEADS])
        part_rows = slots("part_rows", [P, 4, ROW])
        attr_prod = sb("attr_prod", [P, 4, D_EDGE])
        attr_dot = sb("attr_dot", [P, 4])
        logit_sum = sb("logit_sum", [P, 4, HEADS])
        logit_all = sb("logit_all", [P, 4, HEADS])
        logit = sb("logit", [P, 4, HEADS])
        run_fwd = sb("run_fwd", [64, P])
        run_max = sb("run_max", [64, P])
        shifted = sb("shifted", [P, 4, HEADS])

        node_idx = sb("node_idx", [P, GROUPS, 4], I32)
        node_stage = slots("node_stage", [P, 4], I32, n=4)
        last_stage = slots("last_stage", [P, 4], I32, n=4)
        pos_stage = slots("pos_stage", [P, 4], I32, n=4)
        xin = slots("xin", [P, 4, D], n=4)
        self_rows = slots("self_rows", [P, 4, ROW], n=4)
        edge_part = slots("edge_part", [P, 4, ROW], n=4)
        self_sum = sb("self_sum", [P, 4, HEADS])
        self_logit = sb("self_logit", [P, 4, HEADS])
        both_max = sb("both_max", [P, 4, HEADS])
        both_shift = sb("both_shift", [P, 4, 2, HEADS])
        both_w = sb("both_w", [P, 4, 2, HEADS])
        edge_w = sb("edge_w", [P, 4, HEADS])
        total_w = sb("total_w", [P, 4, HEADS])
        inv_w = sb("inv_w", [P, 4, HEADS])
        from_self = sb("from_self", [P, 4, D])
        merged = slots("merged", [P, 4, D])
        x1 = slots("x1", [P, 4, D])
        stats = sb("stats", [P, 4, 6])
        moments = slots("moments", [P, 4, 2])
        std = slots("std", [P, 4])
        var_eps = slots("var_eps", [P, 4])
        rstd = slots("rstd", [P, 4])
        neg_mean = slots("neg_mean", [P, 4])
        h = slots("h", [P, 4, D])
        hT = slots("hT", [P, GROUP])
        below = slots("below", [P, GROUP])
        exp_below = slots("exp_below", [P, GROUP])
        table_rows = slots("table_rows", [P, 4, ROW])
        out_rows = slots("out_rows", [P, 4, D])

        bank = [ctx.enter_context(nc.psum_tensor(f"bank{i}", [P, 512], F32)) for i in range(8)]
        ps_logitT, ps_maxT = bank[0], bank[1]
        from_edges = bank[0][:, :].rearrange("p (j c) -> p j c", j=4)
        norm_w = bank[1][:, 0:P].rearrange("p (j a h) -> p j a h", j=4, a=2)
        b2_psum = bank[1][:, P:P + D]
        ps_hT = [bank[2], bank[3]] * 2
        ps_rows = [[bank[4], bank[5]], [bank[6], bank[7]]] * 2

        def pair(b, width):
            return b[:, :].rearrange("p (j c) -> p j c", j=2)[:, :, 0:width]

        names = """consts b2_psum weights att_mat w_T w_T_sb w_ext_ps w_ext_sb idx_in idx_f idx_start idx_mark idx_last
            idx_T idx_out idx_spread seam_mask seam_const neutral_out seam_loaded seam_wide seam_T seam_maxed seam_a seam_b
            seam_exped seam_c seam_scans seam_back seam_new seam_out seam_idx seam_node seam_lastd
            staged gather_round logit_sum attr_prod attr_dot logit_all logit logitT fwd bwd maxT
            same row_max shifted prob msg agg agg_out
            node_idx node_staged last_staged scatter_round part_round self_sum self_logit both_max both_shift both_exp edge_w total_w
            inv_w zero_w norm_w from_edges from_self merged biased x1 stats stats_round moments var_eps std rstd_v rstd
            neg_mean h hT_ps hT below exp_below above elu proj table_rows out_row""".split()
        S = {n: sem("s_" + n) for n in names}
        slot_names = """marks dst_bc attr src_rows dst_logit part_out xin self_rows edge_part table_out
            x1_out out last_out""".split()
        SL = {n: [sem(f"s_{n}{i}") for i in range(STEPS)] for n in slot_names}

        def done(passes, k, r, s):
            return GROUPS * passes.index(k) + STEPS * r + s + 1

        def landed(passes, k, r, s, n=1):
            in_a_pass = len(range(s, GROUPS, STEPS))
            return 16 * n * (in_a_pass * passes.index(k) + r + 1)

        def wait_landed(eng, name, passes, k, r, s, n=1):
            eng.wait_ge(SL[name][s], landed(passes, k, r, s, n))

        def wait_slot(eng, name, passes, k, r, s, back, n=1):
            r2, s2 = r + (s - back) // STEPS, (s - back) % STEPS
            if not isinstance(r2, int) or r2 >= 0:
                eng.wait_ge(SL[name][s2], landed(passes, k, r2, s2, n))

        def wait_pass(eng, name, passes, k, n=1):
            for s in range(STEPS):
                eng.wait_ge(SL[name][s], 16 * n * len(range(s, GROUPS, STEPS)) * (passes.index(k) + 1))

        def after(eng, s, count):
            if not isinstance(count, int) or count > 0:
                eng.wait_ge(s, count)

        def rounds(eng, *stages):
            def one(r):
                for s in range(STEPS):
                    for stage, lag in stages:
                        r2, s2 = r + (s - lag) // STEPS, (s - lag) % STEPS
                        if not isinstance(r2, int) or 0 <= STEPS * r2 + s2 < GROUPS:
                            stage(r2, s2)
            lags = -(-max(lag for _, lag in stages) // STEPS)
            for r in range(1 + lags):
                one(r)
            with eng.Fori(1 + lags, ROUNDS - 2) as r:
                one(r)
            for r in range(ROUNDS - 2, ROUNDS + lags):
                one(r)

        E = (1, 2, 3)
        def node_rows(t, r, s, rows=GROUP):
            g = STEPS * r + s
            return t[bass.ds(g * GROUP, rows), :].rearrange("(p j) c -> p j c", j=4)

        def edge_rows(t, r, s):
            g = STEPS * r + s
            return t[bass.ds(g * GROUP, GROUP), :].rearrange("(j p) c -> p j c", p=P)

        def more(r, s, ahead):
            return not isinstance(r, int) or STEPS * r + s + ahead < GROUPS

        def is_last(r, s):
            return isinstance(r, int) and STEPS * r + s == GROUPS - 1

        def spread(t, j=4):
            return t.unsqueeze(3).broadcast_to((P, j, HEADS, HEAD_DIM))

        def by_head(t):
            return t.rearrange("p j (h c) -> p j h c", h=HEADS)

        block = ctx.enter_context(nc.Block())

        N_WEIGHTS = 11
        @block.sync
        def _(sp):
            col = lambda a: a.rearrange("h c -> (h c)").unsqueeze(1)
            for dst_ap, src_ap in (
                (w_ext[1][:, 0:D], W1), (w_ext[2][:, 0:D], W2), (wn_sb[:, :], Wn), (we_sb[:, :], We),
                (att_cols[:, 0:1], col(a_src1)), (att_cols[:, 1:2], col(a_dst1)),
                (att_cols[:, 2:3], col(a_src2)), (att_cols[:, 3:4], col(a_dst2)),
                (att_cols[:, 7:8], b1.unsqueeze(1)),
                (b2_row[:, :], b2.unsqueeze(0).broadcast_to((P, D))),
            ):
                sp.dma_start(dst_ap, src_ap).then_inc(S["weights"], 16)
            sp.dma_start(att_cols[:, 4:7], Wa.rearrange("a (s o) -> o (a s)", o=D),
                         allow_slow_non_contiguous=True).then_inc(S["weights"], 16)

            sp.wait_ge(S["consts"], 1)
            full = (GROUPS - 1) * GROUP
            for t, a, shift in ((src_g, src, 0), (dst_g, dst, 0), (next_g, dst, 1)):
                sp.dma_start(t[0:GROUPS - 1, :], a[shift:full + shift].rearrange("(g e) -> g e", e=GROUP))\
                  .then_inc(S["idx_in"], 16)
                sp.dma_start(t[GROUPS - 1:GROUPS, 0:TAIL - shift], a[full + shift:N].unsqueeze(0))\
                  .then_inc(S["idx_in"], 16)
            sp.dma_start(last_edge.rearrange("(g e) a -> g (e a)", e=GROUP), default_g[:, :])\
              .then_inc(S["neutral_out"], 16)
            sp.dma_start(partial[PADDED:PADDED + P, :], neutral_rows[:, :]).then_inc(S["neutral_out"], 16)

            sp.wait_ge(S["idx_mark"], 4)
            sp.dma_start(dst_row.rearrange("(g e) -> g e", e=GROUP), dstf_g[:, :]).then_inc(S["idx_spread"], 16)
            for head in range(HEADS):
                for m, t in enumerate((start_g, end_g)):
                    sp.dma_start(run_marks[:, :, head, m, :], t[:, :].rearrange("g (j e) -> g j e", e=P))\
                      .then_inc(S["idx_spread"], 16)
            sp.dma_start(seam_dst[1:SEAMS + 1].rearrange("(g i) -> g i", i=8), seam_ends[:, :])\
              .then_inc(S["seam_idx"], 16)
            sp.dma_start(seam_dst[0:1].unsqueeze(0), sentinels[0:1, 0:1]).then_inc(S["seam_idx"], 16)
            sp.dma_start(seam_dst[SEAMS + 1:SEAMS + 2].unsqueeze(0), sentinels[0:1, 1:2]).then_inc(S["seam_idx"], 16)
            sp.wait_ge(S["seam_idx"], 48)
            sp.dma_start(seam_cur[:, :], seam_dst[1:SEAMS + 1].unsqueeze(0).broadcast_to((P, SEAMS)))\
              .then_inc(S["seam_const"], 16)
            sp.dma_start(seam_prev[:, :], seam_dst[0:SEAMS].unsqueeze(0).broadcast_to((P, SEAMS)))\
              .then_inc(S["seam_const"], 16)
            for t, first in ((seam_row_cur, 1), (seam_row_next, 2)):
                sp.dma_start(t[:, :], seam_dst[first:first + SEAMS].rearrange("(c p) -> p c", p=SEAM_CHUNK),
                             allow_slow_non_contiguous=True).then_inc(S["seam_const"], 16)

            def load_x(k):
                passes = (0, 2, 3)
                def load(r, s):
                    if isinstance(r, int) and r == 0:
                        after(sp, S["h"] if k == 2 else S["x1"], GROUPS if k > 0 else 0)
                    elif k == 0:
                        sp.wait_ge(S["h"], done((0, 2), 0, r, s) - 4)
                    elif k == 2:
                        sp.wait_ge(S["x1"], done((2,), 2, r, s) - 4)
                    else:
                        sp.wait_ge(S["out_row"], done((3,), 3, r, s) - 4)
                    if k == 3:
                        sp.dma_start(xin[s][:, :, :], node_rows(residual, r, s)).then_inc(SL["xin"][s], 16)
                    elif is_last(r, s):
                        sp.dma_start(xin[s][0:TAIL // 4, :, :], node_rows(x, r, s, TAIL)).then_inc(SL["xin"][s], 16)
                    else:
                        sp.dma_start(xin[s][:, :, :], node_rows(x, r, s)).then_inc(SL["xin"][s], 16)
                return load

            def load_node(k):
                def load(r, s):
                    after(sp, S["from_self"], done((1, 2), k, r, s) - 4)
                    sp.dma_start(self_rows[s][:, :, :], node_rows(table[k], r, s)).then_inc(SL["self_rows"][s], 16)
                return load

            def store_table(k):
                def store(r, s):
                    sp.wait_ge(S["table_rows"], done((0, 1, 2), k, r, s))
                    sp.dma_start(node_rows(table[k + 1], r, s), table_rows[s][:, :, :])\
                      .then_inc(SL["table_out"][s], 16)
                return store

            def store_x1(r, s):
                sp.wait_ge(S["x1"], done((2,), 2, r, s))
                sp.dma_start(node_rows(residual, r, s), x1[s][:, :, :]).then_inc(SL["x1_out"][s], 16)

            def store_out(r, s):
                sp.wait_ge(S["out_row"], done((3,), 3, r, s))
                if is_last(r, s):
                    sp.dma_start(node_rows(out, r, s, TAIL), out_rows[s][0:TAIL // 4, :, :]).then_inc(SL["out"][s], 16)
                else:
                    sp.dma_start(node_rows(out, r, s), out_rows[s][:, :, :]).then_inc(SL["out"][s], 16)

            def load_edge(k):
                def load(r, s):
                    g = STEPS * r + s
                    after(sp, S["bwd"], done(E, k, r, s) - 2)
                    sp.dma_start(marks[s][:, :, :],
                                 run_marks[bass.ds(g, 1), :, :, :, :].rearrange("g j h m e -> (g j h) m e"))\
                      .then_inc(SL["marks"][s], 16)
                    after(sp, S["same"], done(E, k, r, s) - 2)
                    sp.dma_start(dst_bc[s][:, :, :].rearrange("p j e -> p (j e)"),
                                 dst_row[bass.ds(g * GROUP, GROUP)].unsqueeze(0).broadcast_to((P, GROUP)))\
                      .then_inc(SL["dst_bc"][s], 16)
                    if k == 3:
                        after(sp, S["attr_prod"], done((3,), 3, r, s) - 2)
                        if is_last(r, s):
                            whole = TAIL // P
                            base = (GROUPS - 1) * GROUP
                            sp.dma_start(attr[s][:, 0:whole, :],
                                         edge_attr[base:base + whole * P, :].rearrange("(j p) c -> p j c", p=P))\
                              .then_inc(SL["attr"][s], 16)
                            sp.dma_start(attr[s][0:TAIL - whole * P, whole, :], edge_attr[base + whole * P:N, :])\
                              .then_inc(SL["attr"][s], 16)
                        else:
                            sp.dma_start(attr[s][:, :, :], edge_rows(edge_attr, r, s)).then_inc(SL["attr"][s], 16)
                return load

            def store_part(k):
                def store(r, s):
                    sp.wait_ge(S["agg_out"], done(E, k, r, s))
                    sp.wait_ge(S["row_max"], done(E, k, r, s))
                    sp.dma_start(edge_rows(partial, r, s), part_rows[s][:, :, :]).then_inc(SL["part_out"][s], 16)
                return store

            rounds(sp, (load_x(0), 0), (store_table(0), 3))
            wait_pass(sp, "last_out", (0,), 0, 4)
            sp.dma_start(node_idx[:, :, :], last_edge.rearrange("(g p j) a -> p g (j a)", g=GROUPS, p=P))\
              .then_inc(S["node_idx"], 16)
            for k in E:
                sp.wait_ge(S["idx_spread"], 16 * (1 + 2 * HEADS))
                rounds(sp, (load_edge(k), 0), (store_part(k), 1))
                wait_pass(sp, "part_out", E, k)
                if k > 1:
                    sp.wait_ge(S["seam_new"], k - 1)
                for end in range(2):
                    sp.dma_start(seam_rows[end:SEAM_CHUNK:2, :, :],
                                 partial[0:PADDED, :].rearrange("(c t p) w -> t c p w", p=P, c=SEAM_CHUNKS)[
                                     :, :, end * (P - 1), :]).then_inc(S["seam_loaded"], 16)
                if k < 3:
                    wait_pass(sp, "table_out", (0, 1, 2), k - 1)
                if k == 1:
                    rounds(sp, (load_node(1), 0), (store_table(1), 4))
                elif k == 2:
                    rounds(sp, (load_node(2), 0), (load_x(2), 0), (store_x1, 2), (store_table(2), 4))
                else:
                    wait_pass(sp, "x1_out", (2,), 2)
                    rounds(sp, (load_x(3), 0), (store_out, 1))
            wait_pass(sp, "out", (3,), 3)

        @block.gpsimd
        def _(pool):
            pool.memset(src_g[:, :], 0)
            pool.memset(dst_g[:, :], N)
            pool.memset(next_g[:, :], N)
            pool.memset(default_g[:, :], NEUTRAL)
            pool.memset(neutral_rows[:, 0:D + HEADS], 0.0)
            pool.memset(neutral_rows[:, MAXIMUM], LOW)
            pool.memset(sentinels[:, 0:1], -1.0)
            pool.memset(sentinels[:, 1:2], float(N))
            pool.memset(ones[:, :], 1.0)
            pool.memset(minus_half[:, :], -0.5)
            pool.memset(seam_max[:, 0:1], LOW)
            pool.iota(pos_i[:, :], pattern=[[P, TILES]], base=0, channel_multiplier=1)
            pool.memset(head_mask[:, :], 1.0)
            pool.memset(ident[:, :], 0.0).then_inc(S["consts"], 1)
            pool.wait_ge(S["consts"], 1)
            pool.affine_select(out=ident[:, :], in_=ident[:, :], compare_op=ALU.not_equal, fill=1.0,
                               base=0, pattern=[[-1, P]], channel_multiplier=1)
            pool.affine_select(out=head_mask[:, :], in_=head_mask[:, :], compare_op=ALU.is_ge, fill=0.0,
                               base=0, pattern=[[-HEAD_DIM, HEADS]], channel_multiplier=1).then_inc(S["consts"], 1)
            pool.wait_ge(S["consts"], 2)
            pool.affine_select(out=head_mask[:, :], in_=head_mask[:, :], compare_op=ALU.is_ge, fill=0.0,
                               base=HEAD_DIM - 1, pattern=[[HEAD_DIM, HEADS]], channel_multiplier=-1)\
                .then_inc(S["consts"], 1)
            node_limit = pool.to_reg(N - 1)
            row_limit = pool.to_reg(PADDED - 1)
            neutral_limit = pool.to_reg(NEUTRAL)
            part_limit = pool.to_reg(PADDED * ROW // HEADS - 1)

            def gather(to, frm, idx, limit, s):
                pool.indirect_dma_start(out=to, out_offset=None, in_=frm,
                                        in_offset=bass.IndirectOffsetOnAxis(ap=idx, axis=0),
                                        bounds_check=limit, oob_is_err=False).then_inc(s, 16)

            def scatter(to, frm, idx, limit, s):
                pool.indirect_dma_start(out=to, out_offset=bass.IndirectOffsetOnAxis(ap=idx, axis=0),
                                        in_=frm, in_offset=None,
                                        bounds_check=limit, oob_is_err=False).then_inc(s, 16)

            def rsqrt(r, s):
                pool.wait_ge(S["var_eps"], done((0, 2), 2, r, s))
                pool.wait_ge(S["neg_mean"], done((0, 2), 2, r, s) - 2)
                pool.wait_ge(S["h"], done((0, 2), 2, r, s) - 2)
                pool.tensor_tensor(rstd[s][:, :], var_eps[s][:, :], minus_half[:, :], ALU.pow).then_inc(S["rstd"], 1)

            def scatter_last(r, s):
                pool.wait_ge(S["last_staged"], done((0,), 0, r, s))
                pool.sem_inc(S["scatter_round"], 1)
                for j in range(4):
                    scatter(last_edge[:, :], pos_stage[s][:, j:j + 1], last_stage[s][:, j:j + 1], node_limit,
                            SL["last_out"][s])

            def gather_edge(k):
                def step(r, s):
                    pool.wait_ge(S["staged"], done(E, k, r, s))
                    pool.sem_inc(S["gather_round"], 1)
                    for j in range(4):
                        gather(src_rows[s][:, j, :], table[k], src_stage[s][:, j:j + 1], row_limit, SL["src_rows"][s])
                        gather(dst_logit[s][:, j, :], table[k].rearrange("n (a b) -> (n a) b", b=HEADS),
                               dst_stage[s][:, j:j + 1], part_limit, SL["dst_logit"][s])
                return step

            def gather_part(k):
                def step(r, s):
                    pool.wait_ge(S["node_staged"], done(E, k, r, s))
                    pool.sem_inc(S["part_round"], 1)
                    for j in range(4):
                        gather(edge_part[s][:, j, :], partial[0:NEUTRAL + 1, :], node_stage[s][:, j:j + 1],
                               neutral_limit, SL["edge_part"][s])
                return step

            pool.wait_ge(S["neutral_out"], 32)
            rounds(pool, (scatter_last, 0))
            wait_pass(pool, "last_out", (0,), 0, 4)
            pool.wait_ge(S["seam_node"], 1)
            for c in range(SEAM_CHUNKS):
                gather(seam_last_i[:, c:c + 1], last_edge[:, :], seam_node_i[:, c:c + 1], row_limit, S["seam_lastd"])
            for k in E:
                wait_pass(pool, "table_out", (0, 1, 2), k - 1)
                rounds(pool, (gather_edge(k), 0))
                pool.wait_ge(S["seam_new"], k)
                for c in range(SEAM_CHUNKS):
                    scatter(partial[0:PADDED, :], seam_new[:, c, :], seam_to_i[:, c:c + 1], row_limit, S["seam_out"])
                pool.wait_ge(S["seam_out"], 16 * SEAM_CHUNKS * k)
                if k == 2:
                    rounds(pool, (gather_part(k), 0), (rsqrt, 3))
                else:
                    rounds(pool, (gather_part(k), 0))

        @block.tensor
        def _(pe):
            pe.wait_ge(S["weights"], 16 * N_WEIGHTS)
            pe.wait_ge(S["consts"], 3)
            pe.transpose(bank[0][:, 0:P], w_ext[1][:, 0:D], ident[:, :])
            pe.transpose(bank[0][:, P:2 * P], w_ext[2][:, 0:D], ident[:, :])
            pe.transpose(bank[0][:, 2 * P:3 * P], wn_sb[:, :], ident[:, :]).then_inc(S["w_T"], 1)
            pe.wait_ge(S["w_T_sb"], 1)
            pe.wait_ge(S["att_mat"], 1)
            for i, lhs in enumerate((wT[:, 0, :], wT[:, 1, :], wn_sb[:, :])):
                pe.matmul(bank[1][:, 32 * i:32 * i + 32], lhs, att_mat[:, i, :], start=True, stop=True)
            pe.matmul(bank[1][:, 128:128 + D_EDGE], wa_rep[:, :], we_sb[:, :], start=True, stop=True)\
                .then_inc(S["w_ext_ps"], 1)
            for i, t in enumerate((srcf_g, dstf_g, lastf_g)):
                if i == 0:
                    pe.wait_ge(S["idx_f"], 1)
                if i == 2:
                    pe.wait_ge(S["idx_last"], 1)
                for j in range(4):
                    mm = pe.transpose(bank[4 + i][:, j * GROUPS:(j + 1) * GROUPS], t[:, j * P:(j + 1) * P],
                                      ident[0:GROUPS, 0:GROUPS])
                mm.then_inc(S["idx_T"], 1)
            pe.wait_ge(S["idx_out"], 3)

            def transpose_h(k):
                def step(r, s):
                    pe.wait_ge(S["h"] if k != 1 else S["merged"], done((0, 2) if k != 1 else (1, 2), k, r, s))
                    n = done((0, 1, 2), k, r, s) - 2
                    free(k, r, s)
                    rows = merged[s] if k == 1 else h[s]
                    for j in range(4):
                        mm = pe.transpose(ps_hT[s][:, j * P:(j + 1) * P], rows[:, j, :], ident[:, :])
                    mm.then_inc(S["hT_ps"], 1)
                return step

            def free(k, r, s):
                first = isinstance(r, int) and r == 0 and s < 2
                if k == 0:
                    after(pe, S["hT"], done((0, 2), 0, r, s) - 2)
                elif k == 1 and first:
                    pe.wait_ge(S["hT"], GROUPS)
                elif k == 1:
                    pe.wait_ge(S["elu"], done((1,), 1, r, s) - 2)
                elif first:
                    pe.wait_ge(S["elu"], GROUPS)
                else:
                    pe.wait_ge(S["hT"], done((0, 2), 2, r, s) - 2)

            def project(k):
                def step(r, s):
                    pe.wait_ge(S["hT"] if k != 1 else S["elu"], done((0, 2) if k != 1 else (1,), k, r, s))
                    after(pe, S["table_rows"], done((0, 1, 2), k, r, s) - 2)
                    for j in range(4):
                        o = (j % 2) * 256
                        mm = pe.matmul(ps_rows[s][j // 2][:, o:o + ROW], hT[s][:, j * P:(j + 1) * P],
                                       w_ext[k + 1][:, :], start=True, stop=True)
                    mm.then_inc(S["proj"], 1)
                return step

            def edge(k):
                def step(r, s):
                    pe.wait_ge(S["logit"], done(E, k, r, s))
                    after(pe, S["fwd"], done(E, k, r, s) - 1)
                    pe.matmul(ps_logitT[0:64, 0:P], logit[:, :, :].rearrange("p j h -> p (j h)"), ident[:, :],
                              start=True, stop=True).then_inc(S["logitT"], 1)
                    pe.wait_ge(S["bwd"], done(E, k, r, s))
                    after(pe, S["shifted"], done(E, k, r, s) - 1)
                    after(pe, S["row_max"], done(E, k, r, s) - 1)
                    pe.matmul(ps_maxT[:, 0:64], run_max[:, :], ident[0:64, 0:64], start=True, stop=True)\
                        .then_inc(S["maxT"], 1)
                    pe.wait_ge(S["msg"], done(E, k, r, s))
                    pe.wait_ge(S["same"], done(E, k, r, s))
                    after(pe, S["agg_out"], done(E, k, r, s) - 2)
                    for j in range(4):
                        o = (j % 2) * 256
                        mm = pe.matmul(ps_rows[s][j // 2][:, o:o + D + HEADS], same[s][:, j, :], msg[s][:, j, :],
                                       start=True, stop=True)
                    mm.then_inc(S["agg"], 1)
                return step

            def seam(k):
                pe.wait_ge(S["agg_out"], GROUPS * k)
                pe.wait_ge(S["shifted"], GROUPS * k)
                pe.wait_ge(S["row_max"], GROUPS * k)
                pe.wait_ge(S["seam_loaded"], 32 * k)
                pe.wait_ge(S["seam_wide"], 2 * k)
                for half, (c0, c1) in enumerate(HALVES):
                    for c in range(c0, c1):
                        o = (c - c0) * SEAM_CHUNK
                        rows = seam_rows[:, c, :]
                        pe.transpose(bank[half][:, o:o + SEAM_CHUNK], rows[:, 0:D], ident[0:SEAM_CHUNK, 0:SEAM_CHUNK])
                        for i, b in enumerate((2, 4)):
                            mm = pe.transpose(bank[b + half][:, o:o + SEAM_CHUNK], seam_wide[:, c, i, :],
                                              ident[0:SEAM_CHUNK, 0:SEAM_CHUNK])
                mm.then_inc(S["seam_T"], 1)
                pe.wait_ge(S["seam_scans"], 2 * k)
                for b, t in ((0, seam_sumx[:, :]), (2, seam_sumw[:, :]), (4, seam_max[:, 1:SEAMS + 1])):
                    for c in range(SEAM_CHUNKS):
                        mm = pe.transpose(bank[b + c // 4][0:SEAM_CHUNK, (c % 4) * P:(c % 4 + 1) * P],
                                          t[:, c * SEAM_CHUNK:(c + 1) * SEAM_CHUNK], ident[:, :])
                mm.then_inc(S["seam_back"], 1)

            rounds(pe, (transpose_h(0), 0), (project(0), 0))
            for k in E:
                if k > 1:
                    pe.wait_ge(S["table_rows"], GROUPS * k)
                if k == 1:
                    pe.wait_ge(S["table_rows"], GROUPS)
                rounds(pe, (edge(k), 0))
                seam(k)
                pe.wait_ge(S["seam_new"], k)
                if k < 3:
                    rounds(pe, (transpose_h(k), 0), (project(k), 1 if k == 1 else 0))

        @block.scalar
        def _(act):
            def relu_rows(k):
                def step(r, s):
                    act.wait_ge(S["neg_mean"], done((0, 2), k, r, s))
                    n = done((0, 1, 2), k, r, s) - 2
                    if k == 0:
                        wait_landed(act, "xin", (0, 2, 3), 0, r, s)
                        after(act, S["hT_ps"], n)
                    else:
                        act.wait_ge(S["hT_ps"], n)
                    rows = xin[s] if k == 0 else x1[s]
                    for j in range(4):
                        ins = act.activation(h[s][:, j, :], rows[:, j, :], ACT.Relu, bias=neg_mean[s][:, j:j + 1],
                                             scale=rstd[s][:, j:j + 1])
                    ins.then_inc(S["h"], 1)
                return step

            def copy_hT(k):
                def step(r, s):
                    act.wait_ge(S["hT_ps"], done((0, 1, 2), k, r, s))
                    after(act, S["proj"], done((0, 1, 2), k, r, s) - 2)
                    act.activation(hT[s][:, :], ps_hT[s][:, :], ACT.Copy).then_inc(S["hT"], 1)
                return step

            def elu_parts(r, s):
                act.wait_ge(S["below"], done((1,), 1, r, s))
                after(act, S["elu"], done((1,), 1, r, s) - 2)
                act.activation(ps_hT[s][:, :], ps_hT[s][:, :], ACT.Relu, bias=att_cols[:, 7:8])\
                    .then_inc(S["above"], 1)
                act.activation(exp_below[s][:, :], below[s][:, :], ACT.Exp).then_inc(S["exp_below"], 1)

            def evac(k):
                def step(r, s):
                    act.wait_ge(S["proj"], done((0, 1, 2), k, r, s))
                    wait_slot(act, "table_out", (0, 1, 2), k, r, s, 2)
                    act.activation(table_rows[s][:, 0:2, :], pair(ps_rows[s][0], ROW), ACT.Copy)
                    act.activation(table_rows[s][:, 2:4, :], pair(ps_rows[s][1], ROW), ACT.Copy)\
                        .then_inc(S["table_rows"], 1)
                return step

            def merge_exp(k):
                def step(r, s):
                    act.wait_ge(S["both_shift"], done((1, 2), k, r, s))
                    after(act, S["norm_w"], done((1, 2), k, r, s) - 1)
                    act.activation(both_w[:, :, :, :], both_shift[:, :, :, :], ACT.Exp).then_inc(S["both_exp"], 1)
                return step

            def edge(k):
                def step(r, s):
                    act.wait_ge(S["shifted"], done(E, k, r, s))
                    after(act, S["agg"], done(E, k, r, s) - 2)
                    act.activation(msg[s][:, :, D:D + HEADS], shifted[:, :, :], ACT.Exp).then_inc(S["prob"], 1)
                    act.wait_ge(S["agg"], done(E, k, r, s))
                    wait_slot(act, "part_out", E, k, r, s, 2)
                    act.activation(part_rows[s][:, 0:2, 0:D + HEADS], pair(ps_rows[s][0], D + HEADS), ACT.Copy)
                    act.activation(part_rows[s][:, 2:4, 0:D + HEADS], pair(ps_rows[s][1], D + HEADS), ACT.Copy)\
                        .then_inc(S["agg_out"], 1)
                return step

            def root(r, s):
                act.wait_ge(S["var_eps"], done((0, 2), 0, r, s))
                act.activation(std[s][:, :], var_eps[s][:, :], ACT.Sqrt).then_inc(S["std"], 1)

            rounds(act, (root, 0), (relu_rows(0), 1), (copy_hT(0), 1), (evac(0), 2))
            for k in E:
                rounds(act, (edge(k), 0))
                act.wait_ge(S["seam_b"], 2 * k)
                act.activation(seam_exp[:, :, :], seam_exp[:, :, :], ACT.Exp).then_inc(S["seam_exped"], 1)
                if k == 1:
                    rounds(act, (elu_parts, 2), (merge_exp(1), 0), (evac(1), 3))
                if k == 2:
                    rounds(act, (merge_exp(2), 0), (relu_rows(2), 2), (copy_hT(2), 2), (evac(2), 3))

        @block.vector
        def _(dve):
            dve.wait_ge(S["weights"], 16 * N_WEIGHTS)
            dve.wait_ge(S["consts"], 3)
            for i in range(2):
                for j in range(2):
                    c = 2 * i + j
                    dve.tensor_scalar(att_mat[:, i, HEADS * j:HEADS * j + HEADS], head_mask[:, :],
                                      att_cols[:, c:c + 1], None, ALU.mult)
            for j in range(2):
                dve.tensor_scalar(att_mat[:, 2, HEADS * j:HEADS * j + HEADS], ones[:, 0:HEADS],
                                  att_cols[:, 4 + j:5 + j], None, ALU.mult)
            dve.tensor_scalar(wa_rep[:, :], ones[:, :], att_cols[:, 6:7], None, ALU.mult).then_inc(S["att_mat"], 1)
            dve.wait_ge(S["w_T"], 1)
            dve.tensor_copy(w_ext[3][:, 0:D], bank[0][:, 2 * P:3 * P])
            dve.tensor_copy(wT[:, :, :], bank[0][:, 0:2 * P].rearrange("p (a b) -> p a b", a=2))\
                .then_inc(S["w_T_sb"], 1)
            dve.wait_ge(S["w_ext_ps"], 1)
            for i in range(3):
                dve.tensor_copy(w_ext[i + 1][:, D:ROW], bank[1][:, 32 * i:32 * i + 32])
            dve.tensor_copy(we_row[:, :], bank[1][:, 128:128 + D_EDGE]).then_inc(S["w_ext_sb"], 1)

            dve.wait_ge(S["idx_in"], 96)
            dve.tensor_copy(srcf_g[:, :], src_g[:, :])
            dve.tensor_copy(dstf_g[:, :], dst_g[:, :])
            dve.tensor_copy(nextf_g[:, :], next_g[:, :]).then_inc(S["idx_f"], 1)
            dve.wait_ge(S["idx_f"], 1)
            dve.tensor_tensor(end_g[:, :], dstf_g[:, :], nextf_g[:, :], ALU.not_equal)
            dve.memset(start_g[:, 0:1], 1.0)
            dve.tensor_tensor(start_g[:, 1:GROUP], dstf_g[:, 1:GROUP], dstf_g[:, 0:GROUP - 1], ALU.not_equal)\
                .then_inc(S["idx_start"], 1)
            dve.wait_ge(S["idx_start"], 1)
            dve.tensor_scalar(lastf_g[:, :], end_g[:, :], -float(SKIP), float(SKIP), ALU.mult, ALU.add)\
                .then_inc(S["idx_start"], 1)
            dve.wait_ge(S["idx_start"], 2)
            dve.tensor_tensor(lastf_g[:, :], lastf_g[:, :], dstf_g[:, :], ALU.add).then_inc(S["idx_last"], 1)
            dve.tensor_scalar(end_g[:, :], end_g[:, :], LOW, None, ALU.mult).then_inc(S["idx_mark"], 1)
            dve.tensor_scalar(start_g[:, :], start_g[:, :], LOW, None, ALU.mult).then_inc(S["idx_mark"], 1)
            ends = dstf_g[:, :].rearrange("g (j e) -> g j e", e=P)[:, :, 0:P:P - 1]
            dve.tensor_copy(seam_ends[:, :].rearrange("g (j i) -> g j i", i=2), ends).then_inc(S["idx_mark"], 2)
            tile_major = lambda t: t[:, :].rearrange("p (g j) -> p j g", j=4)
            by_tile = lambda b: b[:, 0:TILES].rearrange("p (j g) -> p j g", j=4)
            dve.wait_ge(S["idx_T"], 1)
            dve.tensor_copy(tile_major(src_i), by_tile(bank[4])).then_inc(S["idx_out"], 1)
            dve.wait_ge(S["idx_T"], 2)
            dve.tensor_copy(tile_major(dst_f), by_tile(bank[5]))
            width = ROW // HEADS
            dve.tensor_scalar(tile_major(dst_i), by_tile(bank[5]), float(width), float(width - 1), ALU.mult, ALU.add)\
                .then_inc(S["idx_out"], 1)
            dve.wait_ge(S["idx_T"], 3)
            dve.tensor_copy(tile_major(last_i), by_tile(bank[6])).then_inc(S["idx_out"], 1)
            dve.wait_ge(S["seam_const"], 64)
            dve.tensor_tensor(seam_cur[:, :], seam_cur[:, :], seam_prev[:, :], ALU.is_equal).then_inc(S["seam_mask"], 1)
            dve.tensor_copy(seam_node_i[:, :], seam_row_cur[:, :]).then_inc(S["seam_node"], 1)
            dve.tensor_tensor(seam_to_f[:, :], seam_row_cur[:, :], seam_row_next[:, :], ALU.is_equal)
            dve.memset(seam_once[:, :], 1.0).then_inc(S["seam_mask"], 1)
            dve.wait_ge(S["seam_mask"], 2)
            dve.tensor_scalar(seam_reset[:, :], seam_cur[:, :], -LOW, LOW, ALU.mult, ALU.add)
            dve.tensor_scalar(seam_once[:, 1:SEAMS:2], seam_cur[:, 1:SEAMS:2], -1.0, 1.0, ALU.mult, ALU.add)\
                .then_inc(S["seam_mask"], 1)
            dve.wait_ge(S["seam_mask"], 3)
            dve.wait_ge(S["idx_out"], 3)
            dve.wait_ge(S["w_ext_sb"], 1)

            def stage_last(r, s):
                g = STEPS * r + s
                wait_slot(dve, "last_out", (0,), 0, r, s, 4, 4)
                dve.tensor_scalar(last_stage[s][:, :], last_i[:, bass.ds(g * 4, 4)], 0.0, None, ALU.add)
                dve.tensor_scalar(pos_stage[s][:, :], pos_i[:, bass.ds(g * 4, 4)], 0.0, None, ALU.add)\
                    .then_inc(S["last_staged"], 1)

            def norm_stats(k):
                L = (0, 2)
                def step(r, s):
                    if k == 0:
                        wait_landed(dve, "xin", (0, 2, 3), 0, r, s)
                    else:
                        dve.wait_ge(S["x1"], done((2,), 2, r, s))
                    rows = xin[s] if k == 0 else x1[s]
                    for j in range(4):
                        ins = dve.bn_stats(stats[:, j, :], rows[:, j, :])
                    ins.then_inc(S["stats"], 1)
                    dve.wait_ge(S["stats"], done(L, k, r, s))
                    dve.sem_inc(S["stats_round"], 1)
                    for j in range(4):
                        ins = dve.bn_aggr(moments[s][:, j, :], stats[:, j, :])
                    ins.then_inc(S["moments"], 1)
                    dve.wait_ge(S["moments"], done(L, k, r, s))
                    dve.tensor_scalar(var_eps[s][:, :], moments[s][:, :, 1], EPS, None, ALU.add).then_inc(S["var_eps"], 1)
                return step

            def norm_shift(k):
                L = (0, 2)
                def step(r, s):
                    if k == 0:
                        dve.wait_ge(S["std"], done((0,), 0, r, s))
                        dve.reciprocal(rstd[s][:, :], std[s][:, :]).then_inc(S["rstd_v"], 1)
                        dve.wait_ge(S["rstd_v"], done((0,), 0, r, s))
                    else:
                        dve.wait_ge(S["rstd"], done((2,), 2, r, s))
                    after(dve, S["h"], done(L, k, r, s) - 2)
                    dve.scalar_tensor_tensor(out=neg_mean[s][:, :], in0=moments[s][:, :, 0], scalar=-1.0,
                                             in1=rstd[s][:, :], op0=ALU.mult, op1=ALU.mult).then_inc(S["neg_mean"], 1)
                return step

            def stage_edge(k, r, s):
                g = STEPS * r + s
                dve.tensor_scalar(src_stage[s][:, :], src_i[:, bass.ds(g * 4, 4)], 0.0, None, ALU.add)
                dve.tensor_scalar(dst_stage[s][:, :], dst_i[:, bass.ds(g * 4, 4)], 0.0, None, ALU.add)\
                    .then_inc(S["staged"], 1)

            def stage_node(r, s):
                dve.tensor_scalar(node_stage[s][:, :], node_idx[:, bass.ds(STEPS * r + s, 1), :].rearrange("p g j -> p (g j)"),
                                  0.0, None, ALU.add).then_inc(S["node_staged"], 1)

            def edge(k):
                def step(r, s):
                    n = done(E, k, r, s)
                    if k == 3:
                        dve.wait_ge(SL["attr"][s], 16 * (r + 1) + (16 if is_last(r, s) else 0))
                        dve.tensor_tensor(attr_prod[:, :, :], attr[s][:, :, :],
                                          we_row[:, :].unsqueeze(1).broadcast_to((P, 4, D_EDGE)), ALU.mult)\
                            .then_inc(S["attr_prod"], 1)
                        dve.wait_ge(S["attr_prod"], done((3,), 3, r, s))
                        dve.tensor_reduce(attr_dot[:, :], attr_prod[:, :, :], AX.X, ALU.add).then_inc(S["attr_dot"], 1)
                    wait_landed(dve, "dst_bc", E, k, r, s)
                    after(dve, S["agg"], n - 2)
                    g = STEPS * r + s
                    dve.tensor_tensor(same[s][:, :, :], dst_bc[s][:, :, :],
                                      dst_f[:, bass.ds(g * 4, 4)].unsqueeze(2).broadcast_to((P, 4, P)), ALU.is_equal)\
                        .then_inc(S["same"], 1)
                    wait_landed(dve, "src_rows", E, k, r, s, 4)
                    wait_landed(dve, "dst_logit", E, k, r, s, 4)
                    dve.tensor_tensor(logit_sum[:, :, :], src_rows[s][:, :, LOGIT_SRC], dst_logit[s][:, :, :], ALU.add)\
                        .then_inc(S["logit_sum"], 1)
                    dve.wait_ge(S["logit_sum"], n)
                    summed = logit_sum
                    if k == 3:
                        dve.wait_ge(S["attr_dot"], done((3,), 3, r, s))
                        dve.tensor_tensor(logit_all[:, :, :], logit_sum[:, :, :],
                                          attr_dot[:, :].unsqueeze(2).broadcast_to((P, 4, HEADS)), ALU.add)\
                            .then_inc(S["logit_all"], 1)
                        dve.wait_ge(S["logit_all"], done((3,), 3, r, s))
                        summed = logit_all
                    dve.scalar_tensor_tensor(out=logit[:, :, :], in0=summed[:, :, :], scalar=NEG_SLOPE,
                                             in1=summed[:, :, :], op0=ALU.mult, op1=ALU.max).then_inc(S["logit"], 1)
                    dve.wait_ge(S["logitT"], n)
                    wait_landed(dve, "marks", E, k, r, s)
                    dve.tensor_tensor_scan(run_fwd[:, :], marks[s][:, 0, :], ps_logitT[0:64, 0:P], LOW,
                                           ALU.add, ALU.max).then_inc(S["fwd"], 1)
                    dve.wait_ge(S["fwd"], n)
                    dve.tensor_tensor_scan(run_max[:, ::-1], marks[s][:, 1, ::-1], run_fwd[:, ::-1], LOW,
                                           ALU.add, ALU.max).then_inc(S["bwd"], 1)
                    dve.wait_ge(S["maxT"], n)
                    maxima = ps_maxT[:, 0:64].rearrange("p (j h) -> p j h", h=HEADS)
                    dve.tensor_tensor(shifted[:, :, :], logit[:, :, :], maxima, ALU.subtract).then_inc(S["shifted"], 1)
                    wait_slot(dve, "part_out", E, k, r, s, 2)
                    dve.tensor_copy(part_rows[s][:, :, MAXIMUM], maxima).then_inc(S["row_max"], 1)
                    dve.wait_ge(S["prob"], n)
                    dve.tensor_tensor(by_head(msg[s][:, :, 0:D]), by_head(src_rows[s][:, :, 0:D]),
                                      spread(msg[s][:, :, D:D + HEADS]), ALU.mult).then_inc(S["msg"], 1)
                    dve.wait_ge(S["msg"], n)
                    if more(r, s, 2):
                        stage_edge(k, r + (s + 2) // STEPS, (s + 2) % STEPS)
                return step

            def seam(k):
                if k == 1:
                    dve.wait_ge(S["seam_lastd"], 16 * SEAM_CHUNKS)
                    dve.scalar_tensor_tensor(out=seam_to_i[:, :], in0=seam_to_f[:, :], scalar=float(SKIP),
                                             in1=seam_last_i[:, :], op0=ALU.mult, op1=ALU.add)
                dve.wait_ge(S["seam_loaded"], 32 * k)
                for i, part in enumerate((WEIGHT, MAXIMUM)):
                    dve.tensor_copy(seam_wide[:, :, i, :].rearrange("p c (h d) -> p c h d", h=HEADS),
                                    seam_rows[:, :, part].unsqueeze(3).broadcast_to(
                                        (SEAM_CHUNK, SEAM_CHUNKS, HEADS, HEAD_DIM))).then_inc(S["seam_wide"], 1)
                dve.wait_ge(S["seam_T"], k)
                cols = [(c0 * SEAM_CHUNK, c1 * SEAM_CHUNK) for c0, c1 in HALVES]
                for half, (a, b) in enumerate(cols):
                    if half:
                        dve.wait_ge(S["seam_maxed"], 2 * k - 1)
                    dve.tensor_tensor_scan(seam_max[:, 1 + a:1 + b], seam_reset[:, a:b], bank[4 + half][:, 0:b - a],
                                           seam_max[:, a:a + 1], ALU.add, ALU.max).then_inc(S["seam_maxed"], 1)
                dve.wait_ge(S["seam_maxed"], 2 * k)
                dve.tensor_tensor(seam_w[:, :], seam_max[:, 0:SEAMS], seam_reset[:, :], ALU.add).then_inc(S["seam_a"], 1)
                dve.wait_ge(S["seam_a"], k)
                dve.tensor_tensor(seam_exp[:, 0, :], seam_w[:, :], seam_max[:, 1:SEAMS + 1], ALU.subtract)\
                    .then_inc(S["seam_b"], 1)
                for half, (a, b) in enumerate(cols):
                    ins = dve.tensor_tensor(seam_exp[:, 1, a:b], bank[4 + half][:, 0:b - a], seam_max[:, 1 + a:1 + b],
                                            ALU.subtract)
                ins.then_inc(S["seam_b"], 1)
                dve.wait_ge(S["seam_exped"], k)
                dve.tensor_tensor(seam_x[:, :], seam_exp[:, 1, :], seam_once[:, :], ALU.mult).then_inc(S["seam_c"], 1)
                dve.wait_ge(S["seam_c"], 3 * k - 2)
                for half, (a, b) in enumerate(cols):
                    ins = dve.tensor_tensor(seam_w[:, a:b], seam_x[:, a:b], bank[2 + half][:, 0:b - a], ALU.mult)
                ins.then_inc(S["seam_c"], 1)
                dve.wait_ge(S["seam_c"], 3 * k - 1)
                for half, (a, b) in enumerate(cols):
                    ins = dve.tensor_tensor(seam_x[:, a:b], seam_x[:, a:b], bank[half][:, 0:b - a], ALU.mult)
                ins.then_inc(S["seam_c"], 1)
                dve.tensor_tensor_scan(seam_sumw[:, :], seam_exp[:, 0, :], seam_w[:, :], 0.0, ALU.mult, ALU.add)\
                    .then_inc(S["seam_scans"], 1)
                dve.wait_ge(S["seam_c"], 3 * k)
                dve.tensor_tensor_scan(seam_sumx[:, :], seam_exp[:, 0, :], seam_x[:, :], 0.0, ALU.mult, ALU.add)\
                    .then_inc(S["seam_scans"], 1)
                dve.wait_ge(S["seam_back"], k)
                if k > 1:
                    dve.wait_ge(S["seam_out"], 16 * SEAM_CHUNKS * (k - 1))
                for half in range(2):
                    c0, c1 = 4 * half, min(4 * half + 4, SEAM_CHUNKS)
                    for b, part, step in ((0, slice(0, D), 1), (2, WEIGHT, HEAD_DIM), (4, MAXIMUM, HEAD_DIM)):
                        got = bank[b + half][0:SEAM_CHUNK, 0:(c1 - c0) * P].rearrange("p (c f) -> p c f", f=P)
                        ins = dve.tensor_copy(seam_new[:, c0:c1, part], got[:, :, 0:P:step])
                ins.then_inc(S["seam_new"], 1)

            M = (1, 2)

            def self_sum_of(k):
                def step(r, s):
                    wait_landed(dve, "self_rows", M, k, r, s)
                    dve.tensor_tensor(self_sum[:, :, :], self_rows[s][:, :, LOGIT_SRC], self_rows[s][:, :, LOGIT_DST],
                                      ALU.add).then_inc(S["self_sum"], 1)
                return step

            def self_logit_of(k):
                def step(r, s):
                    dve.wait_ge(S["self_sum"], done(M, k, r, s))
                    dve.scalar_tensor_tensor(out=self_logit[:, :, :], in0=self_sum[:, :, :], scalar=NEG_SLOPE,
                                             in1=self_sum[:, :, :], op0=ALU.mult, op1=ALU.max)\
                        .then_inc(S["self_logit"], 1)
                return step

            def max_of(k):
                def step(r, s):
                    dve.wait_ge(S["self_logit"], done(M, k, r, s))
                    wait_landed(dve, "edge_part", E, k, r, s, 4)
                    dve.tensor_tensor(both_max[:, :, :], self_logit[:, :, :], edge_part[s][:, :, MAXIMUM], ALU.max)\
                        .then_inc(S["both_max"], 1)
                return step

            def shift_of(k):
                def step(r, s):
                    dve.wait_ge(S["both_max"], done(M, k, r, s))
                    dve.tensor_tensor(both_shift[:, :, 0, :], edge_part[s][:, :, MAXIMUM], both_max[:, :, :], ALU.subtract)
                    dve.tensor_tensor(both_shift[:, :, 1, :], self_logit[:, :, :], both_max[:, :, :], ALU.subtract)\
                        .then_inc(S["both_shift"], 1)
                return step

            def edge_weight(k):
                def step(r, s):
                    dve.wait_ge(S["both_exp"], done(M, k, r, s))
                    dve.tensor_tensor(edge_w[:, :, :], edge_part[s][:, :, WEIGHT], both_w[:, :, 0, :], ALU.mult)\
                        .then_inc(S["edge_w"], 1)
                return step

            def total_weight(k):
                def step(r, s):
                    dve.wait_ge(S["edge_w"], done(M, k, r, s))
                    dve.scalar_tensor_tensor(out=total_w[:, :, :], in0=edge_w[:, :, :], scalar=1e-16,
                                             in1=both_w[:, :, 1, :], op0=ALU.add, op1=ALU.add).then_inc(S["total_w"], 1)
                return step

            def invert(k):
                def step(r, s):
                    dve.wait_ge(S["total_w"], done(E, k, r, s))
                    dve.reciprocal(inv_w[:, :, :], total_w[:, :, :]).then_inc(S["inv_w"], 1)
                return step

            def normalise(k):
                def step(r, s):
                    dve.wait_ge(S["inv_w"], done(E, k, r, s))
                    after(dve, S["from_self"], done(M, k, r, s) - 1)
                    dve.tensor_tensor(norm_w, both_w[:, :, :, :],
                                      inv_w[:, :, :].unsqueeze(2).broadcast_to((P, 4, 2, HEADS)), ALU.mult)\
                        .then_inc(S["norm_w"], 1)
                return step

            def edges_share(k):
                def step(r, s):
                    dve.wait_ge(S["norm_w"], done(M, k, r, s))
                    if k == 1 or (isinstance(r, int) and r == s == 0):
                        after(dve, S["merged"], done(M, k, r, s) - 1)
                    else:
                        dve.wait_ge(S["x1"], done((2,), 2, r, s) - 1)
                    dve.tensor_tensor(by_head(from_edges), by_head(edge_part[s][:, :, 0:D]),
                                      spread(norm_w[:, :, 0, :]), ALU.mult).then_inc(S["from_edges"], 1)
                return step

            def self_share(k):
                def step(r, s):
                    dve.tensor_tensor(by_head(from_self[:, :, :]), by_head(self_rows[s][:, :, 0:D]),
                                      spread(norm_w[:, :, 1, :]), ALU.mult).then_inc(S["from_self"], 1)
                    dve.wait_ge(S["from_edges"], done(E, k, r, s))
                    if more(r, s, 4):
                        stage_node(r + 1, s)
                return step

            def merge(k):
                def step(r, s):
                    dve.wait_ge(S["from_self"], done(M, k, r, s))
                    after(dve, S["hT_ps"], done((0, 1, 2), 1, r, s) - 2) if k == 1 else None
                    dve.tensor_tensor(merged[s][:, :, :], from_edges, from_self[:, :, :], ALU.add)\
                        .then_inc(S["merged"], 1)
                return step

            def add_bias(r, s):
                dve.wait_ge(S["merged"], done(M, 2, r, s))
                dve.tensor_tensor(from_edges, merged[s][:, :, :], b2_psum.unsqueeze(1).broadcast_to((P, 4, D)),
                                  ALU.add).then_inc(S["biased"], 1)

            def add_x(r, s):
                dve.wait_ge(S["biased"], done((2,), 2, r, s))
                wait_landed(dve, "xin", (0, 2, 3), 2, r, s)
                wait_slot(dve, "x1_out", (2,), 2, r, s, 2)
                after(dve, S["h"], done((0, 2), 2, r, s) - 2)
                dve.tensor_tensor(x1[s][:, :, :], from_edges, xin[s][:, :, :], ALU.add).then_inc(S["x1"], 1)

            def below_zero(r, s):
                dve.wait_ge(S["hT_ps"], done((0, 1, 2), 1, r, s))
                after(dve, S["exp_below"], done((1,), 1, r, s) - 2)
                dve.tensor_scalar(below[s][:, :], ps_hT[s][:, :], att_cols[:, 7:8], 0.0, ALU.add, ALU.min)\
                    .then_inc(S["below"], 1)

            def elu(r, s):
                dve.wait_ge(S["exp_below"], done((1,), 1, r, s))
                dve.wait_ge(S["above"], done((1,), 1, r, s))
                after(dve, S["proj"], done((0, 1, 2), 1, r, s) - 2)
                dve.scalar_tensor_tensor(out=hT[s][:, :], in0=exp_below[s][:, :], scalar=-1.0, in1=ps_hT[s][:, :],
                                         op0=ALU.add, op1=ALU.add).then_inc(S["elu"], 1)

            def finish(r, s):
                n = done(E, 3, r, s)
                wait_landed(dve, "edge_part", E, 3, r, s, 4)
                dve.tensor_scalar(edge_w[:, :, :], edge_part[s][:, :, WEIGHT], 0.0, None, ALU.is_equal)\
                    .then_inc(S["zero_w"], 1)
                dve.wait_ge(S["zero_w"], done((3,), 3, r, s))
                dve.tensor_tensor(total_w[:, :, :], edge_w[:, :, :], edge_part[s][:, :, WEIGHT], ALU.add)\
                    .then_inc(S["total_w"], 1)
                dve.wait_ge(S["total_w"], n)
                dve.reciprocal(inv_w[:, :, :], total_w[:, :, :]).then_inc(S["inv_w"], 1)
                dve.wait_ge(S["inv_w"], n)
                dve.tensor_tensor(by_head(from_edges), by_head(edge_part[s][:, :, 0:D]),
                                  spread(inv_w[:, :, :]), ALU.mult).then_inc(S["from_edges"], 1)
                dve.wait_ge(S["from_edges"], n)
                if more(r, s, 4):
                    stage_node(r + 1, s)
                wait_landed(dve, "xin", (0, 2, 3), 3, r, s)
                wait_slot(dve, "out", (3,), 3, r, s, 2)
                dve.tensor_tensor(out_rows[s][:, :, :], from_edges, xin[s][:, :, :], ALU.add)\
                    .then_inc(S["out_row"], 1)

            rounds(dve, (stage_last, 0), (norm_stats(0), 0), (norm_shift(0), 1))
            for k in E:
                for s in range(2):
                    stage_edge(k, 0, s)
                rounds(dve, (edge(k), 0))
                seam(k)
                if k == 1:
                    dve.wait_ge(S["node_idx"], 16)
                for s in range(STEPS):
                    stage_node(0, s)
                if k == 1:
                    rounds(dve, (self_sum_of(1), 0), (below_zero, 2), (self_logit_of(1), 0), (edges_share(1), 1),
                           (max_of(1), 0), (self_share(1), 1), (shift_of(1), 0), (merge(1), 1), (edge_weight(1), 0),
                           (elu, 2), (total_weight(1), 0), (invert(1), 0), (normalise(1), 0))
                elif k == 2:
                    dve.wait_ge(S["seam_new"], 2)
                    dve.tensor_copy(b2_psum, b2_row[:, :]).then_inc(S["b2_psum"], 1)
                    dve.wait_ge(S["b2_psum"], 1)
                    rounds(dve, (self_sum_of(2), 0), (edges_share(2), 1), (self_logit_of(2), 0), (self_share(2), 1),
                           (max_of(2), 0), (norm_shift(2), 2), (shift_of(2), 0), (merge(2), 1), (edge_weight(2), 0),
                           (add_bias, 1), (total_weight(2), 0), (add_x, 1), (invert(2), 0), (norm_stats(2), 1),
                           (normalise(2), 0))
                else:
                    rounds(dve, (finish, 0))


_INS = ['x', 'src', 'dst', 'edge_attr_64', 'L0_gnn_W1', 'L0_gnn_a_src1', 'L0_gnn_a_dst1', 'L0_gnn_b1', 'L0_gnn_W2',
        'L0_gnn_a_src2', 'L0_gnn_a_dst2', 'L0_gnn_b2', 'L1_gnn_Wn', 'L1_gnn_We', 'L1_gnn_Wa']


def kernel(**inputs):
    import numpy as _np
    import concourse.bacc as _bacc
    from concourse import mybir as _mybir
    from concourse.bass_utils import run_bass_kernel_spmd as _run

    nc = _bacc.Bacc("TRN2", target_bir_lowering=False, num_devices=1)
    arrays, args = {}, []
    for name in _INS:
        a = _np.ascontiguousarray(inputs[name])
        arrays[f"in_{name}"] = a
        args.append(nc.dram_tensor(f"in_{name}", a.shape, _mybir.dt.from_np(a.dtype), kind="ExternalInput").ap())
    args.append(nc.dram_tensor("out_0", (N, D), _mybir.dt.float32, kind="ExternalOutput").ap())
    build(nc, *args)
    r = _run(nc, [arrays], core_ids=[0])
    return r.results[0]["out_0"]
```

```python
from contextlib import ExitStack

import concourse.bass as bass
from concourse import mybir

F32 = mybir.dt.float32
I32 = mybir.dt.int32
BF16 = mybir.dt.bfloat16
ALU = mybir.AluOpType
ACT = mybir.ActivationFunctionType
AX = mybir.AxisListType

P = 128
N = 50000
TILES_PER_GROUP = 4
GROUP = TILES_PER_GROUP * P
GROUPS = -(-N // GROUP)
STEPS = 4
ROUNDS = -(-GROUPS // STEPS)
TILES = GROUPS * TILES_PER_GROUP
PADDED = GROUPS * GROUP
TAIL = N - (GROUPS - 1) * GROUP
HEADS, HEAD_DIM, D = 16, 8, 128
D_EDGE = 64
ROW = D + 2 * HEADS
LOGIT_SRC = slice(D, D + HEADS)
LOGIT_DST = slice(D + HEADS, ROW)
WEIGHT = slice(D, D + HEADS)
MAXIMUM = slice(D + HEADS, ROW)
SELF_LOGIT = slice(ROW, ROW + HEADS)
LOW = -1.0e30
NEG_SLOPE, EPS = 0.2, 1e-5
SKIP = 65536
NEUTRAL = PADDED
SEAM_CHUNK = 112
SEAM_CHUNKS = 2 * TILES // SEAM_CHUNK
SEAMS = 2 * TILES
WINDOW = 2
PARTS = 3
HALVES = ((0, 4), (4, SEAM_CHUNKS))


def build(nc, x, src, dst, edge_attr, W1, a_src1, a_dst1, b1, W2, a_src2, a_dst2, b2, Wn, We, Wa, out):
    ctx = ExitStack()
    with ctx:
        def sb(name, shape, dt=F32):
            return ctx.enter_context(nc.sbuf_tensor(name, shape, dt))

        def slots(name, shape, dt=F32, n=2):
            made = [sb(f"{name}{i}", shape, dt) for i in range(n)]
            return [made[i % n] for i in range(STEPS)]

        def sem(name):
            return ctx.enter_context(nc.semaphore(name))

        def dram(name, shape, dt=F32):
            return nc.dram_tensor(name, shape, dt, kind="Internal").ap()

        table = {k: dram(f"table{k}", [PADDED, ROW]) for k in (1, 2, 3)}
        dst_parts = {k: dram(f"dst_parts{k}", [PADDED + WINDOW * P, PARTS * HEADS], BF16) for k in (1, 2, 3)}
        partial = dram("partial", [PADDED + P, ROW])
        last_edge = dram("last_edge", [PADDED, 1], I32)
        residual = dram("residual", [PADDED, D])
        dst_row = dram("dst_row", [PADDED])
        rel_row = dram("rel_row", [PADDED], BF16)
        run_marks = dram("run_marks", [GROUPS, 4, HEADS, 2, P])
        seam_dst = dram("seam_dst", [SEAMS + 2])
        window_base = dram("window_base", [1, TILES], I32)
        windows_fit = dram("windows_fit", [1, 1], I32)

        ident = sb("ident", [P, P])
        ones = sb("ones", [P, P])
        head_mask = sb("head_mask", [P, HEADS])
        minus_half = sb("minus_half", [P, 8])
        neutral_rows = sb("neutral_rows", [P, ROW])
        w_ext = {k: sb(f"w_ext{k}", [P, ROW]) for k in (1, 2, 3)}
        wn_sb = sb("wn_sb", [P, P])
        we_sb = sb("we_sb", [P, D_EDGE])
        wT = sb("wT", [P, 2, P])
        att_cols = sb("att_cols", [P, 8])
        att_mat = sb("att_mat", [P, 3, 2 * HEADS])
        wa_rep = sb("wa_rep", [P, P])
        we_row = sb("we_row", [P, D_EDGE])
        b2_row = sb("b2_row", [P, P])

        src_g = sb("src_g", [GROUPS, GROUP], I32)
        dst_g = sb("dst_g", [GROUPS, GROUP], I32)
        next_g = sb("next_g", [GROUPS, GROUP], I32)
        srcf_g = sb("srcf_g", [GROUPS, GROUP])
        dstf_g = sb("dstf_g", [GROUPS, GROUP])
        nextf_g = sb("nextf_g", [GROUPS, GROUP])
        marks_g = sb("marks_g", [GROUPS, 4, 2, P])
        lastf_g = sb("lastf_g", [GROUPS, GROUP])
        default_g = sb("default_g", [GROUPS, GROUP], I32)
        src_i = sb("src_i", [P, TILES], I32)
        dst_i = sb("dst_i", [P, TILES], I32)
        dst_f = sb("dst_f", [P, TILES])
        last_i = sb("last_i", [P, TILES], I32)
        pos_i = sb("pos_i", [P, TILES], I32)

        seam_ends = sb("seam_ends", [GROUPS, 8])
        sentinels = sb("sentinels", [1, 2])
        seam_cur = sb("seam_cur", [P, SEAMS])
        seam_prev = sb("seam_prev", [P, SEAMS])
        seam_reset = sb("seam_reset", [P, SEAMS])
        seam_once = sb("seam_once", [P, SEAMS])
        seam_row_cur = sb("seam_row_cur", [SEAM_CHUNK, SEAM_CHUNKS])
        seam_row_next = sb("seam_row_next", [SEAM_CHUNK, SEAM_CHUNKS])
        seam_node_i = sb("seam_node_i", [SEAM_CHUNK, SEAM_CHUNKS], I32)
        seam_last_i = sb("seam_last_i", [SEAM_CHUNK, SEAM_CHUNKS], I32)
        seam_to_f = sb("seam_to_f", [SEAM_CHUNK, SEAM_CHUNKS])
        seam_to_i = sb("seam_to_i", [SEAM_CHUNK, SEAM_CHUNKS], I32)
        seam_rows = sb("seam_rows", [SEAM_CHUNK, SEAM_CHUNKS, ROW])
        seam_wide = sb("seam_wide", [SEAM_CHUNK, SEAM_CHUNKS, 2, D])
        seam_new = sb("seam_new", [SEAM_CHUNK, SEAM_CHUNKS, ROW])
        seam_max = sb("seam_max", [P, SEAMS + 1])
        seam_exp = sb("seam_exp", [P, 2, SEAMS])
        seam_sumw = sb("seam_sumw", [P, SEAMS])
        seam_sumx = sb("seam_sumx", [P, SEAMS])
        seam_w = sb("seam_w", [P, SEAMS])
        seam_x = sb("seam_x", [P, SEAMS])

        base_g = sb("base_g", [GROUPS, 4], I32)
        width_g = sb("width_g", [GROUPS, 4])
        widest_g = sb("widest_g", [GROUPS, 1])
        widest = sb("widest", [1, 1])
        fit = sb("fit", [1, 1], I32)
        base_bc = sb("base_bc", [P, TILES], I32)
        node_in_window = sb("node_in_window", [P, WINDOW], I32)
        window_node = sb("window_node", [P, WINDOW])
        no_parts = sb("no_parts", [P, WINDOW * PARTS * HEADS], BF16)
        rel_g = sb("rel_g", [GROUPS, GROUP], BF16)
        rel_f = sb("rel_f", [P, TILES])
        rel_bc = slots("rel_bc", [P, 2, 4, P], BF16)
        window_parts = slots("window_parts", [P, 4, WINDOW, PARTS * HEADS], BF16, n=4)
        one_hot = slots("one_hot", [P, WINDOW, 4, P], BF16)
        dst_sum = sb("dst_sum", [P, 4, HEADS])

        src_stage = slots("src_stage", [P, 4], I32, n=4)
        dst_stage = slots("dst_stage", [P, 4], I32, n=4)
        src_rows = slots("src_rows", [P, 4, ROW], n=4)
        dst_logit = slots("dst_logit", [P, 4, HEADS], n=4)
        marks = slots("marks", [64, 2, 2, P])
        dst_bc = slots("dst_bc", [P, 4, P])
        attr = slots("attr", [P, 4, D_EDGE])
        same = slots("same", [P, 4, P])
        msg = slots("msg", [P, 4, D + HEADS])
        part_rows = slots("part_rows", [P, 4, ROW], n=4)
        attr_prod = sb("attr_prod", [P, 4, D_EDGE])
        attr_dot = sb("attr_dot", [P, TILES])
        logit_sum = sb("logit_sum", [P, 4, HEADS])
        with_attr = sb("with_attr", [P, 4, HEADS])
        logit = sb("logit", [P, 4, HEADS])
        run_fwd = sb("run_fwd", [64, P])
        run_max = sb("run_max", [64, P])
        shifted = sb("shifted", [P, 4, HEADS])

        node_idx = sb("node_idx", [P, GROUPS, 4], I32)
        node_stage = slots("node_stage", [P, 4], I32, n=4)
        last_stage = slots("last_stage", [P, 4], I32, n=4)
        pos_stage = slots("pos_stage", [P, 4], I32, n=4)
        xin = slots("xin", [P, 4, D], n=4)
        self_rows = slots("self_rows", [P, 4, ROW], n=4)
        edge_part = slots("edge_part", [P, 4, ROW + HEADS], n=4)
        self_sum = sb("self_sum", [P, 4, HEADS])
        both_max = sb("both_max", [P, 4, HEADS])
        both_shift = sb("both_shift", [P, 4, 2, HEADS])
        both_w = sb("both_w", [P, 4, 2, HEADS])
        edge_w = sb("edge_w", [P, 4, HEADS])
        total_w = sb("total_w", [P, 4, HEADS])
        inv_w = sb("inv_w", [P, 4, HEADS])
        from_self = sb("from_self", [P, 4, D])
        merged = slots("merged", [P, 4, D])
        x1 = slots("x1", [P, 4, D], n=4)
        stats = sb("stats", [P, 4, 6])
        moments = slots("moments", [P, 4, 2], n=4)
        std = slots("std", [P, 4])
        var_pair = slots("var_pair", [P, 8])
        rstd_pair = slots("rstd_pair", [P, 8])
        var_eps = [var_pair[s // 2][:, 4 * (s % 2):4 * (s % 2) + 4] for s in range(STEPS)]
        rstd = [rstd_pair[s // 2][:, 4 * (s % 2):4 * (s % 2) + 4] for s in range(STEPS)]
        neg_mean = slots("neg_mean", [P, 4])
        h = slots("h", [P, 4, D])
        hT = slots("hT", [P, GROUP])
        below = [x1[2 + s % 2][:, :, :].rearrange("p j c -> p (j c)") for s in range(STEPS)]
        table_rows = slots("table_rows", [P, 4, ROW])
        out_rows = merged
        parts = slots("parts", [P, 4, PARTS, HEADS], BF16, n=4)
        rest = slots("rest", [P, 4, HEADS])

        bank = [ctx.enter_context(nc.psum_tensor(f"bank{i}", [P, 512], F32)) for i in range(8)]
        ps_logitT, ps_maxT = bank[0], bank[1]
        from_edges = bank[0][:, :].rearrange("p (j c) -> p j c", j=4)
        norm_w = bank[1][:, 0:P].rearrange("p (j a h) -> p j a h", j=4, a=2)
        ps_hT = [bank[2], bank[3]] * 2
        ps_window = [bank[2], bank[3]] * 2
        ps_rows = [[bank[4], bank[5]], [bank[6], bank[7]]] * 2

        def pair(b, width):
            return b[:, :].rearrange("p (j c) -> p j c", j=2)[:, :, 0:width]

        names = """window_base window_width window_T window_fit window_node window_rel one_hot window_sum dst_sum
            part_high part_rest part_mid part_low
            consts weights att_mat w_T w_T_sb w_ext_ps w_ext_sb idx_in idx_f idx_start idx_mark idx_last
            idx_T idx_out idx_spread seam_mask seam_const neutral_out seam_loaded seam_wide seam_T seam_maxed seam_a seam_b
            seam_exped seam_c seam_scans seam_back seam_new seam_out seam_idx seam_node seam_lastd
            staged logit_sum attr_prod attr_dot with_attr logit logitT fwd bwd maxT
            same row_max shifted prob msg agg agg_out
            node_idx node_staged last_staged self_sum self_logit both_max both_shift both_exp edge_w total_w
            inv_w zero_w norm_w from_edges from_self merged biased x1 stats round_begun moments var_eps std rstd_v rstd
            neg_mean h hT_ps hT below exp_below above elu proj table_rows out_row""".split()
        S = {n: sem("s_" + n) for n in names}
        slot_names = """dst_bc attr src_rows dst_logit part_out xin self_rows edge_part table_out
            x1_out out last_out parts_out""".split()
        SL = {n: [sem(f"s_{n}{i}") for i in range(STEPS)] for n in slot_names}
        SL.update({n: {i: sem(f"s_{n}{i}") for i in range(0, STEPS, 2)} for n in ("marks", "rel_bc")})

        E = (1, 2, 3)

        def done(passes, k, r, s):
            return GROUPS * passes.index(k) + STEPS * r + s + 1

        def landed(passes, k, r, s, n=1):
            in_a_pass = len(range(s, GROUPS, STEPS))
            return 16 * n * (in_a_pass * passes.index(k) + r + 1)

        def wait_landed(eng, name, passes, k, r, s, n=1):
            eng.wait_ge(SL[name][s], landed(passes, k, r, s, n))

        def wait_slot(eng, name, passes, k, r, s, back, n=1):
            r2, s2 = r + (s - back) // STEPS, (s - back) % STEPS
            if not isinstance(r2, int) or r2 >= 0:
                eng.wait_ge(SL[name][s2], landed(passes, k, r2, s2, n))

        def wait_pass(eng, name, passes, k, n=1):
            for s in range(STEPS):
                eng.wait_ge(SL[name][s], 16 * n * len(range(s, GROUPS, STEPS)) * (passes.index(k) + 1))

        def after(eng, s, count):
            if not isinstance(count, int) or count > 0:
                eng.wait_ge(s, count)

        def rounds(eng, *stages):
            def one(r):
                for s in range(STEPS):
                    for stage, lag in stages:
                        r2, s2 = r + (s - lag) // STEPS, (s - lag) % STEPS
                        if not isinstance(r2, int) or 0 <= STEPS * r2 + s2 < GROUPS:
                            stage(r2, s2)
            lags = -(-max(lag for _, lag in stages) // STEPS)
            for r in range(1 + lags):
                one(r)
            with eng.Fori(1 + lags, ROUNDS - 2) as r:
                one(r)
            for r in range(ROUNDS - 2, ROUNDS + lags):
                one(r)

        def either(eng, windowed, gathered):
            eng.wait_ge(S["window_fit"], 17)
            fits = eng.value_load(windows_fit[0:1, 0:1], min_val=0, max_val=1)
            with eng.If(fits == 1):
                rounds(eng, *windowed)
            with eng.Else():
                rounds(eng, *gathered)

        def node_rows(t, r, s, rows=GROUP):
            g = STEPS * r + s
            return t[bass.ds(g * GROUP, rows), :].rearrange("(p j) c -> p j c", j=4)

        def edge_rows(t, r, s):
            g = STEPS * r + s
            return t[bass.ds(g * GROUP, GROUP), :].rearrange("(j p) c -> p j c", p=P)

        def more(r, s, ahead):
            return not isinstance(r, int) or STEPS * r + s + ahead < GROUPS

        def is_last(r, s):
            return isinstance(r, int) and STEPS * r + s == GROUPS - 1

        def spread(t, j=4):
            return t.unsqueeze(3).broadcast_to((P, j, HEADS, HEAD_DIM))

        def by_head(t):
            return t.rearrange("p j (h c) -> p j h c", h=HEADS)

        block = ctx.enter_context(nc.Block())

        N_WEIGHTS = 11
        N_NEUTRAL = 5
        @block.sync
        def _(sp):
            col = lambda a: a.rearrange("h c -> (h c)").unsqueeze(1)
            for dst_ap, src_ap in (
                (w_ext[1][:, 0:D], W1), (w_ext[2][:, 0:D], W2), (wn_sb[:, :], Wn), (we_sb[:, :], We),
                (att_cols[:, 0:1], col(a_src1)), (att_cols[:, 1:2], col(a_dst1)),
                (att_cols[:, 2:3], col(a_src2)), (att_cols[:, 3:4], col(a_dst2)),
                (att_cols[:, 7:8], b1.unsqueeze(1)),
                (b2_row[:, :], b2.unsqueeze(0).broadcast_to((P, D))),
            ):
                sp.dma_start(dst_ap, src_ap).then_inc(S["weights"], 16)
            sp.dma_start(att_cols[:, 4:7], Wa.rearrange("a (s o) -> o (a s)", o=D),
                         allow_slow_non_contiguous=True).then_inc(S["weights"], 16)

            sp.wait_ge(S["consts"], 1)
            full = (GROUPS - 1) * GROUP
            for t, a, shift in ((src_g, src, 0), (dst_g, dst, 0), (next_g, dst, 1)):
                sp.dma_start(t[0:GROUPS - 1, :], a[shift:full + shift].rearrange("(g e) -> g e", e=GROUP))\
                  .then_inc(S["idx_in"], 16)
                sp.dma_start(t[GROUPS - 1:GROUPS, 0:TAIL - shift], a[full + shift:N].unsqueeze(0))\
                  .then_inc(S["idx_in"], 16)
            sp.dma_start(last_edge.rearrange("(g e) a -> g (e a)", e=GROUP), default_g[:, :])\
              .then_inc(S["neutral_out"], 16)
            sp.dma_start(partial[PADDED:PADDED + P, :], neutral_rows[:, :]).then_inc(S["neutral_out"], 16)
            for k in E:
                sp.dma_start(dst_parts[k][PADDED:PADDED + WINDOW * P, :].rearrange("(q a) c -> q (a c)", a=WINDOW),
                             no_parts[:, :]).then_inc(S["neutral_out"], 16)

            sp.wait_ge(S["idx_mark"], 4)
            sp.dma_start(dst_row.rearrange("(g e) -> g e", e=GROUP), dstf_g[:, :]).then_inc(S["idx_spread"], 16)
            for j in range(4):
                sp.dma_start(run_marks[:, j, :, :, :].rearrange("g h m e -> g h (m e)"),
                             marks_g[:, j, :, :].rearrange("g m e -> g (m e)").unsqueeze(1)
                             .broadcast_to((GROUPS, HEADS, 2 * P))).then_inc(S["idx_spread"], 16)
            sp.dma_start(seam_dst[1:SEAMS + 1].rearrange("(g i) -> g i", i=8), seam_ends[:, :])\
              .then_inc(S["seam_idx"], 16)
            sp.dma_start(seam_dst[0:1].unsqueeze(0), sentinels[0:1, 0:1]).then_inc(S["seam_idx"], 16)
            sp.dma_start(seam_dst[SEAMS + 1:SEAMS + 2].unsqueeze(0), sentinels[0:1, 1:2]).then_inc(S["seam_idx"], 16)
            sp.wait_ge(S["window_base"], 1)
            sp.dma_start(window_base[0, :].rearrange("(g j) -> g j", j=4), base_g[:, :]).then_inc(S["window_base"], 16)
            sp.wait_ge(S["window_base"], 17)
            sp.dma_start(base_bc[:, :], window_base.broadcast_to((P, TILES))).then_inc(S["window_base"], 16)
            sp.wait_ge(S["window_rel"], 1)
            sp.dma_start(rel_row.rearrange("(g e) -> g e", e=GROUP), rel_g[:, :]).then_inc(S["idx_spread"], 16)
            sp.wait_ge(S["window_fit"], 1)
            sp.dma_start(windows_fit[:, :], fit[:, :]).then_inc(S["window_fit"], 16)
            sp.wait_ge(S["seam_idx"], 48)
            sp.dma_start(seam_cur[:, :], seam_dst[1:SEAMS + 1].unsqueeze(0).broadcast_to((P, SEAMS)))\
              .then_inc(S["seam_const"], 16)
            sp.dma_start(seam_prev[:, :], seam_dst[0:SEAMS].unsqueeze(0).broadcast_to((P, SEAMS)))\
              .then_inc(S["seam_const"], 16)
            for t, first in ((seam_row_cur, 1), (seam_row_next, 2)):
                sp.dma_start(t[:, :], seam_dst[first:first + SEAMS].rearrange("(c p) -> p c", p=SEAM_CHUNK),
                             allow_slow_non_contiguous=True).then_inc(S["seam_const"], 16)

            def load_x(k):
                passes = (0, 2, 3)
                def load(r, s):
                    if isinstance(r, int) and r == 0:
                        after(sp, S["h"] if k == 2 else S["x1"], GROUPS if k > 0 else 0)
                    elif k == 0:
                        sp.wait_ge(S["h"], done((0, 2), 0, r, s) - 4)
                    elif k == 2:
                        sp.wait_ge(S["x1"], done((2,), 2, r, s) - 4)
                    else:
                        sp.wait_ge(S["out_row"], done((3,), 3, r, s) - 4)
                    if k == 3:
                        sp.dma_start(xin[s][:, :, :], node_rows(residual, r, s)).then_inc(SL["xin"][s], 16)
                    elif is_last(r, s):
                        sp.dma_start(xin[s][0:TAIL // 4, :, :], node_rows(x, r, s, TAIL)).then_inc(SL["xin"][s], 16)
                    else:
                        sp.dma_start(xin[s][:, :, :], node_rows(x, r, s)).then_inc(SL["xin"][s], 16)
                return load

            def load_node(k):
                def load(r, s):
                    after(sp, S["from_self"], done((1, 2), k, r, s) - 4)
                    sp.dma_start(self_rows[s][:, :, :], node_rows(table[k], r, s)).then_inc(SL["self_rows"][s], 16)
                return load

            def store_table(k):
                def store(r, s):
                    sp.wait_ge(S["table_rows"], done((0, 1, 2), k, r, s))
                    sp.dma_start(node_rows(table[k + 1], r, s), table_rows[s][:, :, :])\
                      .then_inc(SL["table_out"][s], 16)
                return store

            def store_x1(r, s):
                sp.wait_ge(S["x1"], done((2,), 2, r, s))
                sp.dma_start(node_rows(residual, r, s), x1[s][:, :, :]).then_inc(SL["x1_out"][s], 16)

            def store_out(r, s):
                sp.wait_ge(S["out_row"], done((3,), 3, r, s))
                if is_last(r, s):
                    sp.dma_start(node_rows(out, r, s, TAIL), out_rows[s][0:TAIL // 4, :, :]).then_inc(SL["out"][s], 16)
                else:
                    sp.dma_start(node_rows(out, r, s), out_rows[s][:, :, :]).then_inc(SL["out"][s], 16)

            def store_parts(k):
                def store(r, s):
                    sp.wait_ge(S["part_low"], done((0, 1, 2), k, r, s))
                    sp.dma_start(node_rows(dst_parts[k + 1], r, s), parts[s][:, :, :, :].rearrange("p j c h -> p j (c h)"))\
                      .then_inc(SL["parts_out"][s], 16)
                return store

            def load_windows(k):
                bases = []
                def load(r, s):
                    if s == 0:
                        n = STEPS * 4 if not isinstance(r, int) else min(STEPS * 4, TILES - STEPS * 4 * r)
                        bases[:] = nc.values_load_multi_w_load_instructions(
                            base_bc[0:1, bass.ds(r * (STEPS * 4), n)], [mybir.EngineType.SP], min_val=0, max_val=PADDED)[1]
                    after(sp, S["window_sum"], done(E, k, r, s) - 4)
                    for j in range(4):
                        sp.dma_start(window_parts[s][:, j, :, :].rearrange("p a c -> p (a c)"),
                                     dst_parts[k][bass.ds(bases[4 * s + j], WINDOW * P), :]
                                     .rearrange("(q a) c -> q (a c)", a=WINDOW)).then_inc(SL["dst_logit"][s], 16)
                return load

            def load_edge(k, windowed):
                def load(r, s):
                    g = STEPS * r + s
                    if s % 2 == 0:
                        after(sp, S["bwd"], done(E, k, r, s) - 3)
                        sp.dma_start(marks[s // 2][:, :, :, :].rearrange("q g m e -> q g (m e)"),
                                     run_marks[bass.ds(g, 2), :, :, :, :].rearrange("g j h m e -> (j h) g (m e)"))\
                          .then_inc(SL["marks"][s], 16)
                        if windowed:
                            after(sp, S["same"], done(E, k, r, s) - 3)
                            after(sp, S["one_hot"], done(E, k, r, s) - 3)
                            sp.dma_start(rel_bc[s // 2][:, :, :, :].rearrange("p g j e -> p (g j e)"),
                                         rel_row[bass.ds(g * GROUP, 2 * GROUP)].unsqueeze(0).broadcast_to((P, 2 * GROUP)))\
                              .then_inc(SL["rel_bc"][s], 16)
                    if not windowed:
                        after(sp, S["same"], done(E, k, r, s) - 2)
                        sp.dma_start(dst_bc[s][:, :, :].rearrange("p j e -> p (j e)"),
                                     dst_row[bass.ds(g * GROUP, GROUP)].unsqueeze(0).broadcast_to((P, GROUP)))\
                          .then_inc(SL["dst_bc"][s], 16)
                return load

            def load_attr(r, s):
                after(sp, S["attr_prod"], done((0,), 0, r, s) - 2)
                if is_last(r, s):
                    whole = TAIL // P
                    base = (GROUPS - 1) * GROUP
                    sp.dma_start(attr[s][:, 0:whole, :],
                                 edge_attr[base:base + whole * P, :].rearrange("(j p) c -> p j c", p=P))\
                      .then_inc(SL["attr"][s], 16)
                    sp.dma_start(attr[s][0:TAIL - whole * P, whole, :], edge_attr[base + whole * P:N, :])\
                      .then_inc(SL["attr"][s], 16)
                else:
                    sp.dma_start(attr[s][:, :, :], edge_rows(edge_attr, r, s)).then_inc(SL["attr"][s], 16)

            rounds(sp, (load_x(0), 0), (load_attr, 0), (store_table(0), 4), (store_parts(0), 6))
            wait_pass(sp, "last_out", (0,), 0, 4)
            sp.dma_start(node_idx[:, :, :], last_edge.rearrange("(g p j) a -> p g (j a)", g=GROUPS, p=P))\
              .then_inc(S["node_idx"], 16)
            for k in E:
                sp.wait_ge(S["idx_spread"], 16 * (2 + 4))
                if k == 1:
                    sp.wait_ge(S["neutral_out"], 16 * N_NEUTRAL)
                wait_pass(sp, "table_out", (0, 1, 2), k - 1)
                wait_pass(sp, "parts_out", (0, 1, 2), k - 1)
                either(sp, ((load_edge(k, True), 0), (load_windows(k), 0)), ((load_edge(k, False), 0),))
                wait_pass(sp, "part_out", E, k)
                if k > 1:
                    sp.wait_ge(S["seam_new"], k - 1)
                for end in range(2):
                    sp.dma_start(seam_rows[end:SEAM_CHUNK:2, :, :],
                                 partial[0:PADDED, :].rearrange("(c t p) w -> t c p w", p=P, c=SEAM_CHUNKS)[
                                     :, :, end * (P - 1), :]).then_inc(S["seam_loaded"], 16)
                if k == 1:
                    rounds(sp, (load_node(1), 0), (store_table(1), 4), (store_parts(1), 7))
                elif k == 2:
                    rounds(sp, (load_node(2), 0), (load_x(2), 0), (store_x1, 2), (store_table(2), 6), (store_parts(2), 9))
                else:
                    wait_pass(sp, "x1_out", (2,), 2)
                    rounds(sp, (load_x(3), 0), (store_out, 1))
            wait_pass(sp, "out", (3,), 3)

        @block.gpsimd
        def _(pool):
            pool.memset(src_g[:, :], 0)
            pool.memset(dst_g[:, :], N)
            pool.memset(next_g[:, :], N)
            pool.memset(default_g[:, :], NEUTRAL)
            pool.memset(neutral_rows[:, 0:D + HEADS], 0.0)
            pool.memset(no_parts[:, :], 0.0)
            pool.memset(neutral_rows[:, MAXIMUM], LOW)
            pool.memset(sentinels[:, 0:1], -1.0)
            pool.memset(sentinels[:, 1:2], float(N))
            pool.memset(ones[:, :], 1.0)
            pool.memset(minus_half[:, :], -0.5)
            pool.memset(seam_max[:, 0:1], LOW)
            pool.iota(node_in_window[:, :], pattern=[[1, WINDOW]], base=0, channel_multiplier=WINDOW)
            pool.iota(pos_i[:, :], pattern=[[P, TILES]], base=0, channel_multiplier=1)
            pool.memset(head_mask[:, :], 1.0)
            pool.memset(ident[:, :], 0.0).then_inc(S["consts"], 1)
            pool.wait_ge(S["consts"], 1)
            pool.affine_select(out=ident[:, :], in_=ident[:, :], compare_op=ALU.not_equal, fill=1.0,
                               base=0, pattern=[[-1, P]], channel_multiplier=1)
            pool.affine_select(out=head_mask[:, :], in_=head_mask[:, :], compare_op=ALU.is_ge, fill=0.0,
                               base=0, pattern=[[-HEAD_DIM, HEADS]], channel_multiplier=1).then_inc(S["consts"], 1)
            pool.wait_ge(S["consts"], 2)
            pool.affine_select(out=head_mask[:, :], in_=head_mask[:, :], compare_op=ALU.is_ge, fill=0.0,
                               base=HEAD_DIM - 1, pattern=[[HEAD_DIM, HEADS]], channel_multiplier=-1)\
                .then_inc(S["consts"], 1)
            node_limit = pool.to_reg(N - 1)
            row_limit = pool.to_reg(PADDED - 1)
            neutral_limit = pool.to_reg(NEUTRAL)
            part_limit = pool.to_reg(PADDED * ROW // HEADS - 1)

            def gather(to, frm, idx, limit, s):
                pool.indirect_dma_start(out=to, out_offset=None, in_=frm,
                                        in_offset=bass.IndirectOffsetOnAxis(ap=idx, axis=0),
                                        bounds_check=limit, oob_is_err=False).then_inc(s, 16)

            def scatter(to, frm, idx, limit, s):
                pool.indirect_dma_start(out=to, out_offset=bass.IndirectOffsetOnAxis(ap=idx, axis=0),
                                        in_=frm, in_offset=None,
                                        bounds_check=limit, oob_is_err=False).then_inc(s, 16)

            def rsqrt(r, s):
                if s % 2 == 1:
                    pool.wait_ge(S["var_eps"], done((0, 2), 2, r, s))
                    pool.wait_ge(S["neg_mean"], done((0, 2), 2, r, s) - 4)
                    pool.wait_ge(S["h"], done((0, 2), 2, r, s) - 4)
                    pool.tensor_tensor(rstd_pair[s // 2][:, :], var_pair[s // 2][:, :], minus_half[:, :], ALU.pow)\
                        .then_inc(S["rstd"], 2)

            def add_bias(r, s):
                wait_landed(pool, "xin", (0, 2, 3), 2, r, s)
                pool.tensor_tensor(xin[s][:, :, :], xin[s][:, :, :], b2_row[:, :].unsqueeze(1).broadcast_to((P, 4, D)),
                                   ALU.add).then_inc(S["biased"], 1)

            def scatter_last(r, s):
                pool.wait_ge(S["last_staged"], done((0,), 0, r, s))
                pool.sem_inc(S["round_begun"], 1)
                for j in range(4):
                    scatter(last_edge[:, :], pos_stage[s][:, j:j + 1], last_stage[s][:, j:j + 1], node_limit,
                            SL["last_out"][s])

            def gather_edge(k, with_dst):
                def step(r, s):
                    pool.wait_ge(S["staged"], done(E, k, r, s))
                    pool.sem_inc(S["round_begun"], 1)
                    for j in range(4):
                        gather(src_rows[s][:, j, :], table[k], src_stage[s][:, j:j + 1], row_limit, SL["src_rows"][s])
                        if with_dst:
                            gather(dst_logit[s][:, j, :], table[k].rearrange("n (a b) -> (n a) b", b=HEADS),
                                   dst_stage[s][:, j:j + 1], part_limit, SL["dst_logit"][s])
                return step

            def gather_part(k):
                def step(r, s):
                    pool.wait_ge(S["node_staged"], done(E, k, r, s))
                    pool.sem_inc(S["round_begun"], 1)
                    for j in range(4):
                        gather(edge_part[s][:, j, 0:ROW], partial[0:NEUTRAL + 1, :], node_stage[s][:, j:j + 1],
                               neutral_limit, SL["edge_part"][s])
                return step

            def split_rest(r, s):
                pool.wait_ge(S["part_high"], done((0, 1, 2), 1, r, s))
                pool.wait_ge(S["part_low"], done((0, 1, 2), 1, r, s) - 2)
                pool.tensor_tensor(rest[s][:, :, :], table_rows[s][:, :, LOGIT_DST], parts[s][:, :, 0, :],
                                   ALU.subtract).then_inc(S["part_rest"], 1)

            pool.wait_ge(S["neutral_out"], 16 * N_NEUTRAL)
            rounds(pool, (scatter_last, 0))
            wait_pass(pool, "last_out", (0,), 0, 4)
            pool.wait_ge(S["seam_node"], 1)
            for c in range(SEAM_CHUNKS):
                gather(seam_last_i[:, c:c + 1], last_edge[:, :], seam_node_i[:, c:c + 1], row_limit, S["seam_lastd"])
            for k in E:
                wait_pass(pool, "table_out", (0, 1, 2), k - 1)
                either(pool, ((gather_edge(k, False), 0),), ((gather_edge(k, True), 0),))
                pool.wait_ge(S["seam_new"], k)
                for c in range(SEAM_CHUNKS):
                    scatter(partial[0:PADDED, :], seam_new[:, c, :], seam_to_i[:, c:c + 1], row_limit, S["seam_out"])
                pool.wait_ge(S["seam_out"], 16 * SEAM_CHUNKS * k)
                if k == 2:
                    rounds(pool, (gather_part(k), 0), (add_bias, 2), (rsqrt, 3))
                elif k == 1:
                    rounds(pool, (gather_part(k), 0), (split_rest, 6))
                else:
                    rounds(pool, (gather_part(k), 0))

        @block.tensor
        def _(pe):
            pe.wait_ge(S["weights"], 16 * N_WEIGHTS)
            pe.wait_ge(S["consts"], 3)
            pe.transpose(bank[0][:, 0:P], w_ext[1][:, 0:D], ident[:, :])
            pe.transpose(bank[0][:, P:2 * P], w_ext[2][:, 0:D], ident[:, :])
            pe.transpose(bank[0][:, 2 * P:3 * P], wn_sb[:, :], ident[:, :]).then_inc(S["w_T"], 1)
            pe.wait_ge(S["w_T_sb"], 1)
            pe.wait_ge(S["att_mat"], 1)
            for i, lhs in enumerate((wT[:, 0, :], wT[:, 1, :], wn_sb[:, :])):
                pe.matmul(bank[1][:, 32 * i:32 * i + 32], lhs, att_mat[:, i, :], start=True, stop=True)
            pe.matmul(bank[1][:, 128:128 + D_EDGE], wa_rep[:, :], we_sb[:, :], start=True, stop=True)\
                .then_inc(S["w_ext_ps"], 1)
            for i, t in enumerate((srcf_g, dstf_g, lastf_g)):
                if i == 0:
                    pe.wait_ge(S["idx_f"], 1)
                if i == 2:
                    pe.wait_ge(S["idx_last"], 1)
                for j in range(4):
                    mm = pe.transpose(bank[4 + i][:, j * GROUPS:(j + 1) * GROUPS], t[:, j * P:(j + 1) * P],
                                      ident[0:GROUPS, 0:GROUPS])
                mm.then_inc(S["idx_T"], 1)
            pe.wait_ge(S["idx_out"], 3)

            pe.wait_ge(S["window_width"], 2)
            pe.transpose(bank[7][0:1, 0:GROUPS], widest_g[:, :], ident[0:GROUPS, 0:GROUPS]).then_inc(S["window_T"], 1)
            pe.wait_ge(S["window_width"], 3)

            def transpose_h(k):
                def step(r, s):
                    pe.wait_ge(S["h"] if k != 1 else S["merged"], done((0, 2) if k != 1 else (1, 2), k, r, s))
                    n = done((0, 1, 2), k, r, s) - 2
                    free(k, r, s)
                    rows = merged[s] if k == 1 else h[s]
                    for j in range(4):
                        mm = pe.transpose(ps_hT[s][:, j * P:(j + 1) * P], rows[:, j, :], ident[:, :])
                    mm.then_inc(S["hT_ps"], 1)
                return step

            def free(k, r, s):
                first = isinstance(r, int) and r == 0 and s < 2
                if k == 0:
                    after(pe, S["hT"], done((0, 2), 0, r, s) - 2)
                elif k == 1 and first:
                    pe.wait_ge(S["hT"], GROUPS)
                elif k == 1:
                    pe.wait_ge(S["elu"], done((1,), 1, r, s) - 2)
                elif first:
                    pe.wait_ge(S["elu"], GROUPS)
                else:
                    pe.wait_ge(S["hT"], done((0, 2), 2, r, s) - 2)

            def project(k):
                def step(r, s):
                    pe.wait_ge(S["hT"] if k != 1 else S["elu"], done((0, 2) if k != 1 else (1,), k, r, s))
                    after(pe, S["table_rows"], done((0, 1, 2), k, r, s) - 2)
                    for j in range(4):
                        o = (j % 2) * 256
                        mm = pe.matmul(ps_rows[s][j // 2][:, o:o + ROW], hT[s][:, j * P:(j + 1) * P],
                                       w_ext[k + 1][:, :], start=True, stop=True)
                    mm.then_inc(S["proj"], 1)
                return step

            def logits_to_rows(k):
                def step(r, s):
                    pe.wait_ge(S["logit"], done(E, k, r, s))
                    after(pe, S["fwd"], done(E, k, r, s) - 1)
                    pe.matmul(ps_logitT[0:64, 0:P], logit[:, :, :].rearrange("p j h -> p (j h)"), ident[:, :],
                              start=True, stop=True).then_inc(S["logitT"], 1)
                return step

            def from_window(k):
                def step(r, s):
                    pe.wait_ge(S["one_hot"], done(E, k, r, s))
                    wait_landed(pe, "dst_logit", E, k, r, s, 4)
                    after(pe, S["dst_sum"], done(E, k, r, s) - 2)
                    for j in range(4):
                        for a in range(WINDOW):
                            mm = pe.matmul(ps_window[s][:, j * PARTS * HEADS:(j + 1) * PARTS * HEADS],
                                           one_hot[s][:, a, j, :], window_parts[s][:, j, a, :], start=(a == 0), stop=(a == WINDOW - 1))
                    mm.then_inc(S["window_sum"], 1)
                return step

            def maxima_to_columns(k):
                def step(r, s):
                    pe.wait_ge(S["bwd"], done(E, k, r, s))
                    after(pe, S["shifted"], done(E, k, r, s) - 1)
                    after(pe, S["row_max"], done(E, k, r, s) - 1)
                    pe.matmul(ps_maxT[:, 0:64], run_max[:, :], ident[0:64, 0:64], start=True, stop=True)\
                        .then_inc(S["maxT"], 1)
                return step

            def run_sums(k, half):
                def step(r, s):
                    if half == 0:
                        pe.wait_ge(S["msg"], done(E, k, r, s))
                        pe.wait_ge(S["same"], done(E, k, r, s))
                        after(pe, S["agg_out"], done(E, k, r, s) - 2)
                    for j in (2 * half, 2 * half + 1):
                        o = (j % 2) * 256
                        mm = pe.matmul(ps_rows[s][half][:, o:o + D + HEADS], same[s][:, j, :], msg[s][:, j, :],
                                       start=True, stop=True)
                    if half == 1:
                        mm.then_inc(S["agg"], 1)
                return step

            def seam(k):
                pe.wait_ge(S["agg_out"], GROUPS * k)
                pe.wait_ge(S["shifted"], GROUPS * k)
                pe.wait_ge(S["row_max"], GROUPS * k)
                pe.wait_ge(S["seam_loaded"], 32 * k)
                for i, b in enumerate((4, 2, 0)):
                    if i < 2:
                        pe.wait_ge(S["seam_wide"], 2 * k - 1 + i)
                    for half, (c0, c1) in enumerate(HALVES):
                        for c in range(c0, c1):
                            o = (c - c0) * SEAM_CHUNK
                            rows = seam_wide[:, c, i, :] if i < 2 else seam_rows[:, c, 0:D]
                            mm = pe.transpose(bank[b + half][:, o:o + SEAM_CHUNK], rows,
                                              ident[0:SEAM_CHUNK, 0:SEAM_CHUNK])
                    mm.then_inc(S["seam_T"], 1)
                for b, t, scanned, count in ((6, seam_max[:, 1:SEAMS + 1], S["seam_maxed"], 2 * k),
                                             (4, seam_sumw[:, :], S["seam_scans"], 2 * k - 1),
                                             (2, seam_sumx[:, :], S["seam_scans"], 2 * k)):
                    pe.wait_ge(scanned, count)
                    for c in range(SEAM_CHUNKS):
                        mm = pe.transpose(bank[b + c // 4][0:SEAM_CHUNK, (c % 4) * P:(c % 4 + 1) * P],
                                          t[:, c * SEAM_CHUNK:(c + 1) * SEAM_CHUNK], ident[:, :])
                    mm.then_inc(S["seam_back"], 1)

            rounds(pe, (transpose_h(0), 0), (project(0), 0))
            for k in E:
                if k > 1:
                    pe.wait_ge(S["table_rows"], GROUPS * k)
                if k == 1:
                    pe.wait_ge(S["table_rows"], GROUPS)
                both = ((logits_to_rows(k), 1), (run_sums(k, 0), 2), (maxima_to_columns(k), 1))
                either(pe, (*both, (from_window(k), 0), (run_sums(k, 1), 2)), (*both, (run_sums(k, 1), 2)))
                seam(k)
                pe.wait_ge(S["seam_new"], k)
                if k < 3:
                    rounds(pe, (transpose_h(k), 0), (project(k), 1 if k == 1 else 0))

        @block.scalar
        def _(act):
            def relu_rows(k):
                def step(r, s):
                    act.wait_ge(S["neg_mean"], done((0, 2), k, r, s))
                    n = done((0, 1, 2), k, r, s) - 2
                    if k == 0:
                        wait_landed(act, "xin", (0, 2, 3), 0, r, s)
                        after(act, S["hT_ps"], n)
                    else:
                        act.wait_ge(S["hT_ps"], n)
                    rows = xin[s] if k == 0 else x1[s]
                    for j in range(4):
                        ins = act.activation(h[s][:, j, :], rows[:, j, :], ACT.Relu, bias=neg_mean[s][:, j:j + 1],
                                             scale=rstd[s][:, j:j + 1])
                    ins.then_inc(S["h"], 1)
                return step

            def copy_hT(k):
                def step(r, s):
                    act.wait_ge(S["hT_ps"], done((0, 1, 2), k, r, s))
                    after(act, S["proj"], done((0, 1, 2), k, r, s) - 2)
                    act.activation(hT[s][:, :], ps_hT[s][:, :], ACT.Copy).then_inc(S["hT"], 1)
                return step

            def elu_parts(r, s):
                act.wait_ge(S["hT_ps"], done((0, 1, 2), 1, r, s))
                after(act, S["elu"], done((1,), 1, r, s) - 2)
                act.activation(below[s], ps_hT[s][:, :], ACT.Exp, bias=att_cols[:, 7:8])\
                    .then_inc(S["exp_below"], 1)
                act.wait_ge(S["exp_below"], done((1,), 1, r, s))
                act.activation(ps_hT[s][:, :], ps_hT[s][:, :], ACT.Relu, bias=att_cols[:, 7:8])\
                    .then_inc(S["above"], 1)

            def evac(k):
                def step(r, s):
                    act.wait_ge(S["proj"], done((0, 1, 2), k, r, s))
                    wait_slot(act, "table_out", (0, 1, 2), k, r, s, 2)
                    after(act, S["part_rest"], done((0, 1, 2), k, r, s) - 2)
                    act.activation(table_rows[s][:, 0:2, :], pair(ps_rows[s][0], ROW), ACT.Copy)
                    act.activation(table_rows[s][:, 2:4, :], pair(ps_rows[s][1], ROW), ACT.Copy)\
                        .then_inc(S["table_rows"], 1)
                return step

            def split_high(k):
                def step(r, s):
                    act.wait_ge(S["table_rows"], done((0, 1, 2), k, r, s))
                    wait_slot(act, "parts_out", (0, 1, 2), k, r, s, 4)
                    act.activation(parts[s][:, :, 0, :], table_rows[s][:, :, LOGIT_DST], ACT.Copy)\
                        .then_inc(S["part_high"], 1)
                return step

            def split_mid(k):
                def step(r, s):
                    act.wait_ge(S["part_rest"], done((0, 1, 2), k, r, s))
                    act.activation(parts[s][:, :, 1, :], rest[s][:, :, :], ACT.Copy).then_inc(S["part_mid"], 1)
                return step

            def store_part(k):
                def step(r, s):
                    act.wait_ge(S["agg_out"], done(E, k, r, s))
                    act.wait_ge(S["row_max"], done(E, k, r, s))
                    act.dma_start(edge_rows(partial, r, s), part_rows[s][:, :, :]).then_inc(SL["part_out"][s], 16)
                return step

            def merge_exp(k):
                def step(r, s):
                    act.wait_ge(S["both_shift"], done((1, 2), k, r, s))
                    after(act, S["norm_w"], done((1, 2), k, r, s) - 1)
                    act.activation(both_w[:, :, :, :], both_shift[:, :, :, :], ACT.Exp).then_inc(S["both_exp"], 1)
                return step

            def run_exp(k):
                def step(r, s):
                    act.wait_ge(S["shifted"], done(E, k, r, s))
                    after(act, S["agg"], done(E, k, r, s) - 2)
                    act.activation(msg[s][:, :, D:D + HEADS], shifted[:, :, :], ACT.Exp).then_inc(S["prob"], 1)
                return step

            def evac_sums(k):
                def step(r, s):
                    act.wait_ge(S["agg"], done(E, k, r, s))
                    wait_slot(act, "part_out", E, k, r, s, 4)
                    act.activation(part_rows[s][:, 0:2, 0:D + HEADS], pair(ps_rows[s][0], D + HEADS), ACT.Copy)
                    act.activation(part_rows[s][:, 2:4, 0:D + HEADS], pair(ps_rows[s][1], D + HEADS), ACT.Copy)\
                        .then_inc(S["agg_out"], 1)
                return step

            def root(r, s):
                act.wait_ge(S["var_eps"], done((0, 2), 0, r, s))
                act.activation(std[s][:, :], var_eps[s][:, :], ACT.Sqrt).then_inc(S["std"], 1)

            rounds(act, (split_mid(0), 4), (root, 0), (relu_rows(0), 1), (evac(0), 2), (copy_hT(0), 1), (split_high(0), 2))
            for k in E:
                rounds(act, (run_exp(k), 1), (evac_sums(k), 2), (store_part(k), 2))
                act.wait_ge(S["seam_b"], 2 * k)
                act.activation(seam_exp[:, :, :], seam_exp[:, :, :], ACT.Exp).then_inc(S["seam_exped"], 1)
                if k == 1:
                    rounds(act, (elu_parts, 2), (split_mid(1), 5), (merge_exp(1), 0), (evac(1), 3), (split_high(1), 3))
                if k == 2:
                    rounds(act, (merge_exp(2), 0), (split_mid(2), 7), (relu_rows(2), 4), (evac(2), 5), (copy_hT(2), 4),
                           (split_high(2), 5))

        @block.vector
        def _(dve):
            dve.wait_ge(S["weights"], 16 * N_WEIGHTS)
            dve.wait_ge(S["consts"], 3)
            for i in range(2):
                for j in range(2):
                    c = 2 * i + j
                    dve.tensor_scalar(att_mat[:, i, HEADS * j:HEADS * j + HEADS], head_mask[:, :],
                                      att_cols[:, c:c + 1], None, ALU.mult)
            for j in range(2):
                dve.tensor_scalar(att_mat[:, 2, HEADS * j:HEADS * j + HEADS], ones[:, 0:HEADS],
                                  att_cols[:, 4 + j:5 + j], None, ALU.mult)
            dve.tensor_scalar(wa_rep[:, :], ones[:, :], att_cols[:, 6:7], None, ALU.mult).then_inc(S["att_mat"], 1)
            dve.wait_ge(S["w_T"], 1)
            dve.tensor_copy(w_ext[3][:, 0:D], bank[0][:, 2 * P:3 * P])
            dve.tensor_copy(wT[:, :, :], bank[0][:, 0:2 * P].rearrange("p (a b) -> p a b", a=2))\
                .then_inc(S["w_T_sb"], 1)
            dve.wait_ge(S["w_ext_ps"], 1)
            for i in range(3):
                dve.tensor_copy(w_ext[i + 1][:, D:ROW], bank[1][:, 32 * i:32 * i + 32])
            dve.tensor_copy(we_row[:, :], bank[1][:, 128:128 + D_EDGE]).then_inc(S["w_ext_sb"], 1)

            dve.wait_ge(S["idx_in"], 96)
            dve.tensor_copy(srcf_g[:, :], src_g[:, :])
            dve.tensor_copy(dstf_g[:, :], dst_g[:, :])
            dve.tensor_copy(nextf_g[:, :], next_g[:, :]).then_inc(S["idx_f"], 1)
            dve.wait_ge(S["idx_f"], 1)
            starts, ends = marks_g[:, :, 0, :], marks_g[:, :, 1, :]
            tiled = lambda t: t[:, :].rearrange("g (j e) -> g j e", e=P)
            dve.tensor_tensor(ends, tiled(dstf_g), tiled(nextf_g), ALU.not_equal)
            dve.memset(starts[:, :, 0:1], 1.0)
            dve.tensor_tensor(starts[:, :, 1:P], tiled(dstf_g)[:, :, 1:P], tiled(dstf_g)[:, :, 0:P - 1],
                              ALU.not_equal).then_inc(S["idx_start"], 1)
            dve.wait_ge(S["idx_start"], 1)
            dve.tensor_scalar(tiled(lastf_g), ends, -float(SKIP), float(SKIP), ALU.mult, ALU.add)\
                .then_inc(S["idx_start"], 1)
            dve.wait_ge(S["idx_start"], 2)
            dve.tensor_tensor(lastf_g[:, :], lastf_g[:, :], dstf_g[:, :], ALU.add).then_inc(S["idx_last"], 1)
            dve.tensor_scalar(ends, ends, LOW, None, ALU.mult).then_inc(S["idx_mark"], 1)
            dve.tensor_scalar(starts, starts, LOW, None, ALU.mult).then_inc(S["idx_mark"], 1)
            dve.tensor_copy(seam_ends[:, :].rearrange("g (j i) -> g j i", i=2), tiled(dstf_g)[:, :, 0:P:P - 1]).then_inc(S["idx_mark"], 2)
            tile_major = lambda t: t[:, :].rearrange("p (g j) -> p j g", j=4)
            by_tile = lambda b: b[:, 0:TILES].rearrange("p (j g) -> p j g", j=4)
            dve.wait_ge(S["idx_T"], 1)
            dve.tensor_copy(tile_major(src_i), by_tile(bank[4])).then_inc(S["idx_out"], 1)
            dve.wait_ge(S["idx_T"], 2)
            dve.tensor_copy(tile_major(dst_f), by_tile(bank[5]))
            width = ROW // HEADS
            dve.tensor_scalar(tile_major(dst_i), by_tile(bank[5]), float(width), float(width - 1), ALU.mult, ALU.add)\
                .then_inc(S["idx_out"], 1)
            dve.wait_ge(S["idx_T"], 3)
            dve.tensor_copy(tile_major(last_i), by_tile(bank[6])).then_inc(S["idx_out"], 1)

            def stage_last(r, s):
                g = STEPS * r + s
                wait_slot(dve, "last_out", (0,), 0, r, s, 4, 4)
                dve.tensor_scalar(last_stage[s][:, :], last_i[:, bass.ds(g * 4, 4)], 0.0, None, ALU.add)
                dve.tensor_scalar(pos_stage[s][:, :], pos_i[:, bass.ds(g * 4, 4)], 0.0, None, ALU.add)\
                    .then_inc(S["last_staged"], 1)

            def stage_next_last(r, s):
                if more(r, s, 4):
                    stage_last(r + 1, s)

            dve.wait_ge(S["idx_out"], 3)
            for s in range(STEPS):
                stage_last(0, s)
            bases = seam_ends[:, :].rearrange("g (j i) -> g j i", i=2)
            dve.wait_ge(S["idx_mark"], 4)
            dve.tensor_copy(base_g[:, :], bases[:, :, 0]).then_inc(S["window_base"], 1)
            dve.tensor_tensor(width_g[:, :], bases[:, :, 1], bases[:, :, 0], ALU.subtract).then_inc(S["window_width"], 1)
            dve.wait_ge(S["window_width"], 1)
            dve.tensor_reduce(widest_g[:, :], width_g[:, :], AX.X, ALU.max).then_inc(S["window_width"], 1)
            dve.wait_ge(S["window_T"], 1)
            dve.tensor_reduce(widest[:, :], bank[7][0:1, 0:GROUPS], AX.X, ALU.max).then_inc(S["window_width"], 1)
            dve.wait_ge(S["window_width"], 3)
            dve.tensor_scalar(fit[:, :], widest[:, :], float(WINDOW * P - 1), None, ALU.is_le)\
                .then_inc(S["window_fit"], 1)
            dve.tensor_tensor(rel_g[:, :].rearrange("g (j e) -> g j e", e=P),
                              dstf_g[:, :].rearrange("g (j e) -> g j e", e=P),
                              bases[:, :, 0].unsqueeze(2).broadcast_to((GROUPS, 4, P)), ALU.subtract)\
                .then_inc(S["window_rel"], 1)
            dve.wait_ge(S["window_base"], 33)
            dve.tensor_tensor(rel_f[:, :], dst_f[:, :], base_bc[:, :], ALU.subtract)
            dve.tensor_copy(window_node[:, :], node_in_window[:, :]).then_inc(S["window_node"], 1)
            dve.wait_ge(S["window_node"], 1)
            dve.wait_ge(S["seam_const"], 64)
            dve.tensor_tensor(seam_cur[:, :], seam_cur[:, :], seam_prev[:, :], ALU.is_equal).then_inc(S["seam_mask"], 1)
            dve.tensor_copy(seam_node_i[:, :], seam_row_cur[:, :]).then_inc(S["seam_node"], 1)
            dve.tensor_tensor(seam_to_f[:, :], seam_row_cur[:, :], seam_row_next[:, :], ALU.is_equal)
            dve.memset(seam_once[:, :], 1.0).then_inc(S["seam_mask"], 1)
            dve.wait_ge(S["seam_mask"], 2)
            dve.tensor_scalar(seam_reset[:, :], seam_cur[:, :], -LOW, LOW, ALU.mult, ALU.add)
            dve.tensor_scalar(seam_once[:, 1:SEAMS:2], seam_cur[:, 1:SEAMS:2], -1.0, 1.0, ALU.mult, ALU.add)\
                .then_inc(S["seam_mask"], 1)
            dve.wait_ge(S["seam_mask"], 3)
            dve.wait_ge(S["idx_out"], 3)
            dve.wait_ge(S["w_ext_sb"], 1)

            def norm_stats(k):
                def step(r, s):
                    if k == 0:
                        wait_landed(dve, "xin", (0, 2, 3), 0, r, s)
                    else:
                        dve.wait_ge(S["x1"], done((2,), 2, r, s))
                    after(dve, S["moments"], done((0, 2), k, r, s) - 1)
                    rows = xin[s] if k == 0 else x1[s]
                    for j in range(4):
                        ins = dve.bn_stats(stats[:, j, :], rows[:, j, :])
                    ins.then_inc(S["stats"], 1)
                return step

            def norm_moments(k):
                def step(r, s):
                    dve.wait_ge(S["stats"], done((0, 2), k, r, s))
                    dve.sem_inc(S["round_begun"], 1)
                    for j in range(4):
                        ins = dve.bn_aggr(moments[s][:, j, :], stats[:, j, :])
                    ins.then_inc(S["moments"], 1)
                return step

            def norm_variance(k):
                def step(r, s):
                    dve.wait_ge(S["moments"], done((0, 2), k, r, s))
                    dve.tensor_scalar(var_eps[s][:, :], moments[s][:, :, 1], EPS, None, ALU.add).then_inc(S["var_eps"], 1)
                return step

            def norm_shift(k):
                L = (0, 2)
                def step(r, s):
                    if k == 0:
                        dve.wait_ge(S["std"], done((0,), 0, r, s))
                        dve.reciprocal(rstd[s][:, :], std[s][:, :]).then_inc(S["rstd_v"], 1)
                        dve.wait_ge(S["rstd_v"], done((0,), 0, r, s))
                    else:
                        dve.wait_ge(S["rstd"], done((2,), 2, r, s))
                    after(dve, S["h"], done(L, k, r, s) - 2)
                    dve.scalar_tensor_tensor(out=neg_mean[s][:, :], in0=moments[s][:, :, 0], scalar=-1.0,
                                             in1=rstd[s][:, :], op0=ALU.mult, op1=ALU.mult).then_inc(S["neg_mean"], 1)
                return step

            def stage_edge(r, s, with_dst=True):
                g = STEPS * r + s
                ins = dve.tensor_scalar(src_stage[s][:, :], src_i[:, bass.ds(g * 4, 4)], 0.0, None, ALU.add)
                if with_dst:
                    ins = dve.tensor_scalar(dst_stage[s][:, :], dst_i[:, bass.ds(g * 4, 4)], 0.0, None, ALU.add)
                ins.then_inc(S["staged"], 1)

            def stage_node(r, s):
                dve.tensor_scalar(node_stage[s][:, :], node_idx[:, bass.ds(STEPS * r + s, 1), :].rearrange("p g j -> p (g j)"),
                                  0.0, None, ALU.add).then_inc(S["node_staged"], 1)

            def one_hot_of(k):
                def step(r, s):
                    wait_landed(dve, "rel_bc", E, k, r, s - s % 2)
                    after(dve, S["window_sum"], done(E, k, r, s) - 2)
                    for a in range(WINDOW):
                        ins = dve.tensor_scalar(one_hot[s][:, a, :, :], rel_bc[s // 2][:, s % 2, :, :],
                                                window_node[:, a:a + 1], None, ALU.is_equal)
                    ins.then_inc(S["one_hot"], 1)
                return step

            def same_of(k, windowed):
                def step(r, s):
                    if windowed:
                        wait_landed(dve, "rel_bc", E, k, r, s - s % 2)
                        along, across = rel_bc[s // 2][:, s % 2, :, :], rel_f
                    else:
                        wait_landed(dve, "dst_bc", E, k, r, s)
                        along, across = dst_bc[s][:, :, :], dst_f
                    after(dve, S["agg"], done(E, k, r, s) - 2)
                    g = STEPS * r + s
                    dve.tensor_tensor(same[s][:, :, :], along,
                                      across[:, bass.ds(g * 4, 4)].unsqueeze(2).broadcast_to((P, 4, P)), ALU.is_equal)\
                        .then_inc(S["same"], 1)
                return step

            def attr_product(r, s):
                dve.wait_ge(SL["attr"][s], 16 * (r + 1) + (16 if is_last(r, s) else 0))
                after(dve, S["attr_dot"], done((0,), 0, r, s) - 1)
                dve.tensor_tensor(attr_prod[:, :, :], attr[s][:, :, :],
                                  we_row[:, :].unsqueeze(1).broadcast_to((P, 4, D_EDGE)), ALU.mult)\
                    .then_inc(S["attr_prod"], 1)

            def attr_sum(r, s):
                dve.wait_ge(S["attr_prod"], done((0,), 0, r, s))
                dve.tensor_reduce(attr_dot[:, bass.ds((STEPS * r + s) * 4, 4)], attr_prod[:, :, :], AX.X, ALU.add)\
                    .then_inc(S["attr_dot"], 1)

            def join_parts(k):
                def step(r, s):
                    dve.wait_ge(S["window_sum"], done(E, k, r, s))
                    after(dve, S["logit_sum"], done(E, k, r, s) - 1)
                    dve.tensor_reduce(dst_sum[:, :, :], ps_window[s][:, 0:4 * PARTS * HEADS].rearrange(
                        "p (j c h) -> p j h c", c=PARTS, h=HEADS), AX.X, ALU.add).then_inc(S["dst_sum"], 1)
                return step

            def add_attr(r, s):
                wait_landed(dve, "src_rows", E, 3, r, s, 4)
                after(dve, S["logit_sum"], done(E, 3, r, s) - 1)
                dve.tensor_tensor(with_attr[:, :, :], src_rows[s][:, :, LOGIT_SRC],
                                  attr_dot[:, bass.ds((STEPS * r + s) * 4, 4)].unsqueeze(2)
                                  .broadcast_to((P, 4, HEADS)), ALU.add).then_inc(S["with_attr"], 1)

            def sum_logits(k, windowed):
                def step(r, s):
                    wait_landed(dve, "src_rows", E, k, r, s, 4)
                    of_src = src_rows[s][:, :, LOGIT_SRC]
                    if k == 3:
                        dve.wait_ge(S["with_attr"], done((3,), 3, r, s))
                        of_src = with_attr[:, :, :]
                    if windowed:
                        dve.wait_ge(S["dst_sum"], done(E, k, r, s))
                        of_dst = dst_sum[:, :, :]
                    else:
                        wait_landed(dve, "dst_logit", E, k, r, s, 4)
                        of_dst = dst_logit[s][:, :, :]
                    dve.tensor_tensor(logit_sum[:, :, :], of_src, of_dst, ALU.add)\
                        .then_inc(S["logit_sum"], 1)
                return step

            def leaky(k):
                def step(r, s):
                    dve.wait_ge(S["logit_sum"], done(E, k, r, s))
                    dve.scalar_tensor_tensor(out=logit[:, :, :], in0=logit_sum[:, :, :], scalar=NEG_SLOPE,
                                             in1=logit_sum[:, :, :], op0=ALU.mult, op1=ALU.max).then_inc(S["logit"], 1)
                return step

            def scan_forward(k):
                def step(r, s):
                    dve.wait_ge(S["logitT"], done(E, k, r, s))
                    wait_landed(dve, "marks", E, k, r, s - s % 2)
                    dve.tensor_tensor_scan(run_fwd[:, :], marks[s // 2][:, s % 2, 0, :], ps_logitT[0:64, 0:P], LOW,
                                           ALU.add, ALU.max).then_inc(S["fwd"], 1)
                return step

            def scan_back(k):
                def step(r, s):
                    dve.wait_ge(S["fwd"], done(E, k, r, s))
                    dve.tensor_tensor_scan(run_max[:, ::-1], marks[s // 2][:, s % 2, 1, ::-1], run_fwd[:, ::-1], LOW,
                                           ALU.add, ALU.max).then_inc(S["bwd"], 1)
                return step

            def subtract_max(k):
                def step(r, s):
                    dve.wait_ge(S["maxT"], done(E, k, r, s))
                    after(dve, S["prob"], done(E, k, r, s) - 1)
                    maxima = ps_maxT[:, 0:64].rearrange("p (j h) -> p j h", h=HEADS)
                    dve.tensor_tensor(shifted[:, :, :], logit[:, :, :], maxima, ALU.subtract).then_inc(S["shifted"], 1)
                    wait_slot(dve, "part_out", E, k, r, s, 4)
                    dve.tensor_copy(part_rows[s][:, :, MAXIMUM], maxima).then_inc(S["row_max"], 1)
                return step

            def weigh(k):
                def step(r, s):
                    dve.wait_ge(S["prob"], done(E, k, r, s))
                    dve.tensor_tensor(by_head(msg[s][:, :, 0:D]), by_head(src_rows[s][:, :, 0:D]),
                                      spread(msg[s][:, :, D:D + HEADS]), ALU.mult).then_inc(S["msg"], 1)
                return step

            def stage_next(k, windowed):
                def step(r, s):
                    dve.wait_ge(S["msg"], done(E, k, r, s))
                    if more(r, s, 4):
                        stage_edge(r + 1, s, not windowed)
                return step

            def edge_stages(k, windowed):
                return [*([(add_attr, 1)] if k == 3 else []), *([(join_parts(k), 1)] if windowed else []),
                        (weigh(k), 2), (sum_logits(k, windowed), 1), (stage_next(k, windowed), 2), (leaky(k), 1),
                        (same_of(k, windowed), 1), (scan_forward(k), 1),
                        (scan_back(k), 1), *([(one_hot_of(k), 0)] if windowed else []), (subtract_max(k), 1)]

            def to_rows(k, back, b, part, step):
                dve.wait_ge(S["seam_back"], 3 * (k - 1) + back)
                for half, (c0, c1) in enumerate(HALVES):
                    got = bank[b + half][0:SEAM_CHUNK, 0:(c1 - c0) * P].rearrange("p (c f) -> p c f", f=P)
                    ins = dve.tensor_copy(seam_new[:, c0:c1, part], got[:, :, 0:P:step])
                return ins

            def seam(k):
                if k == 1:
                    dve.wait_ge(S["seam_lastd"], 16 * SEAM_CHUNKS)
                    dve.scalar_tensor_tensor(out=seam_to_i[:, :], in0=seam_to_f[:, :], scalar=float(SKIP),
                                             in1=seam_last_i[:, :], op0=ALU.mult, op1=ALU.add)
                dve.wait_ge(S["seam_loaded"], 32 * k)
                for i, part in enumerate((MAXIMUM, WEIGHT)):
                    dve.tensor_copy(seam_wide[:, :, i, :].rearrange("p c (h d) -> p c h d", h=HEADS),
                                    seam_rows[:, :, part].unsqueeze(3).broadcast_to(
                                        (SEAM_CHUNK, SEAM_CHUNKS, HEADS, HEAD_DIM))).then_inc(S["seam_wide"], 1)
                dve.wait_ge(S["seam_T"], 3 * k - 2)
                cols = [(c0 * SEAM_CHUNK, c1 * SEAM_CHUNK) for c0, c1 in HALVES]
                for half, (a, b) in enumerate(cols):
                    if half:
                        dve.wait_ge(S["seam_maxed"], 2 * k - 1)
                    dve.tensor_tensor_scan(seam_max[:, 1 + a:1 + b], seam_reset[:, a:b], bank[4 + half][:, 0:b - a],
                                           seam_max[:, a:a + 1], ALU.add, ALU.max).then_inc(S["seam_maxed"], 1)
                dve.wait_ge(S["seam_maxed"], 2 * k)
                dve.tensor_tensor(seam_w[:, :], seam_max[:, 0:SEAMS], seam_reset[:, :], ALU.add).then_inc(S["seam_a"], 1)
                dve.wait_ge(S["seam_a"], k)
                dve.tensor_tensor(seam_exp[:, 0, :], seam_w[:, :], seam_max[:, 1:SEAMS + 1], ALU.subtract)\
                    .then_inc(S["seam_b"], 1)
                for half, (a, b) in enumerate(cols):
                    ins = dve.tensor_tensor(seam_exp[:, 1, a:b], bank[4 + half][:, 0:b - a], seam_max[:, 1 + a:1 + b],
                                            ALU.subtract)
                ins.then_inc(S["seam_b"], 1)
                dve.wait_ge(S["seam_exped"], k)
                dve.tensor_tensor(seam_x[:, :], seam_exp[:, 1, :], seam_once[:, :], ALU.mult).then_inc(S["seam_c"], 1)
                dve.wait_ge(S["seam_c"], 3 * k - 2)
                dve.wait_ge(S["seam_T"], 3 * k - 1)
                for half, (a, b) in enumerate(cols):
                    ins = dve.tensor_tensor(seam_w[:, a:b], seam_x[:, a:b], bank[2 + half][:, 0:b - a], ALU.mult)
                ins.then_inc(S["seam_c"], 1)
                dve.wait_ge(S["seam_c"], 3 * k - 1)
                dve.wait_ge(S["seam_T"], 3 * k)
                for half, (a, b) in enumerate(cols):
                    ins = dve.tensor_tensor(seam_x[:, a:b], seam_x[:, a:b], bank[half][:, 0:b - a], ALU.mult)
                ins.then_inc(S["seam_c"], 1)
                dve.tensor_tensor_scan(seam_sumw[:, :], seam_exp[:, 0, :], seam_w[:, :], 0.0, ALU.mult, ALU.add)\
                    .then_inc(S["seam_scans"], 1)
                if k > 1:
                    dve.wait_ge(S["seam_out"], 16 * SEAM_CHUNKS * (k - 1))
                to_rows(k, 1, 6, MAXIMUM, HEAD_DIM)
                dve.wait_ge(S["seam_c"], 3 * k)
                dve.tensor_tensor_scan(seam_sumx[:, :], seam_exp[:, 0, :], seam_x[:, :], 0.0, ALU.mult, ALU.add)\
                    .then_inc(S["seam_scans"], 1)
                to_rows(k, 2, 4, WEIGHT, HEAD_DIM)
                to_rows(k, 3, 2, slice(0, D), 1).then_inc(S["seam_new"], 1)

            M = (1, 2)

            def self_sum_of(k):
                def step(r, s):
                    wait_landed(dve, "self_rows", M, k, r, s)
                    dve.tensor_tensor(self_sum[:, :, :], self_rows[s][:, :, LOGIT_SRC], self_rows[s][:, :, LOGIT_DST],
                                      ALU.add).then_inc(S["self_sum"], 1)
                return step

            def self_logit_of(k):
                def step(r, s):
                    dve.wait_ge(S["self_sum"], done(M, k, r, s))
                    dve.scalar_tensor_tensor(out=edge_part[s][:, :, SELF_LOGIT], in0=self_sum[:, :, :], scalar=NEG_SLOPE,
                                             in1=self_sum[:, :, :], op0=ALU.mult, op1=ALU.max)\
                        .then_inc(S["self_logit"], 1)
                return step

            def max_of(k):
                def step(r, s):
                    dve.wait_ge(S["self_logit"], done(M, k, r, s))
                    wait_landed(dve, "edge_part", E, k, r, s, 4)
                    dve.tensor_tensor(both_max[:, :, :], edge_part[s][:, :, SELF_LOGIT], edge_part[s][:, :, MAXIMUM],
                                      ALU.max)\
                        .then_inc(S["both_max"], 1)
                return step

            def shift_of(k):
                def step(r, s):
                    dve.wait_ge(S["both_max"], done(M, k, r, s))
                    both = edge_part[s][:, :, MAXIMUM.start:SELF_LOGIT.stop].rearrange("p j (a h) -> p j a h", a=2)
                    dve.tensor_tensor(both_shift[:, :, :, :], both,
                                      both_max[:, :, :].unsqueeze(2).broadcast_to((P, 4, 2, HEADS)), ALU.subtract)\
                        .then_inc(S["both_shift"], 1)
                return step

            def edge_weight(k):
                def step(r, s):
                    dve.wait_ge(S["both_exp"], done(M, k, r, s))
                    dve.tensor_tensor(edge_w[:, :, :], edge_part[s][:, :, WEIGHT], both_w[:, :, 0, :], ALU.mult)\
                        .then_inc(S["edge_w"], 1)
                return step

            def total_weight(k):
                def step(r, s):
                    dve.wait_ge(S["edge_w"], done(M, k, r, s))
                    dve.scalar_tensor_tensor(out=total_w[:, :, :], in0=edge_w[:, :, :], scalar=1e-16,
                                             in1=both_w[:, :, 1, :], op0=ALU.add, op1=ALU.add).then_inc(S["total_w"], 1)
                return step

            def invert(k):
                def step(r, s):
                    dve.wait_ge(S["total_w"], done(E, k, r, s))
                    dve.reciprocal(inv_w[:, :, :], total_w[:, :, :]).then_inc(S["inv_w"], 1)
                return step

            def normalise(k):
                def step(r, s):
                    dve.wait_ge(S["inv_w"], done(E, k, r, s))
                    after(dve, S["from_self"], done(M, k, r, s) - 1)
                    dve.tensor_tensor(norm_w, both_w[:, :, :, :],
                                      inv_w[:, :, :].unsqueeze(2).broadcast_to((P, 4, 2, HEADS)), ALU.mult)\
                        .then_inc(S["norm_w"], 1)
                return step

            def edges_share(k):
                def step(r, s):
                    dve.wait_ge(S["norm_w"], done(M, k, r, s))
                    after(dve, S["merged"], done(M, k, r, s) - 1)
                    dve.tensor_tensor(by_head(from_edges), by_head(edge_part[s][:, :, 0:D]),
                                      spread(norm_w[:, :, 0, :]), ALU.mult).then_inc(S["from_edges"], 1)
                return step

            def self_share(k):
                def step(r, s):
                    dve.tensor_tensor(by_head(from_self[:, :, :]), by_head(self_rows[s][:, :, 0:D]),
                                      spread(norm_w[:, :, 1, :]), ALU.mult).then_inc(S["from_self"], 1)
                    dve.wait_ge(S["from_edges"], done(E, k, r, s))
                    if more(r, s, 4):
                        stage_node(r + 1, s)
                return step

            def merge(k):
                def step(r, s):
                    dve.wait_ge(S["from_self"], done(M, k, r, s))
                    if k == 1:
                        after(dve, S["hT_ps"], done((0, 1, 2), 1, r, s) - 2)
                    else:
                        after(dve, S["x1"], done((2,), 2, r, s) - 2)
                    dve.tensor_tensor(merged[s][:, :, :], from_edges, from_self[:, :, :], ALU.add)\
                        .then_inc(S["merged"], 1)
                return step

            def add_x(r, s):
                dve.wait_ge(S["merged"], done(M, 2, r, s))
                dve.wait_ge(S["biased"], done((2,), 2, r, s))
                wait_slot(dve, "x1_out", (2,), 2, r, s, 4)
                after(dve, S["h"], done((0, 2), 2, r, s) - 4)
                dve.tensor_tensor(x1[s][:, :, :], merged[s][:, :, :], xin[s][:, :, :], ALU.add).then_inc(S["x1"], 1)

            def below_zero(r, s):
                dve.wait_ge(S["exp_below"], done((1,), 1, r, s))
                dve.tensor_scalar(below[s], below[s], 1.0, -1.0, ALU.min, ALU.add).then_inc(S["below"], 1)

            def elu(r, s):
                dve.wait_ge(S["below"], done((1,), 1, r, s))
                dve.wait_ge(S["above"], done((1,), 1, r, s))
                after(dve, S["proj"], done((0, 1, 2), 1, r, s) - 2)
                dve.tensor_tensor(hT[s][:, :], below[s], ps_hT[s][:, :], ALU.add).then_inc(S["elu"], 1)

            def finish(r, s):
                n = done(E, 3, r, s)
                wait_landed(dve, "edge_part", E, 3, r, s, 4)
                dve.tensor_scalar(edge_w[:, :, :], edge_part[s][:, :, WEIGHT], 0.0, None, ALU.is_equal)\
                    .then_inc(S["zero_w"], 1)
                dve.wait_ge(S["zero_w"], done((3,), 3, r, s))
                dve.tensor_tensor(total_w[:, :, :], edge_w[:, :, :], edge_part[s][:, :, WEIGHT], ALU.add)\
                    .then_inc(S["total_w"], 1)
                dve.wait_ge(S["total_w"], n)
                dve.reciprocal(inv_w[:, :, :], total_w[:, :, :]).then_inc(S["inv_w"], 1)
                dve.wait_ge(S["inv_w"], n)
                dve.tensor_tensor(by_head(from_edges), by_head(edge_part[s][:, :, 0:D]),
                                  spread(inv_w[:, :, :]), ALU.mult).then_inc(S["from_edges"], 1)
                dve.wait_ge(S["from_edges"], n)
                if more(r, s, 4):
                    stage_node(r + 1, s)
                wait_landed(dve, "xin", (0, 2, 3), 3, r, s)
                wait_slot(dve, "out", (3,), 3, r, s, 2)
                dve.tensor_tensor(out_rows[s][:, :, :], from_edges, xin[s][:, :, :], ALU.add)\
                    .then_inc(S["out_row"], 1)

            def split_rest(k):
                def step(r, s):
                    dve.wait_ge(S["part_high"], done((0, 1, 2), k, r, s))
                    after(dve, S["part_low"], done((0, 1, 2), k, r, s) - 2)
                    dve.tensor_tensor(rest[s][:, :, :], table_rows[s][:, :, LOGIT_DST], parts[s][:, :, 0, :],
                                      ALU.subtract).then_inc(S["part_rest"], 1)
                return step

            def split_low(k):
                def step(r, s):
                    dve.wait_ge(S["part_mid"], done((0, 1, 2), k, r, s))
                    dve.tensor_tensor(parts[s][:, :, 2, :], rest[s][:, :, :], parts[s][:, :, 1, :],
                                      ALU.subtract).then_inc(S["part_low"], 1)
                return step

            rounds(dve, (split_low(0), 5), (stage_next_last, 0), (norm_shift(0), 1), (norm_stats(0), 0), (attr_product, 0),
                   (norm_moments(0), 0), (split_rest(0), 3), (norm_variance(0), 0), (attr_sum, 0))
            dve.wait_ge(S["attr_dot"], GROUPS)
            for k in E:
                for s in range(STEPS):
                    stage_edge(0, s)
                either(dve, edge_stages(k, True), edge_stages(k, False))
                seam(k)
                if k == 1:
                    dve.wait_ge(S["node_idx"], 16)
                for s in range(STEPS):
                    stage_node(0, s)
                if k == 1:
                    rounds(dve, (self_sum_of(1), 0), (edges_share(1), 1), (self_logit_of(1), 0), (self_share(1), 1),
                           (max_of(1), 0), (below_zero, 2), (shift_of(1), 0), (merge(1), 1), (edge_weight(1), 0),
                           (elu, 2), (total_weight(1), 0), (split_low(1), 6), (invert(1), 0), (normalise(1), 0))
                elif k == 2:
                    rounds(dve, (split_low(2), 8), (self_sum_of(2), 0), (edges_share(2), 1), (self_logit_of(2), 0),
                           (self_share(2), 1), (max_of(2), 0), (norm_shift(2), 4), (shift_of(2), 0), (merge(2), 1),
                           (edge_weight(2), 0), (add_x, 1), (total_weight(2), 0), (norm_stats(2), 1), (invert(2), 0),
                           (norm_moments(2), 1), (split_rest(2), 6), (norm_variance(2), 1), (normalise(2), 0))
                else:
                    rounds(dve, (finish, 0))


_INS = ['x', 'src', 'dst', 'edge_attr_64', 'L0_gnn_W1', 'L0_gnn_a_src1', 'L0_gnn_a_dst1', 'L0_gnn_b1', 'L0_gnn_W2',
        'L0_gnn_a_src2', 'L0_gnn_a_dst2', 'L0_gnn_b2', 'L1_gnn_Wn', 'L1_gnn_We', 'L1_gnn_Wa']


def kernel(**inputs):
    import numpy as _np
    import concourse.bacc as _bacc
    from concourse import mybir as _mybir
    from concourse.bass_utils import run_bass_kernel_spmd as _run

    nc = _bacc.Bacc("TRN2", target_bir_lowering=False, num_devices=1)
    arrays, args = {}, []
    for name in _INS:
        a = _np.ascontiguousarray(inputs[name])
        arrays[f"in_{name}"] = a
        args.append(nc.dram_tensor(f"in_{name}", a.shape, _mybir.dt.from_np(a.dtype), kind="ExternalInput").ap())
    args.append(nc.dram_tensor("out_0", (N, D), _mybir.dt.float32, kind="ExternalOutput").ap())
    build(nc, *args)
    r = _run(nc, [arrays], core_ids=[0])
    return r.results[0]["out_0"]
```
